# Optimizing a Trainium2 kernel written in Bass

```python
import numpy as np
import jax
import jax.numpy as jnp

def _softmax(x, axis=-1):
    return jax.nn.softmax(x, axis=axis)

def _gelu(x):
    return jax.nn.gelu(x, approximate=True)

def _silu(x):
    return jax.nn.silu(x)

def _sigmoid(x):
    return jax.nn.sigmoid(x)

def _layernorm(x, axis=-1, eps=1e-05):
    m = jnp.mean(x, axis=axis, keepdims=True)
    v = jnp.var(x, axis=axis, keepdims=True)
    return (x - m) / jnp.sqrt(v + eps)

def _scatter_add(tgt, idx, src, axis=0):
    return tgt.at[idx].add(src)

def _segment_sum(src, seg, n):
    return jax.ops.segment_sum(src, seg, n)
kernel_name = 'mk_flamingo_gated_d4_seqx_r8_b2ec23'

def setup_inputs(seed: int=0):
    np.random.seed(seed)
    _w = jnp.asarray

    def _rec_inputs():
        import jax
        import jax.numpy as jnp
        _rk = jax.random.key(seed)
        x = 7.22e-05 + 1 * jax.random.normal(jax.random.fold_in(_rk, 1), (16, 56, 256), jnp.float32)
        _lenS = 56 - jax.random.randint(jax.random.fold_in(_rk, 7), (16,), 0, max(1, 56 // 4) + 1, jnp.int32)
        _lenS2 = 1500 - jax.random.randint(jax.random.fold_in(_rk, 8), (16,), 0, max(1, 1500 // 4) + 1, jnp.int32)
        _ctx_512P = jax.random.normal(jax.random.fold_in(_rk, 11), (16, 16, 64), jnp.float32)
        _ctx_512c = jax.random.dirichlet(jax.random.fold_in(_rk, 511), 0.3 * jnp.ones((16,), jnp.float32), (16, 1500))
        _ctx_512t = jnp.einsum('bsk,bkd->bsd', _ctx_512c, _ctx_512P)
        _ctx_512t = _ctx_512t * jax.lax.rsqrt(jnp.mean(jnp.square(_ctx_512t)) + 1e-12) * 0.953939
        ctx_512 = -0.000514642 + 1.00011 * (_ctx_512t + 0.3 * jax.random.normal(jax.random.fold_in(_rk, 611), (16, 1500, 64), jnp.float32))
        _g = jax.random.normal(jax.random.fold_in(_rk, 9001), (2, 4), jnp.float32)
        _g = jnp.sign(_g) * jnp.maximum(jnp.abs(_g), 1.0) + (_g == 0) * 1.0
        g_xattn = _g[0]
        g_ffn = _g[1]
        return (x, ctx_512, g_xattn, g_ffn)
    x, ctx_512, g_xattn, g_ffn = _rec_inputs()

    def _L0_xattn_setup():
        import jax, jax.numpy as jnp
        import numpy as np
        B, S, H, NH, L = (2, 256, 256, 16, 64)
        HD = H // NH
        key = jax.random.key(seed)
        k1, k2, k3, k4, k5 = jax.random.split(key, 5)
        scale = 0.02
        return {'q': jax.random.normal(k1, (B, S, H), dtype=jnp.float32), 'latent_kv': jax.random.normal(k2, (B, S, L), dtype=jnp.float32), 'Wq': jax.random.normal(k3, (H, H), dtype=jnp.float32) * scale, 'Wkv_expand': jax.random.normal(k4, (2 * H, L), dtype=jnp.float32) * scale, 'Wout': jax.random.normal(k5, (H, H), dtype=jnp.float32) * scale}
    _L0_xattn_all = _L0_xattn_setup()
    _L0_xattn_in = {k: v for k, v in _L0_xattn_all.items() if k in ('Wq', 'Wkv_expand', 'Wout')}
    del _L0_xattn_all

    def _L0_ffn_setup():
        import jax, jax.numpy as jnp
        import numpy as np
        E = 64
        K = 6
        NG = 8
        TKG = 4
        SCALE = 2.5
        CAP = 64

        def _router(x, gate_w, e_bias):
            logits = x.astype(jnp.float32) @ gate_w.T
            scores = jax.nn.sigmoid(logits)
            sc = scores + e_bias[None, :]
            T = x.shape[0]
            gs = sc.reshape(T, NG, E // NG)
            grp_score = jax.lax.top_k(gs, 2)[0].sum(-1)
            _, gidx = jax.lax.top_k(grp_score, TKG)
            gmask = jax.nn.one_hot(gidx, NG, dtype=sc.dtype).sum(1)
            emask = jnp.repeat(gmask, E // NG, axis=1)
            masked = jnp.where(emask > 0, sc, -jnp.inf)
            _, idx = jax.lax.top_k(masked, K)
            w = jnp.take_along_axis(scores, idx, axis=1)
            w = w / (w.sum(-1, keepdims=True) + 1e-20) * SCALE
            return (idx, w)

        def _relu2(h):
            return jnp.square(jax.nn.relu(h))

        def _moe(x, idx, w, w1, w2):
            T, D = x.shape
            e_flat = idx.reshape(-1)
            tok = jnp.repeat(jnp.arange(T), K)
            oh = jax.nn.one_hot(e_flat, E, dtype=jnp.float32)
            pos = jnp.cumsum(oh, axis=0) - oh
            pos = (pos * oh).sum(-1).astype(jnp.int32)
            keep = pos < CAP
            slot = jnp.where(keep, pos, CAP)
            xd = jnp.zeros((E, CAP + 1, D), x.dtype).at[e_flat, slot].set(x[tok])
            h = _relu2(jnp.einsum('ecd,eid->eci', xd, w1))
            yd = jnp.einsum('eci,edi->ecd', h, w2)
            gate = w.reshape(-1)[:, None] * keep[:, None].astype(x.dtype)
            y_assign = yd[e_flat, slot] * gate
            return jnp.zeros((T, D), x.dtype).at[tok].add(y_assign)
        key = jax.random.key(seed)
        ks = jax.random.split(key, 6)
        D, I, SH, T = (256, 128, 512, 256)
        x = jax.random.normal(ks[0], (1, T, D), jnp.float32)
        gate_w = jax.random.normal(ks[1], (E, D), jnp.float32) * D ** (-0.5)
        e_bias = jnp.zeros((E,), jnp.float32)
        w1 = jax.random.normal(ks[2], (E, I, D), jnp.float32) * D ** (-0.5)
        w2 = jax.random.normal(ks[3], (E, D, I), jnp.float32) * I ** (-0.5)
        su = jax.random.normal(ks[4], (SH, D), jnp.float32) * D ** (-0.5)
        sd = jax.random.normal(ks[5], (D, SH), jnp.float32) * SH ** (-0.5)
        return {'hidden_states': x, 'gate_w': gate_w, 'e_bias': e_bias, 'w1': w1, 'w2': w2, 'shared_up_w': su, 'shared_down_w': sd}
    _L0_ffn_all = _L0_ffn_setup()
    _L0_ffn_in = {k: v for k, v in _L0_ffn_all.items() if k in ('gate_w', 'e_bias', 'w1', 'w2', 'shared_up_w', 'shared_down_w')}
    del _L0_ffn_all

    def _L1_xattn_setup():
        import jax, jax.numpy as jnp
        import numpy as np
        B, S, L = (2, 128, 128)
        DIM_Q, H, K, D_C, D_CQ, R = (256, 16, 128, 64, 192, 64)

        def _rope_tables(seq_len, dim, dtype):
            inv_freq = 1.0 / 10000.0 ** (jnp.arange(0, dim, 2, dtype=dtype) / dim)
            t = jnp.arange(seq_len, dtype=dtype)
            freqs = t[:, None] * inv_freq[None, :]
            sin = jnp.repeat(jnp.sin(freqs), 2, axis=-1)
            cos = jnp.repeat(jnp.cos(freqs), 2, axis=-1)
            return (sin, cos)

        def _rotate_half(x):
            h = x.shape[-1] // 2
            return jnp.concatenate([-x[..., h:], x[..., :h]], axis=-1)
        key = jax.random.key(seed)
        ks = jax.random.split(key, 8)
        s_in = 1.0 / np.sqrt(DIM_Q)
        s_k = 1.0 / np.sqrt(K)
        s_cq = 1.0 / np.sqrt(D_CQ)
        s_c = 1.0 / np.sqrt(D_C)
        return {'hidden_q': jax.random.normal(ks[0], (B, S, DIM_Q), jnp.float32), 'kv_c': jax.random.normal(ks[1], (B, L, D_C), jnp.float32), 'Wq': jax.random.normal(ks[2], (H * K, DIM_Q), jnp.float32) * s_in, 'w_kc_q': jax.random.normal(ks[3], (H, K, D_CQ), jnp.float32) * s_k, 'w_kc_kv': jax.random.normal(ks[4], (H, K, D_C), jnp.float32) * s_k, 'W_qr': jax.random.normal(ks[5], (H, D_CQ, R), jnp.float32) * s_cq / np.sqrt(R), 'W_kr': jax.random.normal(ks[6], (H, D_C, R), jnp.float32) * s_c, 'Wo': jax.random.normal(ks[7], (DIM_Q, H * K), jnp.float32) * s_k}
    _L1_xattn_all = _L1_xattn_setup()
    _L1_xattn_in = {k: v for k, v in _L1_xattn_all.items() if k in ('Wq', 'w_kc_q', 'w_kc_kv', 'W_qr', 'W_kr', 'Wo')}
    del _L1_xattn_all

    def _L1_ffn_setup():
        import jax, jax.numpy as jnp
        import numpy as np
        EPS = 1e-05
        RMS_EPS = 1e-06

        def activation_quant(x, num_bits=8):
            qn = -2 ** (num_bits - 1)
            qp = 2 ** (num_bits - 1) - 1
            xf = x.astype(jnp.float32)
            s = qp / jnp.clip(jnp.max(jnp.abs(xf), axis=-1, keepdims=True), EPS, None)
            return (jnp.clip(jnp.round(xf * s), qn, qp) / s).astype(x.dtype)

        def weight_quant(w):
            wf = w.astype(jnp.float32)
            s = 1.0 / jnp.clip(jnp.mean(jnp.abs(wf)), EPS, None)
            return (jnp.clip(jnp.round(wf * s), -1.0, 1.0) / s).astype(w.dtype)

        def bit_linear(x, w):
            qx = x + jax.lax.stop_gradient(activation_quant(x) - x)
            qw = w + jax.lax.stop_gradient(weight_quant(w) - w)
            return jnp.einsum('bsh,oh->bso', qx, qw)

        def rms_norm(x, weight, eps=RMS_EPS):
            xf = x.astype(jnp.float32)
            var = jnp.mean(xf * xf, axis=-1, keepdims=True)
            return weight * (xf * jax.lax.rsqrt(var + eps)).astype(x.dtype)
        key = jax.random.key(seed)
        k1, k2, k3, k4 = jax.random.split(key, 4)
        B, S, H, I = (2, 256, 256, 1024)
        scale = 1.0 / np.sqrt(H)
        return {'x': jax.random.normal(k1, (B, S, H), dtype=jnp.float32), 'w_gate': jax.random.normal(k2, (I, H), dtype=jnp.float32) * scale, 'w_up': jax.random.normal(k3, (I, H), dtype=jnp.float32) * scale, 'w_down': jax.random.normal(k4, (H, I), dtype=jnp.float32) * (1.0 / np.sqrt(I)), 'ln_weight': jnp.ones((I,), dtype=jnp.float32)}
    _L1_ffn_all = _L1_ffn_setup()
    _L1_ffn_in = {k: v for k, v in _L1_ffn_all.items() if k in ('w_gate', 'w_up', 'w_down', 'ln_weight')}
    del _L1_ffn_all

    def _L2_xattn_setup():
        import jax, jax.numpy as jnp
        import numpy as np
        B, S, L = (2, 128, 128)
        DIM_Q, H, K, D_C, D_CQ, R = (256, 16, 128, 64, 192, 64)

        def _rope_tables(length, dim):
            inv = 1.0 / 10000.0 ** (jnp.arange(0, dim, 2, dtype=jnp.float32) / dim)
            f = jnp.arange(length, dtype=jnp.float32)[:, None] * inv[None, :]
            sin = jnp.repeat(jnp.sin(f), 2, axis=-1)
            cos = jnp.repeat(jnp.cos(f), 2, axis=-1)
            return (sin, cos)

        def _rotate_half(x):
            half = x.shape[-1] // 2
            return jnp.concatenate([-x[..., half:], x[..., :half]], axis=-1)

        def _apply_rope(x, sin, cos):
            return x * cos + _rotate_half(x) * sin
        key = jax.random.key(seed)
        ks = jax.random.split(key, 8)
        return {'hidden_q': jax.random.normal(ks[0], (B, S, DIM_Q), jnp.float32), 'kv_c': jax.random.normal(ks[1], (B, L, D_C), jnp.float32), 'Wq': jax.random.normal(ks[2], (H * K, DIM_Q), jnp.float32) / np.sqrt(DIM_Q).astype(np.float32), 'w_kc_q': jax.random.normal(ks[3], (H, K, D_CQ), jnp.float32) / np.sqrt(K).astype(np.float32), 'w_kc_kv': jax.random.normal(ks[4], (H, K, D_C), jnp.float32) / np.sqrt(K).astype(np.float32), 'W_qr': jax.random.normal(ks[5], (H, D_CQ, R), jnp.float32) / np.float32(np.sqrt(D_CQ) * np.sqrt(R)), 'W_kr': jax.random.normal(ks[6], (H, D_C, R), jnp.float32) / np.sqrt(D_C).astype(np.float32), 'Wo': jax.random.normal(ks[7], (DIM_Q, H * K), jnp.float32) / np.sqrt(H * K).astype(np.float32)}
    _L2_xattn_all = _L2_xattn_setup()
    _L2_xattn_in = {k: v for k, v in _L2_xattn_all.items() if k in ('Wq', 'w_kc_q', 'w_kc_kv', 'W_qr', 'W_kr', 'Wo')}
    del _L2_xattn_all

    def _L2_ffn_setup():
        import jax, jax.numpy as jnp
        import numpy as np
        B, S, D = (2, 256, 256)
        MOE_D = 176
        E = 16
        K = 6
        ALPHA = 0.001

        def _moe_forward(x, gate_w, w_gate, w_up, w_down):
            b, s, d = x.shape
            T = b * s
            h = x.reshape(T, d)
            logits = h @ gate_w.T
            scores = jax.nn.softmax(logits.astype(jnp.float32), axis=-1)
            topk_w, topk_idx = jax.lax.top_k(scores, K)
            cw = jnp.zeros((T, E), jnp.float32)
            cw = cw.at[jnp.arange(T)[:, None], topk_idx].add(topk_w)
            y = jnp.zeros((T, d), x.dtype)
            for e in range(E):
                g = h @ w_gate[e].T
                u = h @ w_up[e].T
                out = jax.nn.silu(g) * u @ w_down[e].T
                y = y + cw[:, e:e + 1].astype(x.dtype) * out
            counts = jnp.sum(jax.nn.one_hot(topk_idx.reshape(b, s * K), E, dtype=jnp.float32), axis=1)
            ce = counts * (E / (s * K))
            scores_bse = scores.reshape(b, s, E)
            aux = jnp.mean(jnp.sum(ce * scores_bse.mean(axis=1), axis=1)) * ALPHA
            return (y.reshape(b, s, d), aux)
        key = jax.random.key(seed)
        ks = jax.random.split(key, 5)
        sd = 1.0 / np.sqrt(D)
        sm = 1.0 / np.sqrt(MOE_D)
        return {'x': jax.random.normal(ks[0], (B, S, D), jnp.float32), 'gate_w': jax.random.normal(ks[1], (E, D), jnp.float32) * sd, 'w_gate': jax.random.normal(ks[2], (E, MOE_D, D), jnp.float32) * sd, 'w_up': jax.random.normal(ks[3], (E, MOE_D, D), jnp.float32) * sd, 'w_down': jax.random.normal(ks[4], (E, D, MOE_D), jnp.float32) * sm}
    _L2_ffn_all = _L2_ffn_setup()
    _L2_ffn_in = {k: v for k, v in _L2_ffn_all.items() if k in ('gate_w', 'w_gate', 'w_up', 'w_down')}
    del _L2_ffn_all

    def _L3_xattn_setup():
        import jax, jax.numpy as jnp
        import numpy as np
        B, S, L = (2, 128, 128)
        DIM_Q, H, K, D_C, D_CQ, R = (256, 16, 128, 64, 192, 64)

        def _rope_tables(seq_len, dim, dtype):
            inv_freq = 1.0 / 10000.0 ** (jnp.arange(0, dim, 2, dtype=dtype) / dim)
            t = jnp.arange(seq_len, dtype=dtype)
            freqs = t[:, None] * inv_freq[None, :]
            sin = jnp.repeat(jnp.sin(freqs), 2, axis=-1)
            cos = jnp.repeat(jnp.cos(freqs), 2, axis=-1)
            return (sin, cos)

        def _rotate_half(x):
            h = x.shape[-1] // 2
            return jnp.concatenate([-x[..., h:], x[..., :h]], axis=-1)
        key = jax.random.key(seed)
        ks = jax.random.split(key, 8)
        s_in = 1.0 / np.sqrt(DIM_Q)
        s_k = 1.0 / np.sqrt(K)
        s_cq = 1.0 / np.sqrt(D_CQ)
        s_c = 1.0 / np.sqrt(D_C)
        return {'hidden_q': jax.random.normal(ks[0], (B, S, DIM_Q), jnp.float32), 'kv_c': jax.random.normal(ks[1], (B, L, D_C), jnp.float32), 'Wq': jax.random.normal(ks[2], (H * K, DIM_Q), jnp.float32) * s_in, 'w_kc_q': jax.random.normal(ks[3], (H, K, D_CQ), jnp.float32) * s_k, 'w_kc_kv': jax.random.normal(ks[4], (H, K, D_C), jnp.float32) * s_k, 'W_qr': jax.random.normal(ks[5], (H, D_CQ, R), jnp.float32) * s_cq / np.sqrt(R), 'W_kr': jax.random.normal(ks[6], (H, D_C, R), jnp.float32) * s_c, 'Wo': jax.random.normal(ks[7], (DIM_Q, H * K), jnp.float32) * s_k}
    _L3_xattn_all = _L3_xattn_setup()
    _L3_xattn_in = {k: v for k, v in _L3_xattn_all.items() if k in ('Wq', 'w_kc_q', 'w_kc_kv', 'W_qr', 'W_kr', 'Wo')}
    del _L3_xattn_all

    def _L3_ffn_setup():
        import jax, jax.numpy as jnp
        import numpy as np
        B, S, D = (4, 256, 256)
        E, F, K = (8, 128, 2)
        SF = 128
        EPS = 1e-06

        def _rmsnorm(x, w, eps=EPS):
            var = jnp.mean(x * x, axis=-1, keepdims=True)
            return x * jax.lax.rsqrt(var + eps) * w
        key = jax.random.key(seed)
        ks = jax.random.split(key, 9)
        g = lambda k, shape, scale: jax.random.normal(k, shape, jnp.float32) * scale
        return {'x': g(ks[0], (B, S, D), 1.0), 'rms_weight': jnp.ones((D,), jnp.float32), 'router_w': g(ks[1], (D, E), 0.02), 'w_gate': g(ks[2], (E, D, F), 0.02), 'w_up': g(ks[3], (E, D, F), 0.02), 'w_down': g(ks[4], (E, F, D), 0.02), 'sw_gate': g(ks[5], (D, SF), 0.02), 'sw_up': g(ks[6], (D, SF), 0.02), 'sw_down': g(ks[7], (SF, D), 0.02)}
    _L3_ffn_all = _L3_ffn_setup()
    _L3_ffn_in = {k: v for k, v in _L3_ffn_all.items() if k in ('rms_weight', 'router_w', 'w_gate', 'w_up', 'w_down', 'sw_gate', 'sw_up', 'sw_down')}
    del _L3_ffn_all
    return {'x': x, 'ctx_512': ctx_512, 'g_xattn': g_xattn, 'g_ffn': g_ffn, 'L0_xattn_Wq': _L0_xattn_in['Wq'], 'L0_xattn_Wkv_expand': _L0_xattn_in['Wkv_expand'], 'L0_xattn_Wout': _L0_xattn_in['Wout'], 'L0_ffn_gate_w': _L0_ffn_in['gate_w'], 'L0_ffn_e_bias': _L0_ffn_in['e_bias'], 'L0_ffn_w1': _L0_ffn_in['w1'], 'L0_ffn_w2': _L0_ffn_in['w2'], 'L0_ffn_shared_up_w': _L0_ffn_in['shared_up_w'], 'L0_ffn_shared_down_w': _L0_ffn_in['shared_down_w'], 'L1_xattn_Wq': _L1_xattn_in['Wq'], 'L1_xattn_w_kc_q': _L1_xattn_in['w_kc_q'], 'L1_xattn_w_kc_kv': _L1_xattn_in['w_kc_kv'], 'L1_xattn_W_qr': _L1_xattn_in['W_qr'], 'L1_xattn_W_kr': _L1_xattn_in['W_kr'], 'L1_xattn_Wo': _L1_xattn_in['Wo'], 'L1_ffn_w_gate': _L1_ffn_in['w_gate'], 'L1_ffn_w_up': _L1_ffn_in['w_up'], 'L1_ffn_w_down': _L1_ffn_in['w_down'], 'L1_ffn_ln_weight': _L1_ffn_in['ln_weight'], 'L2_xattn_Wq': _L2_xattn_in['Wq'], 'L2_xattn_w_kc_q': _L2_xattn_in['w_kc_q'], 'L2_xattn_w_kc_kv': _L2_xattn_in['w_kc_kv'], 'L2_xattn_W_qr': _L2_xattn_in['W_qr'], 'L2_xattn_W_kr': _L2_xattn_in['W_kr'], 'L2_xattn_Wo': _L2_xattn_in['Wo'], 'L2_ffn_gate_w': _L2_ffn_in['gate_w'], 'L2_ffn_w_gate': _L2_ffn_in['w_gate'], 'L2_ffn_w_up': _L2_ffn_in['w_up'], 'L2_ffn_w_down': _L2_ffn_in['w_down'], 'L3_xattn_Wq': _L3_xattn_in['Wq'], 'L3_xattn_w_kc_q': _L3_xattn_in['w_kc_q'], 'L3_xattn_w_kc_kv': _L3_xattn_in['w_kc_kv'], 'L3_xattn_W_qr': _L3_xattn_in['W_qr'], 'L3_xattn_W_kr': _L3_xattn_in['W_kr'], 'L3_xattn_Wo': _L3_xattn_in['Wo'], 'L3_ffn_rms_weight': _L3_ffn_in['rms_weight'], 'L3_ffn_router_w': _L3_ffn_in['router_w'], 'L3_ffn_w_gate': _L3_ffn_in['w_gate'], 'L3_ffn_w_up': _L3_ffn_in['w_up'], 'L3_ffn_w_down': _L3_ffn_in['w_down'], 'L3_ffn_sw_gate': _L3_ffn_in['sw_gate'], 'L3_ffn_sw_up': _L3_ffn_in['sw_up'], 'L3_ffn_sw_down': _L3_ffn_in['sw_down']}

def reference(x, ctx_512, g_xattn, g_ffn, L0_xattn_Wq, L0_xattn_Wkv_expand, L0_xattn_Wout, L0_ffn_gate_w, L0_ffn_e_bias, L0_ffn_w1, L0_ffn_w2, L0_ffn_shared_up_w, L0_ffn_shared_down_w, L1_xattn_Wq, L1_xattn_w_kc_q, L1_xattn_w_kc_kv, L1_xattn_W_qr, L1_xattn_W_kr, L1_xattn_Wo, L1_ffn_w_gate, L1_ffn_w_up, L1_ffn_w_down, L1_ffn_ln_weight, L2_xattn_Wq, L2_xattn_w_kc_q, L2_xattn_w_kc_kv, L2_xattn_W_qr, L2_xattn_W_kr, L2_xattn_Wo, L2_ffn_gate_w, L2_ffn_w_gate, L2_ffn_w_up, L2_ffn_w_down, L3_xattn_Wq, L3_xattn_w_kc_q, L3_xattn_w_kc_kv, L3_xattn_W_qr, L3_xattn_W_kr, L3_xattn_Wo, L3_ffn_rms_weight, L3_ffn_router_w, L3_ffn_w_gate, L3_ffn_w_up, L3_ffn_w_down, L3_ffn_sw_gate, L3_ffn_sw_up, L3_ffn_sw_down):
    import jax
    import jax.numpy as jnp

    def _L0_xattn_ref(q, latent_kv, Wq, Wkv_expand, Wout):
        import jax, jax.numpy as jnp
        import numpy as np
        B, S, H, NH, L = (2, 256, 256, 16, 64)
        HD = H // NH
        b, sq, _ = q.shape
        sk = latent_kv.shape[1]
        qp = q @ Wq.T
        kv = latent_kv @ Wkv_expand.T
        k, v = jnp.split(kv, 2, axis=-1)
        qh = qp.reshape(b, sq, NH, HD).transpose(0, 2, 1, 3)
        kh = k.reshape(b, sk, NH, HD).transpose(0, 2, 1, 3)
        vh = v.reshape(b, sk, NH, HD).transpose(0, 2, 1, 3)
        inv_sqrt_d = 1.0 / jnp.sqrt(jnp.float32(HD))
        scores = jnp.einsum('bhqd,bhkd->bhqk', qh, kh) * inv_sqrt_d
        causal = jnp.tril(jnp.ones((sq, sk), dtype=bool))
        scores = jnp.where(causal, scores, jnp.finfo(scores.dtype).min)
        attn = jax.nn.softmax(scores, axis=-1)
        out = jnp.einsum('bhqk,bhkd->bhqd', attn, vh)
        out = out.transpose(0, 2, 1, 3).reshape(b, sq, H)
        return out @ Wout.T

    def _L0_ffn_ref(hidden_states, gate_w, e_bias, w1, w2, shared_up_w, shared_down_w):
        import jax, jax.numpy as jnp
        import numpy as np
        E = 64
        K = 6
        NG = 8
        TKG = 4
        SCALE = 2.5
        CAP = 64

        def _router(x, gate_w, e_bias):
            logits = x.astype(jnp.float32) @ gate_w.T
            scores = jax.nn.sigmoid(logits)
            sc = scores + e_bias[None, :]
            T = x.shape[0]
            gs = sc.reshape(T, NG, E // NG)
            grp_score = jax.lax.top_k(gs, 2)[0].sum(-1)
            _, gidx = jax.lax.top_k(grp_score, TKG)
            gmask = jax.nn.one_hot(gidx, NG, dtype=sc.dtype).sum(1)
            emask = jnp.repeat(gmask, E // NG, axis=1)
            masked = jnp.where(emask > 0, sc, -jnp.inf)
            _, idx = jax.lax.top_k(masked, K)
            w = jnp.take_along_axis(scores, idx, axis=1)
            w = w / (w.sum(-1, keepdims=True) + 1e-20) * SCALE
            return (idx, w)

        def _relu2(h):
            return jnp.square(jax.nn.relu(h))

        def _moe(x, idx, w, w1, w2):
            T, D = x.shape
            e_flat = idx.reshape(-1)
            tok = jnp.repeat(jnp.arange(T), K)
            oh = jax.nn.one_hot(e_flat, E, dtype=jnp.float32)
            pos = jnp.cumsum(oh, axis=0) - oh
            pos = (pos * oh).sum(-1).astype(jnp.int32)
            keep = pos < CAP
            slot = jnp.where(keep, pos, CAP)
            xd = jnp.zeros((E, CAP + 1, D), x.dtype).at[e_flat, slot].set(x[tok])
            h = _relu2(jnp.einsum('ecd,eid->eci', xd, w1))
            yd = jnp.einsum('eci,edi->ecd', h, w2)
            gate = w.reshape(-1)[:, None] * keep[:, None].astype(x.dtype)
            y_assign = yd[e_flat, slot] * gate
            return jnp.zeros((T, D), x.dtype).at[tok].add(y_assign)
        orig = hidden_states.shape
        x = hidden_states.reshape(-1, orig[-1])
        idx, wts = _router(x, gate_w, e_bias)
        shared = _relu2(x @ shared_up_w.T) @ shared_down_w.T
        routed = _moe(x, idx, wts.astype(x.dtype), w1, w2)
        return (shared + routed).reshape(orig)

    def _L1_xattn_ref(hidden_q, kv_c, Wq, w_kc_q, w_kc_kv, W_qr, W_kr, Wo):
        import jax, jax.numpy as jnp
        import numpy as np
        B, S, L = (2, 128, 128)
        DIM_Q, H, K, D_C, D_CQ, R = (256, 16, 128, 64, 192, 64)

        def _rope_tables(seq_len, dim, dtype):
            inv_freq = 1.0 / 10000.0 ** (jnp.arange(0, dim, 2, dtype=dtype) / dim)
            t = jnp.arange(seq_len, dtype=dtype)
            freqs = t[:, None] * inv_freq[None, :]
            sin = jnp.repeat(jnp.sin(freqs), 2, axis=-1)
            cos = jnp.repeat(jnp.cos(freqs), 2, axis=-1)
            return (sin, cos)

        def _rotate_half(x):
            h = x.shape[-1] // 2
            return jnp.concatenate([-x[..., h:], x[..., :h]], axis=-1)
        b, s, _ = hidden_q.shape
        l = kv_c.shape[1]
        q_hk = (hidden_q @ Wq.T).reshape(b, s, H, K)
        q_big = jnp.einsum('bshk,hkq->bshq', q_hk, w_kc_q)
        sin, cos = _rope_tables(l, D_C, kv_c.dtype)
        kv_rope = kv_c * cos[None] + _rotate_half(kv_c) * sin[None]
        q_r = jnp.einsum('bshq,hqr->bhsr', q_big, W_qr)
        k_r = jnp.einsum('bld,hdr->bhlr', kv_rope, W_kr)
        scores = jnp.einsum('bhsr,bhlr->bhsl', q_r, k_r)
        attn = jax.nn.softmax(scores, axis=-1)
        ctx_c = jnp.einsum('bhsl,bld->bhsd', attn, kv_rope)
        ctx_lat = jnp.einsum('bhsd,hkd->bshk', ctx_c, w_kc_kv)
        out = ctx_lat.reshape(b, s, H * K) @ Wo.T
        return out

    def _L1_ffn_ref(x, w_gate, w_up, w_down, ln_weight):
        import jax, jax.numpy as jnp
        import numpy as np
        EPS = 1e-05
        RMS_EPS = 1e-06

        def activation_quant(x, num_bits=8):
            qn = -2 ** (num_bits - 1)
            qp = 2 ** (num_bits - 1) - 1
            xf = x.astype(jnp.float32)
            s = qp / jnp.clip(jnp.max(jnp.abs(xf), axis=-1, keepdims=True), EPS, None)
            return (jnp.clip(jnp.round(xf * s), qn, qp) / s).astype(x.dtype)

        def weight_quant(w):
            wf = w.astype(jnp.float32)
            s = 1.0 / jnp.clip(jnp.mean(jnp.abs(wf)), EPS, None)
            return (jnp.clip(jnp.round(wf * s), -1.0, 1.0) / s).astype(w.dtype)

        def bit_linear(x, w):
            qx = x + jax.lax.stop_gradient(activation_quant(x) - x)
            qw = w + jax.lax.stop_gradient(weight_quant(w) - w)
            return jnp.einsum('bsh,oh->bso', qx, qw)

        def rms_norm(x, weight, eps=RMS_EPS):
            xf = x.astype(jnp.float32)
            var = jnp.mean(xf * xf, axis=-1, keepdims=True)
            return weight * (xf * jax.lax.rsqrt(var + eps)).astype(x.dtype)
        h = jax.nn.silu(bit_linear(x, w_gate)) * bit_linear(x, w_up)
        h = rms_norm(h, ln_weight)
        return bit_linear(h, w_down)

    def _L2_xattn_ref(hidden_q, kv_c, Wq, w_kc_q, w_kc_kv, W_qr, W_kr, Wo):
        import jax, jax.numpy as jnp
        import numpy as np
        B, S, L = (2, 128, 128)
        DIM_Q, H, K, D_C, D_CQ, R = (256, 16, 128, 64, 192, 64)

        def _rope_tables(length, dim):
            inv = 1.0 / 10000.0 ** (jnp.arange(0, dim, 2, dtype=jnp.float32) / dim)
            f = jnp.arange(length, dtype=jnp.float32)[:, None] * inv[None, :]
            sin = jnp.repeat(jnp.sin(f), 2, axis=-1)
            cos = jnp.repeat(jnp.cos(f), 2, axis=-1)
            return (sin, cos)

        def _rotate_half(x):
            half = x.shape[-1] // 2
            return jnp.concatenate([-x[..., half:], x[..., :half]], axis=-1)

        def _apply_rope(x, sin, cos):
            return x * cos + _rotate_half(x) * sin
        Bv, Sv, _ = hidden_q.shape
        _, Lv, _ = kv_c.shape
        q_hk = (hidden_q @ Wq.T).reshape(Bv, Sv, H, K)
        q_big = jnp.einsum('bshk,hkq->bshq', q_hk, w_kc_q)
        sin_q, cos_q = _rope_tables(Sv, D_CQ)
        q_big = _apply_rope(q_big, sin_q[None, :, None, :], cos_q[None, :, None, :])
        sin_k, cos_k = _rope_tables(Lv, D_C)
        kv_r = _apply_rope(kv_c, sin_k[None], cos_k[None])
        q_r = jnp.einsum('bshq,hqr->bhsr', q_big, W_qr)
        k_r = jnp.einsum('bld,hdr->bhlr', kv_r, W_kr)
        scores = jnp.einsum('bhsr,bhlr->bhsl', q_r, k_r)
        attn = jax.nn.softmax(scores, axis=-1)
        ctx_c = jnp.einsum('bhsl,bld->bhsd', attn, kv_r)
        ctx_lat = jnp.einsum('bhsd,hkd->bhsk', ctx_c, w_kc_kv)
        ctx = ctx_lat.transpose(0, 2, 1, 3).reshape(Bv, Sv, H * K)
        return ctx @ Wo.T

    def _L2_ffn_ref(x, gate_w, w_gate, w_up, w_down):
        import jax, jax.numpy as jnp
        import numpy as np
        B, S, D = (2, 256, 256)
        MOE_D = 176
        E = 16
        K = 6
        ALPHA = 0.001

        def _moe_forward(x, gate_w, w_gate, w_up, w_down):
            b, s, d = x.shape
            T = b * s
            h = x.reshape(T, d)
            logits = h @ gate_w.T
            scores = jax.nn.softmax(logits.astype(jnp.float32), axis=-1)
            topk_w, topk_idx = jax.lax.top_k(scores, K)
            cw = jnp.zeros((T, E), jnp.float32)
            cw = cw.at[jnp.arange(T)[:, None], topk_idx].add(topk_w)
            y = jnp.zeros((T, d), x.dtype)
            for e in range(E):
                g = h @ w_gate[e].T
                u = h @ w_up[e].T
                out = jax.nn.silu(g) * u @ w_down[e].T
                y = y + cw[:, e:e + 1].astype(x.dtype) * out
            counts = jnp.sum(jax.nn.one_hot(topk_idx.reshape(b, s * K), E, dtype=jnp.float32), axis=1)
            ce = counts * (E / (s * K))
            scores_bse = scores.reshape(b, s, E)
            aux = jnp.mean(jnp.sum(ce * scores_bse.mean(axis=1), axis=1)) * ALPHA
            return (y.reshape(b, s, d), aux)
        y, _aux = _moe_forward(x, gate_w, w_gate, w_up, w_down)
        return y

    def _L3_xattn_ref(hidden_q, kv_c, Wq, w_kc_q, w_kc_kv, W_qr, W_kr, Wo):
        import jax, jax.numpy as jnp
        import numpy as np
        B, S, L = (2, 128, 128)
        DIM_Q, H, K, D_C, D_CQ, R = (256, 16, 128, 64, 192, 64)

        def _rope_tables(seq_len, dim, dtype):
            inv_freq = 1.0 / 10000.0 ** (jnp.arange(0, dim, 2, dtype=dtype) / dim)
            t = jnp.arange(seq_len, dtype=dtype)
            freqs = t[:, None] * inv_freq[None, :]
            sin = jnp.repeat(jnp.sin(freqs), 2, axis=-1)
            cos = jnp.repeat(jnp.cos(freqs), 2, axis=-1)
            return (sin, cos)

        def _rotate_half(x):
            h = x.shape[-1] // 2
            return jnp.concatenate([-x[..., h:], x[..., :h]], axis=-1)
        b, s, _ = hidden_q.shape
        l = kv_c.shape[1]
        q_hk = (hidden_q @ Wq.T).reshape(b, s, H, K)
        q_big = jnp.einsum('bshk,hkq->bshq', q_hk, w_kc_q)
        sin, cos = _rope_tables(l, D_C, kv_c.dtype)
        kv_rope = kv_c * cos[None] + _rotate_half(kv_c) * sin[None]
        q_r = jnp.einsum('bshq,hqr->bhsr', q_big, W_qr)
        k_r = jnp.einsum('bld,hdr->bhlr', kv_rope, W_kr)
        scores = jnp.einsum('bhsr,bhlr->bhsl', q_r, k_r)
        attn = jax.nn.softmax(scores, axis=-1)
        ctx_c = jnp.einsum('bhsl,bld->bhsd', attn, kv_rope)
        ctx_lat = jnp.einsum('bhsd,hkd->bshk', ctx_c, w_kc_kv)
        out = ctx_lat.reshape(b, s, H * K) @ Wo.T
        return out

    def _L3_ffn_ref(x, rms_weight, router_w, w_gate, w_up, w_down, sw_gate, sw_up, sw_down):
        import jax, jax.numpy as jnp
        import numpy as np
        B, S, D = (4, 256, 256)
        E, F, K = (8, 128, 2)
        SF = 128
        EPS = 1e-06

        def _rmsnorm(x, w, eps=EPS):
            var = jnp.mean(x * x, axis=-1, keepdims=True)
            return x * jax.lax.rsqrt(var + eps) * w
        b, s, d = x.shape
        e = router_w.shape[1]
        h = _rmsnorm(x, rms_weight)
        ht = h.reshape(-1, d)
        t = ht.shape[0]
        logits = ht @ router_w
        probs = jax.nn.softmax(logits, axis=-1)
        topv, topi = jax.lax.top_k(probs, K)
        topv = topv / jnp.sum(topv, axis=-1, keepdims=True)
        w_dense = jnp.zeros((t, e), ht.dtype).at[jnp.arange(t)[:, None], topi].set(topv)
        g = jnp.einsum('td,edf->tef', ht, w_gate)
        u = jnp.einsum('td,edf->tef', ht, w_up)
        eo = jnp.einsum('tef,efd->ted', jax.nn.silu(g) * u, w_down)
        moe = jnp.einsum('te,ted->td', w_dense, eo)
        sh = jax.nn.silu(ht @ sw_gate) * (ht @ sw_up) @ sw_down
        return (moe + sh).reshape(b, s, d)
    x = x + jnp.tanh(g_xattn[0]) * _L0_xattn_ref(_layernorm(x, axis=-1), ctx_512, L0_xattn_Wq, L0_xattn_Wkv_expand, L0_xattn_Wout)
    x = x + jnp.tanh(g_ffn[0]) * _L0_ffn_ref(_layernorm(x, axis=-1), L0_ffn_gate_w, L0_ffn_e_bias, L0_ffn_w1, L0_ffn_w2, L0_ffn_shared_up_w, L0_ffn_shared_down_w)
    x = x + jnp.tanh(g_xattn[1]) * _L1_xattn_ref(_layernorm(x, axis=-1), ctx_512, L1_xattn_Wq, L1_xattn_w_kc_q, L1_xattn_w_kc_kv, L1_xattn_W_qr, L1_xattn_W_kr, L1_xattn_Wo)
    x = x + jnp.tanh(g_ffn[1]) * _L1_ffn_ref(_layernorm(x, axis=-1), L1_ffn_w_gate, L1_ffn_w_up, L1_ffn_w_down, L1_ffn_ln_weight)
    x = x + jnp.tanh(g_xattn[2]) * _L2_xattn_ref(_layernorm(x, axis=-1), ctx_512, L2_xattn_Wq, L2_xattn_w_kc_q, L2_xattn_w_kc_kv, L2_xattn_W_qr, L2_xattn_W_kr, L2_xattn_Wo)
    x = x + jnp.tanh(g_ffn[2]) * _L2_ffn_ref(_layernorm(x, axis=-1), L2_ffn_gate_w, L2_ffn_w_gate, L2_ffn_w_up, L2_ffn_w_down)
    x = x + jnp.tanh(g_xattn[3]) * _L3_xattn_ref(_layernorm(x, axis=-1), ctx_512, L3_xattn_Wq, L3_xattn_w_kc_q, L3_xattn_w_kc_kv, L3_xattn_W_qr, L3_xattn_W_kr, L3_xattn_Wo)
    x = x + jnp.tanh(g_ffn[3]) * _L3_ffn_ref(_layernorm(x, axis=-1), L3_ffn_rms_weight, L3_ffn_router_w, L3_ffn_w_gate, L3_ffn_w_up, L3_ffn_w_down, L3_ffn_sw_gate, L3_ffn_sw_up, L3_ffn_sw_down)
    return x

_drawn_inputs = setup_inputs


def setup_inputs(seed=0):
    import zlib

    import numpy as np

    out = dict(_drawn_inputs(seed))
    spreads = {'L0_ffn_e_bias': (0.0, 0.1),
     'L1_ffn_ln_weight': (1.0, 0.2),
     'L3_ffn_rms_weight': (1.0, 0.6)}
    factors = {'g_ffn': 40.024,
     'L0_xattn_Wq': 4.105,
     'L3_ffn_router_w': 8.0,
     'L3_ffn_w_gate': 8.0,
     'L3_ffn_w_up': 8.0,
     'L3_ffn_w_down': 8.0,
     'L3_ffn_sw_gate': 8.0,
     'L3_ffn_sw_up': 8.0,
     'L3_ffn_sw_down': 8.0}
    for name, (base, spread) in spreads.items():
        noise = np.random.default_rng([zlib.crc32(name.encode()), seed]).standard_normal(out[name].shape)
        drawn = base * np.exp(spread * noise) if base else spread * noise
        out[name] = jnp.asarray(drawn.astype(out[name].dtype))
    for name, factor in factors.items():
        out[name] = (out[name] * factor).astype(out[name].dtype)
    return out
```

```python
from collections import namedtuple

import numpy as np

import concourse.bass as bass
from concourse import mybir

F32, F32R, BF16 = mybir.dt.float32, mybir.dt.float32r, mybir.dt.bfloat16
ALU = mybir.AluOpType
ACT = mybir.ActivationFunctionType
AX = mybir.AxisListType

P = 128
B, S, D = 16, 56, 256
T = B * S
NT = T // P
KD = D // P
HT = T // 2
L, DC = 1500, 64
NL, LP = 12, 125
H = 16
K1 = 128
DQ, DQH = 192, 96
E0, TOP0, NG0, TOPG0, CAP0 = 64, 6, 8, 4, 64
I1 = 1024
E2, I2, TOP2 = 16, 176, 6
E3, TOP3 = 8, 2
NB0, NB2, NB3 = E0 + 4, E2 * I2 // P, E3 + 1
BIG = 3.0e38
ROUND = 1.5 * 2.0 ** 23

Tick = namedtuple("Tick", "sem value")


class Stream:

    def __init__(self, sem):
        self.sem, self.count, self.items, self.seen = sem, 0, [], {}

    def wait(self, *ticks):
        for t in ticks:
            if t is not None and self.seen.get(t.sem, 0) < t.value:
                self.seen[t.sem] = t.value
                self.items.append(lambda e, t=t: e.wait_ge(t.sem, t.value))

    def run(self, fn):
        self.items.append(fn)

    def do(self, fn):
        self.count += 1
        self.items.append(lambda e: fn(e).then_inc(self.sem, 1))
        return Tick(self.sem, self.count)

    def tick(self):
        return Tick(self.sem, self.count)

    def emit(self, engine):
        for item in self.items:
            item(engine)


class Loads:

    def __init__(self, stream):
        self.stream, self.counts = stream, {}

    def start(self, sem, out, src, n=1):
        self.counts[sem] = self.counts.get(sem, 0) + 16
        self.stream.items.append(lambda e: e.dma_start(out, src).then_inc(sem, 16))
        return Tick(sem, self.counts[sem])


class Memory:

    def __init__(self, nc):
        self.nc, self.at, self.end, self.n = nc, (nc.sbuf_base + 31) // 32 * 32, nc.sbuf_usable_end, 0

    def take(self, name, shape, dt):
        size = int(np.prod(shape[1:])) * (2 if dt == BF16 else 4)
        self.n += 1
        t = self.nc.alloc_sbuf_tensor_at(f"{name}_{self.n}", list(shape), dt, offset=self.at)
        self.at += (size + 31) // 32 * 32
        assert self.at <= self.end, (name, self.at, self.end)
        return t


def rope_tables(length, dim):
    f = np.float32
    inv = (f(1.0) / np.power(f(10000.0), np.arange(0, dim, 2, dtype=f) / f(dim))).astype(f)
    angle = np.arange(length, dtype=f)[:, None] * inv[None, :]
    return np.repeat(np.sin(angle), 2, axis=-1).astype(f), np.repeat(np.cos(angle), 2, axis=-1).astype(f)


def constants():
    f = np.float32
    c = {}
    c["ident"] = np.eye(P, dtype=f)
    c["before"] = np.triu(np.ones((P, P), f), 1)
    sin, cos = rope_tables(L, DC)
    signed = sin.copy()
    signed[:, :DC // 2] *= -1
    c["cos_k"] = cos.reshape(LP, NL * DC)
    c["sin_k"] = signed.reshape(LP, NL * DC)
    sin, cos = rope_tables(S, DQ)
    halves = [cos[:, :DQH], sin[:, :DQH], cos[:, DQH:], sin[:, DQH:]]
    c["rope_q"] = np.stack([x.T for x in halves], 1).astype(f)
    late = np.where(np.arange(S)[None, :] > np.arange(S)[:, None], f(-1e30), f(0))
    s_of_q = (np.arange(NT * P) % S).reshape(NT, P).T
    c["mask_q"] = late[s_of_q].astype(f)
    c["mask_k"] = np.ascontiguousarray(late.T).astype(f)
    bd = np.zeros((NT, NT, P), f)
    bd[np.arange(NT), np.arange(NT)] = 1
    c["blockdiag"] = bd
    c["sel0"] = (np.arange(P)[:, None] % E0 == np.arange(E0)[None, :]).astype(f)
    rows = np.arange(64)[:, None] % 32
    c["sel2"] = (rows == np.arange(E2 * I2)[None, :] // I2).astype(f)
    c["sel3"] = (rows == np.arange(E3)[None, :]).astype(f)
    return c


def build(nc, io, out, steps=8):
    mem = Memory(nc)
    sems = {n: nc.alloc_semaphore(n) for n in ("pe_done", "act_done", "dve_done", "pool_done")}
    pe, act, dve, pool = (Stream(sems[n]) for n in ("pe_done", "act_done", "dve_done", "pool_done"))
    sp = Stream(None)
    dma = Loads(sp)
    load_sems = {}

    def dsem(name):
        if name not in load_sems:
            load_sems[name] = nc.alloc_semaphore("dma_" + name)
        return load_sems[name]

    psum = nc.alloc_psum_tensor("psum", [P, 8, 512], F32)
    bank_free = [None] * 8

    def phase_barrier():
        ticks = [s.tick() for s in (pe, act, dve, pool)]
        loads = [Tick(s, n) for s, n in dma.counts.items()]
        for s in (pe, act, dve, pool, sp):
            s.wait(*ticks, *loads)

    def mm(o, lhsT, rhs, start, stop, **kw):
        return lambda e: e.matmul(o, lhsT, rhs, start=start, stop=stop, **kw)

    def product(o, pairs, skip=False):
        for n, (a, b) in enumerate(pairs):
            last = n == len(pairs) - 1
            f = mm(o, a, b, n == 0, last, skip_group_check=skip)
            if last:
                return pe.do(f)
            pe.run(f)

    def split_pairs(ah, al, bh, bl):
        return [(ah, bh), (ah, bl), (al, bh)]

    X = mem.take("X", [P, NT, D], F32)
    YH = mem.take("YH", [P, KD, T], F32R)
    YL = mem.take("YL", [P, KD, T], F32R)
    ident = mem.take("ident", [P, P], F32)
    ones = mem.take("ones", [P, P], F32)
    exponent = mem.take("exponent", [P, NT], F32)
    gates = mem.take("gates", [P, 8], F32)
    tanh_g = mem.take("tanh_g", [P, 8], F32)
    V = mem.take("V", [P, B, NL * DC], F32)
    base = mem.at

    KT = nc.dram_tensor("kt_scratch", (B, P, L), F32, kind="Internal").ap()

    t_ident = dma.start(dsem("ident"), ident[:, :], io["ident"])
    t_x = dma.start(dsem("x"), X[:, :, :], io["x"].rearrange("b s d -> (b s) d").rearrange("(i p) d -> p i d", p=P))
    dma.start(dsem("g"), gates[:, 0:4], io["g_xattn"].rearrange("(a n) -> a n", a=1).broadcast_to([P, 4]))
    t_g = dma.start(dsem("g"), gates[:, 4:8], io["g_ffn"].rearrange("(a n) -> a n", a=1).broadcast_to([P, 4]))
    t_ones = dve.do(lambda e: e.memset(ones[:, :], 1.0))
    t_exponent = dve.do(lambda e: e.memset(exponent[:, :], -0.5))
    act.wait(t_g)
    t_tanh = act.do(lambda e: e.activation(tanh_g[:, :], gates[:, :], ACT.Tanh))

    def dve_barrier_self():
        dve.wait(dve.tick())

    def layer_norm(t_in, Y, stats, mv, rstd):
        dve.wait(t_in)
        for i in range(NT):
            dve.do(lambda e, i=i: e.bn_stats(stats[:, i, :], X[:, i, :]))
        dve.wait(dve.tick())
        for i in range(NT):
            dve.do(lambda e, i=i: e.bn_aggr(mv[:, i, :], stats[:, i, :]))
        dve.wait(dve.tick())
        t = dve.do(lambda e: e.tensor_scalar(rstd[:, :], mv[:, :, 1], 1e-5, None, ALU.add))
        pool.wait(t, t_exponent)
        t = pool.do(lambda e: e.tensor_tensor(rstd[:, :], rstd[:, :], exponent[:, :], ALU.pow))
        dve.wait(t)
        return [dve.do(lambda e, i=i: e.tensor_scalar(Y[:, i, :], X[:, i, :], mv[:, i, 0:1], rstd[:, i:i + 1],
                                                      ALU.subtract, ALU.mult)) for i in range(NT)]

    def transpose_y(Y, t_y):
        pe.wait(t_ident, *t_y)
        t_hi = t_lo = None
        for kd in range(KD):
            for a, tiles in enumerate((range(0, 4), range(4, NT))):
                bank = 4 + (kd * 2 + a) % 4
                pe.wait(bank_free[bank])
                for i in tiles:
                    t = pe.do(lambda e, i=i, kd=kd, bank=bank, a=a: e.transpose(
                        psum[:, bank, (i - 4 * a) * P:(i - 4 * a + 1) * P], Y[:, i, kd * P:(kd + 1) * P], ident[:, :]))
                n = len(tiles) * P
                cols = slice(a * 512, a * 512 + n)
                act.wait(t)
                t_hi = act.do(lambda e, kd=kd, bank=bank, n=n, cols=cols: e.activation(
                    YH[:, kd, cols], psum[:, bank, 0:n], ACT.Copy))
                dve.wait(t_hi)
                t_lo = dve.do(lambda e, kd=kd, bank=bank, n=n, cols=cols: e.tensor_tensor(
                    YL[:, kd, cols], psum[:, bank, 0:n], YH[:, kd, cols].bitcast(F32), ALU.subtract))
                bank_free[bank] = t_lo
        return t_hi, t_lo

    def norm_buffers():
        return (mem.take("Y", [P, NT, D], F32), mem.take("stats", [P, NT, 6], F32),
                mem.take("mv", [P, NT, 2], F32), mem.take("rstd", [P, NT], F32))

    def back_to_tokens(acc_ticks, gate_col, OT):
        ts = []
        for m in range(KD):
            for c in range(2):
                act.wait(acc_ticks)
                ts.append(act.do(lambda e, m=m, c=c: e.activation(
                    OT[:, m, c * HT:(c + 1) * HT], psum[:, m * 2 + c, 0:HT], ACT.Copy)))
        for bank in range(4):
            bank_free[bank] = ts[-1]
        pe.wait(ts[-1])
        t_x = None
        for g in range(4):
            bank = 4 + g
            tiles = [i for i in (2 * g, 2 * g + 1) if i < NT]
            pe.wait(bank_free[bank])
            for i in tiles:
                for m in range(KD):
                    t = pe.do(lambda e, i=i, m=m, bank=bank, g=g: e.transpose(
                        psum[:, bank, (i - 2 * g) * D + m * P:(i - 2 * g) * D + (m + 1) * P],
                        OT[:, m, i * P:(i + 1) * P], ident[:, :]))
            n = len(tiles) * D
            dve.wait(t, t_tanh)
            t_x = dve.do(lambda e, g=g, bank=bank, n=n: e.scalar_tensor_tensor(
                X[:, 2 * g:2 * g + n // D, :].rearrange("p a d -> p (a d)"), psum[:, bank, 0:n],
                tanh_g[:, gate_col:gate_col + 1],
                X[:, 2 * g:2 * g + n // D, :].rearrange("p a d -> p (a d)"), ALU.mult, ALU.add))
            bank_free[bank] = t_x
        return t_x

    def prepare_context():
        mem.at = base
        cos = mem.take("cos_k", [P, NL * DC], F32)
        sin = mem.take("sin_k", [P, NL * DC], F32)
        raw = [mem.take("ctx_raw", [P, NL, DC], F32) for _ in range(3)]
        rot = [mem.take("ctx_rot", [P, NL, DC], F32) for _ in range(2)]
        kt = [mem.take("kt", [P, L], F32R) for _ in range(2)]
        dma.start(dsem("rope"), cos[0:LP, :], io["cos_k"])
        t_tab = dma.start(dsem("rope"), sin[0:LP, :], io["sin_k"])
        t_raw_free, t_rot_free, t_kt_free, t_kt_st = [None] * 3, [None] * 2, [None] * 2, [None] * 2
        loads = []
        half = DC // 2
        cos3 = cos[0:LP, :].rearrange("p (j d) -> p j d", d=DC)
        sin3 = sin[0:LP, :].rearrange("p (j d) -> p j d", d=DC)
        for b in range(B):
            r = raw[b % 3]
            sp.wait(t_raw_free[b % 3])
            t_load = dma.start(dsem(f"raw{b % 3}"), r[0:LP, :, :].rearrange("p j d -> p (j d)"),
                               io["ctx"][b].rearrange("(p j) d -> p (j d)", j=NL))
            q = rot[b % 2]
            Vb = V[0:LP, b, :].rearrange("p (j d) -> p j d", d=DC)
            pool.wait(t_load, t_tab, t_rot_free[b % 2])
            pool.do(lambda e, r=r, q=q: e.tensor_tensor(q[0:LP, :, 0:half], r[0:LP, :, half:DC], sin3[:, :, 0:half], ALU.mult))
            t_q = pool.do(lambda e, r=r, q=q: e.tensor_tensor(q[0:LP, :, half:DC], r[0:LP, :, 0:half], sin3[:, :, half:DC], ALU.mult))
            dve.wait(t_load, t_tab)
            t_c = dve.do(lambda e, r=r, Vb=Vb: e.tensor_tensor(Vb, r[0:LP, :, :], cos3, ALU.mult))
            t_raw_free[b % 3] = t_c
            sp.wait(t_q)
            dve.wait(t_c, t_q)
            t_v = dve.do(lambda e, q=q, Vb=Vb: e.tensor_tensor(Vb, Vb, q[0:LP, :, :], ALU.add))
            t_rot_free[b % 2] = t_v
            k = kt[b % 2]
            for g in range(3):
                bank = (3 * b + g) % 8
                pe.wait(t_v, t_ident, bank_free[bank])
                for j in range(4):
                    t_p = pe.do(lambda e, b=b, g=g, j=j, bank=bank: e.transpose(
                        psum[0:DC, bank, j * LP:(j + 1) * LP],
                        V[0:LP, b, (4 * g + j) * DC:(4 * g + j + 1) * DC], ident[0:LP, 0:LP]))
                cols = slice(g * 4 * LP, (g + 1) * 4 * LP)
                act.wait(t_p, t_kt_free[b % 2])
                t_h = act.do(lambda e, k=k, cols=cols, bank=bank: e.activation(
                    k[0:DC, cols], psum[0:DC, bank, 0:4 * LP], ACT.Copy))
                dve.wait(t_h)
                t_l = dve.do(lambda e, k=k, cols=cols, bank=bank: e.tensor_tensor(
                    k[DC:P, cols], psum[0:DC, bank, 0:4 * LP], k[0:DC, cols].bitcast(F32), ALU.subtract))
                bank_free[bank] = t_l
            sp.wait(t_l)
            t_kt_free[b % 2] = dma.start(dsem(f"kt_st{b % 2}"), KT[b], k[:, :].bitcast(F32))
        return t_kt_free

    def attention(layer, t_in):
        mem.at = base
        first = layer == 0
        KH = 16 if first else K1
        AH = mem.take("AH", [P, KD, H * DC], F32R)
        AL = mem.take("AL", [P, KD, H * DC], F32R)
        MH = mem.take("MH", [P, H // 2, D], F32R)
        ML = mem.take("ML", [P, H // 2, D], F32R)
        qr_at = mem.at
        QR = mem.take("QR", [P, H // 2, T], F32)
        top = mem.at
        w = lambda n: io[f"a{layer}_{n}"]

        mem.at = qr_at
        WoT = mem.take("WoT", [P, H, D], F32)
        Wv = mem.take("Wv", [P, H, DC], F32)
        mem.at = top
        Wq = mem.take("Wq", [P, H, D], F32)
        t_wq = dma.start(dsem("wq"), Wq[0:KH, :, :], w("Wq"))
        t_wo = dma.start(dsem("wo"), WoT[0:KH, :, :], w("WoT"))
        t_wv = dma.start(dsem("wv"), Wv[0:KH, :, :], w("Wv"))
        pe.wait(t_wv, t_wo)
        for g in range(4):
            bank = 4 + g
            pe.wait(bank_free[bank])
            for h in range(4 * g, 4 * g + 4):
                odd, pair = h % 2, (h % 4) // 2
                t = pe.do(mm(psum[odd * DC:(odd + 1) * DC, bank, pair * D:(pair + 1) * D],
                             Wv[0:KH, h, :], WoT[0:KH, h, :], True, True))
            act.wait(t)
            t_MH = act.do(lambda e, g=g, bank=bank: e.activation(
                MH[:, 2 * g:2 * g + 2, :].rearrange("p a d -> p (a d)"), psum[:, bank, :], ACT.Copy))
            dve.wait(t_MH)
            t_ML = dve.do(lambda e, g=g, bank=bank: e.tensor_tensor(
                ML[:, 2 * g:2 * g + 2, :].rearrange("p a d -> p (a d)"), psum[:, bank, :],
                MH[:, 2 * g:2 * g + 2, :].rearrange("p a d -> p (a d)").bitcast(F32), ALU.subtract))
            bank_free[bank] = t_ML

        G = mem.take("G", [P, H, DC], F32)
        t_G = None
        U = None
        if first:
            t_G = dma.start(dsem("wk"), G[0:KH, :, :], w("Wk"))
        else:
            if layer == 2:
                Wc = mem.take("Wc", [P, H, DQ], F32)
            else:
                Wc = mem.take("WcT", [DQH, H, 2, K1], F32)
            U = mem.take("U", [DQH, H, 2, DC], F32)
            wqr_at = mem.at
            Wqr = mem.take("WqrT", [64, H, DQ], F32)
            Wkr = mem.take("WkrT", [64, H, DC], F32)
            t_qr = dma.start(dsem("wqr"), Wqr[:, :, :], w("WqrT"))
            t_kr = dma.start(dsem("wkr"), Wkr[:, :, :], w("WkrT"))
            if layer == 2:
                t_c = dma.start(dsem("wc"), Wc[:, :, :], w("Wc"))
            else:
                t_c = dma.start(dsem("wc"), Wc[:, :, :, :], w("WcT"))
            pe.wait(t_qr, t_kr)
            for g in range(4):
                pe.wait(bank_free[g])
                for h in range(4 * g, 4 * g + 4):
                    for c in range(2):
                        o = psum[0:DQH, g, ((h % 4) * 2 + c) * DC:((h % 4) * 2 + c + 1) * DC]
                        t = pe.do(mm(o, Wqr[:, h, c * DQH:(c + 1) * DQH], Wkr[:, h, :], True, True))
                act.wait(t)
                bank_free[g] = t_U = act.do(lambda e, g=g: e.activation(
                    U[:, 4 * g:4 * g + 4, :, :].rearrange("p h c d -> p (h c d)"), psum[0:DQH, g, :], ACT.Copy))
            if layer != 2:
                pe.wait(t_U, t_c)
                for g in range(2):
                    pe.wait(bank_free[4 + g])
                    for h in range(8 * g, 8 * g + 8):
                        t = product(psum[:, 4 + g, (h % 8) * DC:(h % 8 + 1) * DC],
                                    [(Wc[:, h, c, :], U[:, h, c, :]) for c in range(2)])
                    act.wait(t)
                    bank_free[4 + g] = t_G = act.do(lambda e, g=g: e.activation(
                        G[:, 8 * g:8 * g + 8, :].rearrange("p h d -> p (h d)"), psum[:, 4 + g, :], ACT.Copy))
        t_AL = t_AH = None
        if layer != 2:
            pe.wait(t_wq, t_G)
            for kd in range(KD):
                for g in range(2):
                    bank = kd * 2 + g
                    pe.wait(bank_free[bank])
                    for h in range(8 * g, 8 * g + 8):
                        t = pe.do(mm(psum[:, bank, (h % 8) * DC:(h % 8 + 1) * DC],
                                     Wq[0:KH, h, kd * P:(kd + 1) * P], G[0:KH, h, :], True, True))
                    cols = slice(g * 512, (g + 1) * 512)
                    scale = 1.0 / np.sqrt(16.0) if first else 1.0
                    act.wait(t)
                    t_AH = act.do(lambda e, kd=kd, bank=bank, cols=cols, scale=scale: e.activation(
                        AH[:, kd, cols], psum[:, bank, :], ACT.Copy, scale=float(scale)))
                    dve.wait(t_AH)
                    t_AL = dve.do(lambda e, kd=kd, bank=bank, cols=cols, scale=scale: e.scalar_tensor_tensor(
                        AL[:, kd, cols], psum[:, bank, :], float(scale), AH[:, kd, cols].bitcast(F32),
                        ALU.mult, ALU.subtract))
                    bank_free[bank] = t_AL
        if layer == 2:
            mem.at = wqr_at
            sp.wait(t_U)
            dve.wait(t_U)
        Y, stats, mv, rstd = norm_buffers()
        t_y = layer_norm(t_in, Y, stats, mv, rstd)
        t_yh, t_yl = transpose_y(Y, t_y)

        if layer != 2:
            pe.wait(t_yh, t_yl, t_AH, t_AL)
            for mt in range(H // 2):
                for c in range(2):
                    bank = (mt * 2 + c) % 8
                    pe.wait(bank_free[bank])
                    pairs = []
                    for kd in range(KD):
                        m, n = slice(mt * P, (mt + 1) * P), slice(c * HT, (c + 1) * HT)
                        pairs += split_pairs(AH[:, kd, m], AL[:, kd, m], YH[:, kd, n], YL[:, kd, n])
                    t = product(psum[:, bank, 0:HT], pairs)
                    act.wait(t)
                    bank_free[bank] = act.do(lambda e, mt=mt, c=c, bank=bank: e.activation(
                        QR[:, mt, c * HT:(c + 1) * HT], psum[:, bank, 0:HT], ACT.Copy))
        else:
            rope = mem.take("rope_q", [DQH, 4, S], F32)
            t_rope = dma.start(dsem("rope_q"), rope[:, :, :], io["rope_q"])
            BH = [mem.take("BH", [P, KD, DQ], F32R) for _ in range(2)]
            BL = [mem.take("BL", [P, KD, DQ], F32R) for _ in range(2)]
            terms = [mem.take("rope_term", [DQH, 4, HT], F32) for _ in range(2)]
            turned = [mem.take("turned", [DQH, 2, HT], F32) for _ in range(2)]
            t_turn_free, t_term_free, t_B_free = [None] * 2, [None] * 2, [None] * 2
            unit = 0
            for h in range(H):
                pe.wait(t_wq, t_c, bank_free[0])
                for kd in range(KD):
                    t = pe.do(mm(psum[:, 0, kd * DQ:(kd + 1) * DQ], Wq[:, h, kd * P:(kd + 1) * P],
                                 Wc[:, h, :], True, True))
                bh, bl = BH[h % 2], BL[h % 2]
                act.wait(t, t_B_free[h % 2])
                t_bh = act.do(lambda e, bh=bh: e.activation(
                    bh[:, :, :].rearrange("p k q -> p (k q)"), psum[:, 0, 0:KD * DQ], ACT.Copy))
                dve.wait(t_bh)
                t_bl = dve.do(lambda e, bh=bh, bl=bl: e.tensor_tensor(
                    bl[:, :, :].rearrange("p k q -> p (k q)"), psum[:, 0, 0:KD * DQ],
                    bh[:, :, :].rearrange("p k q -> p (k q)").bitcast(F32), ALU.subtract))
                bank_free[0] = t_bl
                for c in range(2):
                    n = slice(c * HT, (c + 1) * HT)
                    banks = (1 + 2 * (unit % 2), 2 + 2 * (unit % 2))
                    pe.wait(t_bh, t_bl, t_yh, t_yl)
                    for half, bank in enumerate(banks):
                        pe.wait(bank_free[bank])
                        m = slice(half * DQH, (half + 1) * DQH)
                        pairs = []
                        for kd in range(KD):
                            pairs += split_pairs(bh[:, kd, m], bl[:, kd, m], YH[:, kd, n], YL[:, kd, n])
                        t = product(psum[0:DQH, bank, 0:HT], pairs)
                    if c == 1:
                        t_B_free[h % 2] = t
                    tm, tu = terms[unit % 2], turned[unit % 2]
                    dve.wait(t, t_rope, t_term_free[unit % 2])
                    for k, (half, tab) in enumerate(((0, 0), (1, 1), (1, 2), (0, 3))):
                        t_m = dve.do(lambda e, k=k, half=half, tab=tab, tm=tm, banks=banks: e.tensor_tensor(
                            tm[:, k, :].rearrange("p (b s) -> p b s", s=S),
                            psum[0:DQH, banks[half], 0:HT].rearrange("p (b s) -> p b s", s=S),
                            rope[:, tab:tab + 1, :].broadcast_to([DQH, HT // S, S]), ALU.mult))
                    for bank in banks:
                        bank_free[bank] = t_m
                    pool.wait(t_m, t_turn_free[unit % 2])
                    pool.do(lambda e, tm=tm, tu=tu: e.tensor_tensor(tu[:, 0, :], tm[:, 0, :], tm[:, 1, :], ALU.subtract))
                    t_t = pool.do(lambda e, tm=tm, tu=tu: e.tensor_tensor(tu[:, 1, :], tm[:, 2, :], tm[:, 3, :], ALU.add))
                    t_term_free[unit % 2] = t_t
                    bank = 5 + unit % 3
                    odd = h % 2
                    pe.wait(t_t, t_U, bank_free[bank])
                    t = product(psum[odd * DC:(odd + 1) * DC, bank, 0:HT],
                                [(U[:, h, half, :], tu[:, half, :]) for half in range(2)])
                    t_turn_free[unit % 2] = t
                    act.wait(t)
                    bank_free[bank] = act.do(lambda e, h=h, odd=odd, n=n, bank=bank: e.activation(
                        QR[odd * DC:(odd + 1) * DC, h // 2, n], psum[odd * DC:(odd + 1) * DC, bank, 0:HT], ACT.Copy))
                    unit += 1
        t_qr_done = act.tick()
        phase_barrier()

        mem.at = top
        keys = S if first else LP
        ntile = 1 if first else NL
        NK = keys * ntile
        CH = 1 if first else 3
        CW = NK // CH
        K1t = [mem.take("K1", [P, L if not first else B * S], F32R) for _ in range(1 if first else 2)]
        K2t = [mem.take("K2", [P, L if not first else B * S], F32R) for _ in range(1 if first else 2)]
        Q1 = [mem.take("Q1", [P, T], F32R) for _ in range(2)]
        Q2 = [mem.take("Q2", [P, T], F32R) for _ in range(2)]
        NE = 4
        E = [mem.take("E", [P, T], F32) for _ in range(NE)]
        SA = [mem.take("SA", [P, T], F32) for _ in range(2)]
        SB = [mem.take("SB", [P, T], F32) for _ in range(2)]
        O1 = mem.take("O1", [DC, T], F32)
        RD = mem.take("RD", [NT, T], F32)
        bd = mem.take("bd", [NT, T], F32)
        mx = mem.take("mx", [P, 2, NT * CH], F32)
        nm = mem.take("nm", [P, 2, NT], F32)
        rden = mem.take("rden", [P, NT], F32)
        t_bd = dma.start(dsem("bd"), bd[:, :], io["blockdiag"])
        for k in K2t:
            t_k2 = dve.do(lambda e, k=k: e.memset(k[DC:DC + NT, :].bitcast(F32), 1.0))
        if first:
            V0 = mem.take("V0", [S, B, DC], F32)
            mq = mem.take("mask_q", [P, NT, S], F32)
            mk = mem.take("mask_k", [S, S], F32)
            masked = [mem.take("masked", [P, T], F32) for _ in range(2)]
            masked_q = mem.take("masked_q", [P, 2, NT, S], F32)
            t_v0 = dma.start(dsem("v0"), V0[:, :, :], io["ctx"][:, 0:S, :].rearrange("b l d -> l b d"))
            dma.start(dsem("masks"), mq[:, :, :], io["mask_q"])
            t_masks = dma.start(dsem("masks"), mk[:, :], io["mask_k"])
            for c in range(2):
                pe.wait(t_v0, bank_free[c])
                for b in range(8 * c, 8 * c + 8):
                    t = pe.do(lambda e, b=b, c=c: e.transpose(psum[0:DC, c, (b % 8) * S:(b % 8 + 1) * S], V0[:, b, :],
                                                              ident[0:S, 0:S]))
                n = slice(c * HT, (c + 1) * HT)
                act.wait(t)
                act.do(lambda e, c=c, n=n: e.activation(K1t[0][0:DC, n], psum[0:DC, c, 0:HT], ACT.Copy))
                t_h = act.do(lambda e, c=c, n=n: e.activation(K2t[0][0:DC, n], psum[0:DC, c, 0:HT], ACT.Copy))
                dve.wait(t_h)
                t_l = dve.do(lambda e, c=c, n=n: e.tensor_tensor(
                    K1t[0][DC:P, n], psum[0:DC, c, 0:HT], K1t[0][0:DC, n].bitcast(F32), ALU.subtract))
                bank_free[c] = t_l

        t_key = [None] * B
        t_q1, t_q2, t_m = [None] * B, [None] * B, [None] * B
        t_scored, t_maxed, t_out = [None] * B, [None] * B, [None] * B
        ring = {"at": 0}

        def small_bank():
            ring["at"] += 1
            bank = 6 + ring["at"] % 2
            pe.wait(bank_free[bank])
            return bank

        def load_keys(b):
            if first:
                t_key[b] = t_l
                return
            k = K1t[b % 2]
            if b >= 2:
                sp.wait(t_scored[b - 2])
            t_ld = dma.start(dsem(f"k1{b % 2}"), k[:, :].bitcast(F32), KT[b])
            if b >= 2:
                act.wait(t_scored[b - 2])
            act.wait(t_ld)
            t_key[b] = act.do(lambda e, k=k, b=b: e.activation(K2t[b % 2][0:DC, :], k[0:DC, :].bitcast(F32), ACT.Copy))

        def key_cols(b, lo, n):
            at = b * S if first else 0
            return slice(at + lo, at + lo + n)

        def make_queries(b):
            q1, q2 = Q1[b % 2], Q2[b % 2]
            tok = slice(b * S, (b + 1) * S)
            if b >= 2:
                act.wait(t_scored[b - 2])
                dve.wait(t_scored[b - 2])
            act.wait(t_qr_done)
            for odd in range(2):
                raw = QR[odd * DC:(odd + 1) * DC, :, tok]
                for copy in range(2):
                    t = act.do(lambda e, raw=raw, copy=copy, odd=odd, q1=q1: e.activation(
                        q1[copy * DC:(copy + 1) * DC, odd * HT:(odd + 1) * HT].rearrange("p (m s) -> p m s", s=S),
                        raw, ACT.Copy))
            t_q1[b] = t
            dve.wait(t)
            for odd in range(2):
                raw = QR[odd * DC:(odd + 1) * DC, :, tok]
                part = slice(odd * DC, (odd + 1) * DC)
                t = dve.do(lambda e, raw=raw, odd=odd, q1=q1, q2=q2, part=part: e.tensor_tensor(
                    q2[0:DC, odd * HT:(odd + 1) * HT].rearrange("p (m s) -> p m s", s=S), raw,
                    q1[part, odd * HT:(odd + 1) * HT].bitcast(F32).rearrange("p (m s) -> p m s", s=S), ALU.subtract))
            t_q2[b] = t

        def max_unit(b, j, c):
            bank = small_bank()
            pe.wait(t_q1[b], t_key[b])
            cols = key_cols(b, c * CW, CW)
            o = psum[:, bank, 0:CW]
            k = K1t[0 if first else b % 2]
            t = pe.do(mm(o, Q1[b % 2][:, j * P:(j + 1) * P], k[:, cols], True, True))
            if first:
                dve.wait(t, t_masks)
                o2 = masked_q[:, b % 2, j, :]
                t2 = dve.do(lambda e, o=o, o2=o2: e.tensor_tensor(o2, o, mq[:, j, :], ALU.add))
                dve.wait(t2)
            else:
                dve.wait(t)
                o2 = o
            t = dve.do(lambda e, o2=o2: e.tensor_reduce(mx[:, b % 2, j * CH + c:j * CH + c + 1], o2, AX.X, ALU.max))
            bank_free[bank] = t
            return t

        def max_finish(b, t_last):
            dve.wait(t_last)
            t = dve.do(lambda e: e.tensor_reduce(
                nm[:, b % 2, :], mx[:, b % 2, :].rearrange("p (j c) -> p j c", c=CH), AX.X, ALU.max, negate=True))
            bank = small_bank()
            pe.wait(t)
            t = pe.do(lambda e, bank=bank: e.transpose(psum[0:NT, bank, 0:P], nm[:, b % 2, :], ident[:, :]))
            dve.wait(t, t_bd)
            row = psum[0:NT, bank, 0:P].unsqueeze(1).broadcast_to([NT, NT, P])
            q2 = Q2[b % 2]
            t = dve.do(lambda e, row=row, q2=q2: e.tensor_tensor(
                q2[DC:DC + NT, :].rearrange("p (j q) -> p j q", q=P), row,
                bd[:, :].rearrange("p (j q) -> p j q", q=P), ALU.mult))
            bank_free[bank] = t
            t_maxed[b] = t

        e_free = [None] * NE
        t_exp = {}

        def scores(b, k):
            pair = (0, 1) if k % 2 == 0 else (2, 3)
            ki = 0 if first else b % 2
            cols = key_cols(b, k * keys, keys)
            pe.wait(t_key[b], t_q1[b], t_q2[b], t_maxed[b], bank_free[pair[0]], bank_free[pair[1]], t_k2)
            for c in range(2):
                pe.run(mm(psum[0:keys, pair[c], 0:HT], K1t[ki][:, cols], Q1[b % 2][:, c * HT:(c + 1) * HT], True, False))
            for c in range(2):
                t = pe.do(mm(psum[0:keys, pair[c], 0:HT], K2t[ki][0:DC + NT, cols],
                             Q2[b % 2][0:DC + NT, c * HT:(c + 1) * HT], False, True))
            if k == ntile - 1:
                t_scored[b] = t
            n = (b * ntile + k) % NE
            e_tile = E[n][0:keys, :].rearrange("p (c q) -> p c q", c=2)
            src = psum[0:keys, pair[0]:pair[0] + 2, 0:HT]
            if first:
                dve.wait(t, t_masks, t_exp.get((b - 2, 0)))
                mb = masked[b % 2]
                for c in range(2):
                    t = dve.do(lambda e, c=c, src=src, mb=mb: e.tensor_tensor(
                        mb[0:keys, c * HT:(c + 1) * HT].rearrange("p (m s) -> p m s", s=S),
                        psum[0:keys, pair[c], 0:HT].rearrange("p (m s) -> p m s", s=S),
                        mk[:, :].unsqueeze(1).broadcast_to([S, HT // S, S]), ALU.add))
                for q in pair:
                    bank_free[q] = t
                src = mb[0:keys, :].rearrange("p (c q) -> p c q", c=2)
            act.wait(t, *(e_free[n] or ()))
            t = act.do(lambda e, e_tile=e_tile, src=src: e.activation(e_tile, src, ACT.Exp))
            if not first:
                for q in pair:
                    bank_free[q] = t
            t_exp[b, k] = t
            e_free[n] = []

        s_free = [None, None]

        def values(b, ks):
            pe.wait(t_exp[b, ks[-1]], bank_free[4], bank_free[5])
            for c in range(2):
                for k in ks:
                    n = (b * ntile + k) % NE
                    v = V0[:, b, :] if first else V[0:LP, b, k * DC:(k + 1) * DC]
                    t = pe.do(mm(psum[(k % 2) * DC:(k % 2 + 1) * DC, 4 + c, 0:HT], v,
                                 E[n][0:keys, c * HT:(c + 1) * HT], k < 2, k >= ntile - 2))
            for k in ks:
                e_free[(b * ntile + k) % NE].append(t)
            return t

        def sums(b, k):
            if first:
                return
            n = (b * ntile + k) % NE
            split = 9
            eng, acc = (pool, SA) if k < split else (dve, SB)
            a = acc[b % 2][0:keys, :]
            if k in (0, split):
                return
            if k in (1, split + 1):
                prev = E[(b * ntile + k - 1) % NE][0:keys, :]
                eng.wait(t_exp[b, k], s_free[b % 2])
            else:
                prev = a
                eng.wait(t_exp[b, k], eng.tick())
            t = eng.do(lambda e, a=a, prev=prev, n=n: e.tensor_tensor(a, prev, E[n][0:keys, :], ALU.add))
            e_free[n].append(t)
            if k in (1, split + 1):
                e_free[(b * ntile + k - 1) % NE].append(t)
            if k == split - 1:
                t_sa[b] = t
            if k == ntile - 1:
                t_sb[b] = t

        t_sa, t_sb, t_pv = {}, {}, {}

        def finish(b):
            parts = [E[(b * ntile) % NE]] if first else [SA[b % 2], SB[b % 2]]
            bank = small_bank()
            if first:
                pe.wait(t_exp[b, 0])
            else:
                pe.wait(t_sa[b], t_sb[b])
            pe.wait(t_ones)
            for j in range(NT):
                t = product(psum[:, bank, j:j + 1],
                            [(a[0:keys, j * P:(j + 1) * P], ones[0:keys, 0:1]) for a in parts])
            s_free[b % 2] = t
            if first:
                e_free[b % NE].append(t)
            dve.wait(t)
            t = dve.do(lambda e, bank=bank: e.reciprocal(rden[:, :], psum[:, bank, 0:NT]))
            bank_free[bank] = t
            bank = small_bank()
            pe.wait(t)
            t = pe.do(lambda e, bank=bank: e.transpose(psum[0:NT, bank, 0:P], rden[:, :], ident[:, :]))
            row = psum[0:NT, bank, 0:P].unsqueeze(1).broadcast_to([NT, NT, P])
            dve.wait(t, t_bd)
            t_r = dve.do(lambda e, row=row: e.tensor_tensor(
                RD[:, :].rearrange("p (j q) -> p j q", q=P), row,
                bd[:, :].rearrange("p (j q) -> p j q", q=P), ALU.mult))
            bank_free[bank] = t_r
            act.wait(t_pv[b], dve.tick())
            lower = psum[0:DC, 4:6, 0:HT]
            o1 = O1[:, :].rearrange("p (c q) -> p c q", c=2)
            if first:
                t = act.do(lambda e: e.activation(o1, lower, ACT.Copy))
            else:
                t = act.do(lambda e: e.activation(o1, psum[DC:P, 4:6, 0:HT], ACT.Copy))
                dve.wait(t)
                t = dve.do(lambda e: e.tensor_tensor(o1, lower, o1, ALU.add))
            bank_free[4] = bank_free[5] = t
            for odd in range(2):
                bank = small_bank()
                pe.wait(t_r)
                t_b = pe.do(mm(psum[0:DC, bank, 0:HT], ones[0:NT, 0:DC], RD[:, odd * HT:(odd + 1) * HT], True, True))
                dve.wait(t, t_b)
                t_o = dve.do(lambda e, odd=odd, bank=bank: e.tensor_tensor(
                    QR[odd * DC:(odd + 1) * DC, :, b * S:(b + 1) * S],
                    O1[:, odd * HT:(odd + 1) * HT].rearrange("p (m s) -> p m s", s=S),
                    psum[0:DC, bank, 0:HT].rearrange("p (m s) -> p m s", s=S), ALU.mult))
                bank_free[bank] = t_o
            t_out[b] = t_o

        units = [(j, c) for j in range(NT) for c in range(CH)]

        def all_max(b, todo):
            t = None
            for j, c in todo:
                t = max_unit(b, j, c)
            return t

        load_keys(0)
        make_queries(0)
        max_finish(0, all_max(0, units))
        for b in range(B):
            if b + 1 < B:
                load_keys(b + 1)
                make_queries(b + 1)
            todo = list(units) if b + 1 < B else []
            t_last = None
            npair = (ntile + 1) // 2
            per = -(-len(todo) // npair)
            for kp in range(npair + 1):
                if kp < npair:
                    for k in range(2 * kp, min(2 * kp + 2, ntile)):
                        scores(b, k)
                    if todo:
                        t_last = all_max(b + 1, todo[:per])
                        todo = todo[per:]
                if kp > 0:
                    ks = list(range(2 * kp - 2, min(2 * kp, ntile)))
                    t_pv[b] = values(b, ks)
                    for k in ks:
                        sums(b, k)
                        if not first and k == 9:
                            pass
            if b + 1 < B:
                max_finish(b + 1, t_last)
            finish(b)
        phase_barrier()

        mem.at = top
        CHh = mem.take("CH", [P, H // 2, T], F32R)
        CL = mem.take("CL", [P, H // 2, T], F32R)
        for m in range(H // 2):
            act.wait(t_out[B - 1])
            t_h = act.do(lambda e, m=m: e.activation(CHh[:, m, :], QR[:, m, :], ACT.Copy))
            dve.wait(t_h)
            t_l2 = dve.do(lambda e, m=m: e.tensor_tensor(CL[:, m, :], QR[:, m, :], CHh[:, m, :].bitcast(F32), ALU.subtract))
        pe.wait(t_h, t_l2)
        t_x = None
        for i in range(NT):
            bank = i
            pe.wait(bank_free[bank])
            tok = slice(i * P, (i + 1) * P)
            pairs = []
            for m in range(H // 2):
                pairs += split_pairs(CHh[:, m, tok], CL[:, m, tok], MH[:, m, :], ML[:, m, :])
            t = product(psum[:, bank, 0:D], pairs)
            dve.wait(t, t_tanh)
            t_x = dve.do(lambda e, i=i, bank=bank: e.scalar_tensor_tensor(
                X[:, i, :], psum[:, bank, 0:D], tanh_g[:, layer:layer + 1], X[:, i, :], ALU.mult, ALU.add))
            bank_free[bank] = t_x
        phase_barrier()
        return t_x

    def logits(gate, n_exp, t_yh, t_yl):
        GW = mem.take("gate_w", [P, KD, n_exp], F32)
        GH = mem.take("gate_hi", [P, KD, n_exp], F32R)
        GL = mem.take("gate_lo", [P, KD, n_exp], F32R)
        t = dma.start(dsem("gate_w"), GW[:, :, :], gate)
        dve.wait(t)
        t = dve.do(lambda e: e.tensor_copy(GH[:, :, :], GW[:, :, :]))
        dve.wait(t)
        t = dve.do(lambda e: e.tensor_tensor(GL[:, :, :], GW[:, :, :], GH[:, :, :].bitcast(F32), ALU.subtract))
        pe.wait(t, t_yh, t_yl, bank_free[4])
        for i in range(NT):
            tok = slice(i * P, (i + 1) * P)
            pairs = []
            for kd in range(KD):
                pairs += split_pairs(YH[:, kd, tok], YL[:, kd, tok], GH[:, kd, :], GL[:, kd, :])
            t = product(psum[:, 4, i * n_exp:(i + 1) * n_exp], pairs)
        return t, psum[:, 4, 0:NT * n_exp].rearrange("p (i n) -> p i n", n=n_exp)

    def choose(values, t_in, n, top, name):
        wide = n + 8 - top
        v8 = mem.take(name + "_top8", [P, NT, 8], F32)
        left = mem.take(name + "_left", [P, NT, wide], F32)
        mask = mem.take(name + "_mask", [P, NT, n], F32)
        dve.wait(t_in)
        for i in range(NT):
            t = dve.do(lambda e, i=i: e.max(v8[:, i, :], values[:, i, :]))
        dve.wait(t)
        for i in range(NT):
            t = dve.do(lambda e, i=i: e.match_replace(left[:, i, :], v8[:, i, :], values[:, i, :], -BIG))
        dve.wait(t)
        t = dve.do(lambda e: e.tensor_tensor(mask[:, :, :], values[:, :, 0:n], left[:, :, 0:n], ALU.not_equal))
        return mask, t

    def softmax_rows(src, n, t_in, wide):
        m = mem.take("lmax", [P, NT], F32)
        ex = mem.take("lexp", [P, NT, n], F32)
        sm = mem.take("lsum", [P, NT], F32)
        pr = mem.take("probs", [P, NT, wide], F32)
        t0 = dve.do(lambda e: e.memset(pr[:, :, :], BIG))
        dve.wait(t_in)
        t = dve.do(lambda e: e.tensor_reduce(m[:, :], src, AX.X, ALU.max))
        dve.wait(t)
        t = dve.do(lambda e: e.tensor_tensor(ex[:, :, :], src, m[:, :].unsqueeze(2).broadcast_to([P, NT, n]), ALU.subtract))
        bank_free[4] = t
        act.wait(t)
        t = act.do(lambda e: e.activation(ex[:, :, :], ex[:, :, :], ACT.Exp))
        dve.wait(t)
        t = dve.do(lambda e: e.tensor_reduce(sm[:, :], ex[:, :, :], AX.X, ALU.add))
        dve.wait(t)
        t = dve.do(lambda e: e.reciprocal(sm[:, :], sm[:, :]))
        dve.wait(t, t0)
        t = dve.do(lambda e: e.tensor_tensor(pr[:, :, 0:n], ex[:, :, :], sm[:, :].unsqueeze(2).broadcast_to([P, NT, n]), ALU.mult))
        return pr, t

    def gates_transposed(Gt, n, lo_row, t_in):
        GT = mem.take("GT", [P, T], F32R)
        t0 = None
        if lo_row != n:
            t0 = dve.do(lambda e: e.memset(GT[:, :].bitcast(F32), 0.0))
        pe.wait(t_in)
        for a, tiles in enumerate((range(0, 4), range(4, NT))):
            bank = 5 + a
            pe.wait(bank_free[bank])
            for i in tiles:
                t = pe.do(lambda e, i=i, a=a, bank=bank: e.transpose(
                    psum[0:n, bank, (i - 4 * a) * P:(i - 4 * a + 1) * P], Gt[:, i, :], ident[:, :]))
            w = len(tiles) * P
            cols = slice(a * 512, a * 512 + w)
            dve.wait(t, t0)
            t = dve.do(lambda e, cols=cols, bank=bank, w=w: e.tensor_copy(GT[0:n, cols], psum[0:n, bank, 0:w]))
            dve.wait(t)
            t = dve.do(lambda e, cols=cols, bank=bank, w=w: e.tensor_tensor(
                GT[lo_row:lo_row + n, cols], psum[0:n, bank, 0:w], GT[0:n, cols].bitcast(F32), ALU.subtract))
            bank_free[bank] = t
        return GT, t

    def expert_blocks(weights, nblk, swiglu, selector, sel_rows, n_gated, GT, t_gt, t_yh, t_yl):
        WID = 768 if swiglu else 512
        NW = 3
        WS = [mem.take("WS", [P, WID], F32) for _ in range(NW)]
        WH = [mem.take("WH", [P, WID], F32R) for _ in range(NW)]
        WL = [mem.take("WL", [P, WID], F32R) for _ in range(NW)]
        NH = 3
        R = [mem.take("R", [P, HT], F32) for _ in range(NH)]
        G1 = [mem.take("G1", [P, HT], F32) for _ in range(NH)]
        HF = [mem.take("HF", [P, HT], F32) for _ in range(NH)]
        HH = [mem.take("HH", [P, HT], F32R) for _ in range(NH)]
        HL = [mem.take("HL", [P, HT], F32R) for _ in range(NH)]
        ws_free, w_free = [None] * NW, [None] * NW
        r_free, h_free, hf_free = [None] * NH, [None] * NH, [None] * NH
        ring = [0]
        t_w = {}

        def next_bank():
            bank = 4 + ring[0] % 4
            ring[0] += 1
            pe.wait(bank_free[bank])
            return bank

        t_load = {}

        def fetch(n):
            k = n % NW
            sp.wait(*(ws_free[k] or ()))
            t_load[n] = dma.start(dsem(f"ws{k}"), WS[k][:, :], weights[n])

        def split(n):
            k = n % NW
            act.wait(t_load[n], w_free[k])
            t_h = act.do(lambda e: e.activation(WH[k][:, :], WS[k][:, :], ACT.Copy))
            pool.wait(t_h, w_free[k])
            t_l = pool.do(lambda e: e.tensor_tensor(WL[k][:, :], WS[k][:, :], WH[k][:, :].bitcast(F32), ALU.subtract))
            ws_free[k] = (t_h, t_l)
            t_w[n] = (t_h, t_l)

        def up(n, c):
            k, u = n % NW, (2 * n + c) % NH
            cols = slice(c * HT, (c + 1) * HT)
            pe.wait(*t_w[n], t_yh, t_yl)
            outs = []
            for part in range(2 if swiglu else 1):
                bank = next_bank()
                pairs = []
                for kd in range(KD):
                    m = slice(part * D + kd * P, part * D + (kd + 1) * P)
                    pairs += split_pairs(WH[k][:, m], WL[k][:, m], YH[:, kd, cols], YL[:, kd, cols])
                t = product(psum[:, bank, 0:HT], pairs)
                outs.append((bank, t))
            gated = n < n_gated
            if gated:
                gb = next_bank()
                pe.wait(t_gt)
                t_g = pe.do(mm(psum[:, gb, 0:HT], selector(n), GT[0:sel_rows, cols], True, True))
            r, g1, hf, hh, hl = R[u], G1[u], HF[u], HH[u], HL[u]
            bank, t = outs[0]
            act.wait(t, *(r_free[u] or ()))
            t_r = act.do(lambda e: e.activation(r[:, :], psum[:, bank, 0:HT], ACT.Silu if swiglu else ACT.Relu))
            bank_free[bank] = t_r
            dve.wait(t_r)
            if swiglu:
                b2, t2 = outs[1]
                dve.wait(t2)
                first_out = g1 if gated else hf
                if not gated:
                    dve.wait(hf_free[u])
                t = dve.do(lambda e: e.tensor_tensor(first_out[:, :], r[:, :], psum[:, b2, 0:HT], ALU.mult))
                bank_free[b2] = t
                if gated:
                    dve.wait(t, t_g, hf_free[u])
                    t = dve.do(lambda e: e.tensor_tensor(hf[:, :], g1[:, :], psum[:, gb, 0:HT], ALU.mult))
                    bank_free[gb] = t
            else:
                if gated:
                    dve.wait(t_g)
                    t = dve.do(lambda e: e.tensor_tensor(g1[:, :], r[:, :], psum[:, gb, 0:HT], ALU.mult))
                    bank_free[gb] = t
                    dve.wait(t)
                src = g1 if gated else r
                dve.wait(hf_free[u])
                t = dve.do(lambda e: e.tensor_tensor(hf[:, :], src[:, :], r[:, :], ALU.mult))
            r_free[u] = (t,)
            dve.wait(t, h_free[u])
            t_hh = dve.do(lambda e: e.tensor_copy(hh[:, :], hf[:, :]))
            pool.wait(t_hh, h_free[u])
            t_hl = pool.do(lambda e: e.tensor_tensor(hl[:, :], hf[:, :], hh[:, :].bitcast(F32), ALU.subtract))
            hf_free[u] = t_hl
            return t_hh, t_hl

        def down(n, c, ticks):
            k, u = n % NW, (2 * n + c) % NH
            off = WID - D
            pe.wait(*ticks)
            for m in range(KD):
                mcol = slice(off + m * P, off + (m + 1) * P)
                if n == 0:
                    pe.wait(bank_free[m * 2 + c])
                prs = split_pairs(WH[k][:, mcol], WL[k][:, mcol], HH[u][:, :], HL[u][:, :])
                for q, (a, bb) in enumerate(prs):
                    f = mm(psum[:, m * 2 + c, 0:HT], a, bb, n == 0 and q == 0, n == nblk - 1 and q == 2)
                    if q == 2:
                        t = pe.do(f)
                    else:
                        pe.run(f)
            h_free[u] = t
            if c == 1:
                w_free[k] = t
            return t

        for n in range(min(2, nblk)):
            fetch(n)
        split(0)
        pending = []
        for n in range(nblk):
            for c in range(2):
                ticks = up(n, c)
                if c == 0 and n + 1 < nblk:
                    if n + 2 < nblk:
                        fetch(n + 2)
                    if len(pending) and pending[0][0] < n - 1:
                        pass
                pending.append((n, c, ticks))
                if len(pending) > 1:
                    t = down(*pending.pop(0))
                if c == 1 and n + 1 < nblk:
                    split(n + 1)
        while pending:
            t = down(*pending.pop(0))
        return t

    def begin_ffn(t_in):
        mem.at = base
        Y, stats, mv, rstd = norm_buffers()
        t_y = layer_norm(t_in, Y, stats, mv, rstd)
        return Y, t_y

    def ffn0(t_in):
        Y, t_y = begin_ffn(t_in)
        t_yh, t_yl = transpose_y(Y, t_y)
        t, lg = logits(io["f0_gate"], E0, t_yh, t_yl)
        sc = mem.take("scores", [P, NT, E0], F32)
        sb = mem.take("biased", [P, NT, E0], F32)
        eb = mem.take("e_bias", [P, E0], F32)
        t_eb = dma.start(dsem("eb"), eb[:, :], io["f0_bias"].rearrange("(a n) -> a n", a=1).broadcast_to([P, E0]))
        act.wait(t)
        t_sc = act.do(lambda e: e.activation(sc[:, :, :], lg, ACT.Sigmoid))
        bank_free[4] = t_sc
        dve.wait(t_sc, t_eb)
        t = dve.do(lambda e: e.tensor_tensor(sb[:, :, :], sc[:, :, :], eb[:, :].unsqueeze(1).broadcast_to([P, NT, E0]), ALU.add))
        g8 = mem.take("group_top8", [P, NT, NG0, 8], F32)
        gs = mem.take("group_score", [P, NT, NG0 + 8 - TOPG0], F32)
        t0 = dve.do(lambda e: e.memset(gs[:, :, :], BIG))
        dve.wait(t, t0)
        for i in range(NT):
            for g in range(NG0):
                t = dve.do(lambda e, i=i, g=g: e.max(g8[:, i, g, :], sb[:, i, g * 8:(g + 1) * 8]))
        dve.wait(t)
        t = dve.do(lambda e: e.tensor_tensor(gs[:, :, 0:NG0], g8[:, :, :, 0], g8[:, :, :, 1], ALU.add))
        gm, t = choose(gs, t, NG0, TOPG0, "group")
        low = mem.take("low", [P, NT, NG0], F32)
        ms = mem.take("masked", [P, NT, E0 + 8 - TOP0], F32)
        dve.wait(t)
        t0 = dve.do(lambda e: e.memset(ms[:, :, :], BIG))
        t = dve.do(lambda e: e.tensor_scalar(low[:, :, :], gm[:, :, :], 1.0, 1e30, ALU.subtract, ALU.mult))
        dve.wait(t0, t)
        for i in range(NT):
            out3 = ms[:, i, 0:E0].rearrange("p (g k) -> p g k", k=8)
            t = dve.do(lambda e, i=i, out3=out3: e.tensor_tensor(
                out3, sb[:, i, :].rearrange("p (g k) -> p g k", k=8),
                gm[:, i, :].unsqueeze(2).broadcast_to([P, NG0, 8]), ALU.mult))
        dve.wait(t)
        for i in range(NT):
            out3 = ms[:, i, 0:E0].rearrange("p (g k) -> p g k", k=8)
            t = dve.do(lambda e, i=i, out3=out3: e.tensor_tensor(
                out3, out3, low[:, i, :].unsqueeze(2).broadcast_to([P, NG0, 8]), ALU.add))
        mask, t = choose(ms, t, E0, TOP0, "expert")
        mb = mem.take("mask_bf", [P, NT, E0], BF16)
        tri = mem.take("before", [P, P], F32)
        trib = mem.take("before_bf", [P, P], BF16)
        onesb = mem.take("ones_bf", [P, P], BF16)
        t_tri = dma.start(dsem("tri"), tri[:, :], io["before"])
        dve.wait(t_tri, t)
        dve.do(lambda e: e.memset(onesb[:, :], 1.0))
        dve.do(lambda e: e.tensor_copy(trib[:, :], tri[:, :]))
        t_mb = dve.do(lambda e: e.tensor_copy(mb[:, :, :], mask[:, :, :]))
        pe.wait(t_mb, bank_free[7])
        for i in range(NT):
            t_pos = product(psum[:, 7, i * E0:(i + 1) * E0],
                            [(trib[:, :], mb[:, i, :])] + [(onesb[:, :], mb[:, j, :]) for j in range(i)])
        w = mem.take("w", [P, NT, E0], F32)
        keep = mem.take("keep", [P, NT, E0], F32)
        ws = mem.take("wsum", [P, NT], F32)
        t = dve.do(lambda e: e.tensor_tensor(w[:, :, :], sc[:, :, :], mask[:, :, :], ALU.mult))
        dve.wait(t)
        t = dve.do(lambda e: e.tensor_reduce(ws[:, :], w[:, :, :], AX.X, ALU.add))
        dve.wait(t)
        t = dve.do(lambda e: e.tensor_scalar(ws[:, :], ws[:, :], 1e-20, None, ALU.add))
        dve.wait(t)
        t = dve.do(lambda e: e.reciprocal(ws[:, :], ws[:, :]))
        dve.wait(t)
        t = dve.do(lambda e: e.tensor_tensor(w[:, :, :], w[:, :, :], ws[:, :].unsqueeze(2).broadcast_to([P, NT, E0]), ALU.mult))
        dve.wait(t, t_pos)
        pos = psum[:, 7, 0:NT * E0].rearrange("p (i n) -> p i n", n=E0)
        t = dve.do(lambda e: e.tensor_scalar(keep[:, :, :], pos, float(CAP0), 2.5, ALU.is_lt, ALU.mult))
        bank_free[7] = t
        dve.wait(t)
        t = dve.do(lambda e: e.tensor_tensor(w[:, :, :], w[:, :, :], keep[:, :, :], ALU.mult))
        GT, t_gt = gates_transposed(w, E0, E0, t)
        sel = mem.take("sel", [P, E0], F32)
        selr = mem.take("selr", [P, E0], F32R)
        t = dma.start(dsem("sel"), sel[:, :], io["sel0"])
        dve.wait(t)
        t_sel = dve.do(lambda e: e.tensor_copy(selr[:, :], sel[:, :]))
        pe.wait(t_sel)
        t = expert_blocks(io["f0_w"], NB0, False, lambda n: selr[:, n:n + 1].broadcast_to([P, P]), P, E0,
                          GT, t_gt, t_yh, t_yl)
        OT = mem.take("OT", [P, KD, T], F32)
        t = back_to_tokens(t, 4, OT)
        phase_barrier()
        return t

    def ffn2(t_in):
        Y, t_y = begin_ffn(t_in)
        t_yh, t_yl = transpose_y(Y, t_y)
        t, lg = logits(io["f2_gate"], E2, t_yh, t_yl)
        pr, t = softmax_rows(lg, E2, t, E2 + 8 - TOP2)
        mask, t = choose(pr, t, E2, TOP2, "expert")
        w = mem.take("w", [P, NT, E2], F32)
        dve.wait(t)
        t = dve.do(lambda e: e.tensor_tensor(w[:, :, :], pr[:, :, 0:E2], mask[:, :, :], ALU.mult))
        GT, t_gt = gates_transposed(w, E2, 32, t)
        sel = mem.take("sel", [64, E2 * I2], F32)
        selr = mem.take("selr", [64, E2 * I2], F32R)
        t = dma.start(dsem("sel"), sel[:, :], io["sel2"])
        dve.wait(t)
        t_sel = dve.do(lambda e: e.tensor_copy(selr[:, :], sel[:, :]))
        pe.wait(t_sel)
        rows = 32 + E2
        t = expert_blocks(io["f2_w"], NB2, True, lambda n: selr[0:rows, n * P:(n + 1) * P], rows, NB2,
                          GT, t_gt, t_yh, t_yl)
        OT = mem.take("OT", [P, KD, T], F32)
        t = back_to_tokens(t, 6, OT)
        phase_barrier()
        return t

    def ffn3(t_in):
        Y, t_y = begin_ffn(t_in)
        rw = mem.take("rms_w", [P, D], F32)
        t_rw = dma.start(dsem("rms_w"), rw[:, :], io["f3_rms"].rearrange("(a n) -> a n", a=1).broadcast_to([P, D]))
        sq = mem.take("sq", [P, D], F32)
        ss = mem.take("ss", [P, NT], F32)
        act.wait(*t_y)
        for i in range(NT):
            t = act.do(lambda e, i=i: e.activation(sq[:, :], Y[:, i, :], ACT.Square, accum_out=ss[:, i:i + 1]))
            act.wait(t)
        rr = mem.take("rr", [P, NT], F32)
        dve.wait(t)
        t = dve.do(lambda e: e.tensor_scalar(rr[:, :], ss[:, :], 1.0 / D, 1e-6, ALU.mult, ALU.add))
        dve.wait(t)
        pool.wait(t)
        t = pool.do(lambda e: e.tensor_tensor(rr[:, :], rr[:, :], exponent[:, :], ALU.pow))
        dve.wait(t, t_rw)
        t_y = [dve.do(lambda e, i=i: e.scalar_tensor_tensor(
            Y[:, i, :], Y[:, i, :], rr[:, i:i + 1], rw[:, :], ALU.mult, ALU.mult)) for i in range(NT)]
        t_yh, t_yl = transpose_y(Y, t_y)
        t, lg = logits(io["f3_gate"], E3, t_yh, t_yl)
        pr, t = softmax_rows(lg, E3, t, E3 + 8 - TOP3)
        mask, t = choose(pr, t, E3, TOP3, "expert")
        w = mem.take("w", [P, NT, E3], F32)
        ws = mem.take("wsum", [P, NT], F32)
        dve.wait(t)
        t = dve.do(lambda e: e.tensor_tensor(w[:, :, :], pr[:, :, 0:E3], mask[:, :, :], ALU.mult))
        dve.wait(t)
        t = dve.do(lambda e: e.tensor_reduce(ws[:, :], w[:, :, :], AX.X, ALU.add))
        dve.wait(t)
        t = dve.do(lambda e: e.reciprocal(ws[:, :], ws[:, :]))
        dve.wait(t)
        t = dve.do(lambda e: e.tensor_tensor(w[:, :, :], w[:, :, :], ws[:, :].unsqueeze(2).broadcast_to([P, NT, E3]), ALU.mult))
        GT, t_gt = gates_transposed(w, E3, 32, t)
        sel = mem.take("sel", [64, E3], F32)
        selr = mem.take("selr", [64, E3], F32R)
        t = dma.start(dsem("sel"), sel[:, :], io["sel3"])
        dve.wait(t)
        t_sel = dve.do(lambda e: e.tensor_copy(selr[:, :], sel[:, :]))
        pe.wait(t_sel)
        rows = 32 + E3
        t = expert_blocks(io["f3_w"], NB3, True, lambda n: selr[0:rows, n:n + 1].broadcast_to([rows, P]), rows, E3,
                          GT, t_gt, t_yh, t_yl)
        OT = mem.take("OT", [P, KD, T], F32)
        t = back_to_tokens(t, 7, OT)
        phase_barrier()
        return t

    def ffn1(t_in):
        Y, t_y = begin_ffn(t_in)
        NW = [I1 * KD, I1 * KD, D * I1 // P]
        raws = [mem.take("wraw", [P, n], F32) for n in NW]
        qs = [mem.take("wq", [P, n], BF16) for n in NW]
        part = mem.take("wpart", [P, 3], F32)
        for k, name in enumerate(("f1_gate", "f1_up", "f1_down")):
            t = dma.start(dsem(f"w1_{k}"), raws[k][:, :], io[name])
            dve.wait(t)
            t = dve.do(lambda e, k=k: e.tensor_reduce(part[:, k:k + 1], raws[k][:, :], AX.X, ALU.add,
                                                      apply_absolute_value=True))
        lw = mem.take("ln_w", [P, I1], F32)
        t_lw = dma.start(dsem("ln_w"), lw[:, :], io["f1_ln"].rearrange("(a n) -> a n", a=1).broadcast_to([P, I1]))
        pe.wait(t, t_ones, bank_free[0])
        t = pe.do(mm(psum[:, 0, 0:3], ones[:, :], part[:, :], True, True))
        inv = mem.take("w_unit", [P, 3], F32)
        sw = mem.take("w_scale", [P, 3], F32)
        dve.wait(t)
        t = dve.do(lambda e: e.tensor_scalar(inv[:, :], psum[:, 0, 0:3], 1.0 / (I1 * D), 1e-5, ALU.mult, ALU.max))
        bank_free[0] = t
        dve.wait(t)
        t = dve.do(lambda e: e.reciprocal(sw[:, :], inv[:, :]))
        dve.wait(t)

        def quantise(raw, scale, low, high, last_out):
            t = dve.do(lambda e: e.tensor_scalar(raw, raw, scale, ROUND, ALU.mult, ALU.add))
            dve.wait(t)
            t = dve.do(lambda e: e.tensor_scalar(raw, raw, ROUND, high, ALU.subtract, ALU.min))
            dve.wait(t)
            return dve.do(lambda e: e.tensor_scalar(last_out, raw, low, None, ALU.max))

        for k in range(3):
            t_wq = quantise(raws[k][:, :], sw[:, k:k + 1], -1.0, 1.0, qs[k][:, :])
        am = mem.take("amax", [P, NT], F32)
        sx = mem.take("x_scale", [P, NT], F32)
        ux = mem.take("x_unit", [P, NT], F32)
        cg = mem.take("c_gate", [P, NT], F32)
        cu = mem.take("c_up", [P, NT], F32)
        t = dve.do(lambda e: e.tensor_reduce(am[:, :], Y[:, :, :], AX.X, ALU.max, apply_absolute_value=True))
        dve.wait(t)
        t = dve.do(lambda e: e.tensor_scalar(am[:, :], am[:, :], 1e-5, None, ALU.max))
        dve.wait(t)
        t = dve.do(lambda e: e.reciprocal(sx[:, :], am[:, :]))
        dve.wait(t)
        t = dve.do(lambda e: e.tensor_scalar(sx[:, :], sx[:, :], 127.0, None, ALU.mult))
        t = dve.do(lambda e: e.tensor_scalar(ux[:, :], am[:, :], 1.0 / 127.0, None, ALU.mult))
        dve.wait(t)
        dve.do(lambda e: e.tensor_scalar(cg[:, :], ux[:, :], inv[:, 0:1], None, ALU.mult))
        t_cu = dve.do(lambda e: e.tensor_scalar(cu[:, :], ux[:, :], inv[:, 1:2], None, ALU.mult))
        t_q = [quantise(Y[:, i, :], sx[:, i:i + 1], -128.0, 127.0, Y[:, i, :]) for i in range(NT)]
        XT = mem.take("xqT", [P, KD, T], BF16)
        pe.wait(*t_q)
        for kd in range(KD):
            for a, tiles in enumerate((range(0, 4), range(4, NT))):
                bank = 4 + kd * 2 + a
                pe.wait(bank_free[bank])
                for i in tiles:
                    t = pe.do(lambda e, i=i, a=a, bank=bank, kd=kd: e.transpose(
                        psum[:, bank, (i - 4 * a) * P:(i - 4 * a + 1) * P], Y[:, i, kd * P:(kd + 1) * P], ident[:, :]))
                n = len(tiles) * P
                act.wait(t)
                t_xt = act.do(lambda e, kd=kd, a=a, n=n, bank=bank: e.activation(
                    XT[:, kd, a * 512:a * 512 + n], psum[:, bank, 0:n], ACT.Copy))
                bank_free[bank] = t_xt
        Wg = qs[0][:, :].rearrange("p (k n) -> p k n", k=KD)
        Wu = qs[1][:, :].rearrange("p (k n) -> p k n", k=KD)
        Wd = qs[2][:, :].rearrange("p (k n) -> p k n", k=I1 // P)
        Hb = mem.take("h", [P, NT, I1], F32)
        SG = [mem.take("sg", [P, I1], F32) for _ in range(2)]
        ss = mem.take("ss", [P, NT], F32)
        sg_free = [None] * 2
        pe.wait(t_xt, t_wq)
        t_sq = None
        for i in range(NT):
            b0 = 4 * (i % 2)
            for which, W in ((0, Wg), (1, Wu)):
                for n in range(2):
                    bank = b0 + 2 * which + n
                    pe.wait(bank_free[bank])
                    t = product(psum[:, bank, :], [(XT[:, kd, i * P:(i + 1) * P], W[:, kd, n * 512:(n + 1) * 512])
                                                   for kd in range(KD)])
                if which == 0:
                    t_gm = t
            sg = SG[i % 2]
            act.wait(t_gm, t_cu, sg_free[i % 2])
            t_s = act.do(lambda e, i=i, b0=b0, sg=sg: e.activation(
                sg[:, :].rearrange("p (a n) -> p a n", a=2), psum[:, b0:b0 + 2, :], ACT.Silu, scale=cg[:, i:i + 1]))
            bank_free[b0] = bank_free[b0 + 1] = t_s
            dve.wait(t_s, t)
            t_h = dve.do(lambda e, i=i, b0=b0, sg=sg: e.scalar_tensor_tensor(
                Hb[:, i, :].rearrange("p (a n) -> p a n", a=2), psum[:, b0 + 2:b0 + 4, :], cu[:, i:i + 1],
                sg[:, :].rearrange("p (a n) -> p a n", a=2), ALU.mult, ALU.mult))
            bank_free[b0 + 2] = bank_free[b0 + 3] = t_h
            act.wait(t_h)
            t_sq = act.do(lambda e, i=i, sg=sg: e.activation(sg[:, :], Hb[:, i, :], ACT.Square, accum_out=ss[:, i:i + 1]))
            sg_free[i % 2] = t_sq
            act.wait(t_sq)
        rr = mem.take("rr", [P, NT], F32)
        dve.wait(t_sq)
        t = dve.do(lambda e: e.tensor_scalar(rr[:, :], ss[:, :], 1.0 / I1, 1e-6, ALU.mult, ALU.add))
        dve.wait(t)
        pool.wait(t)
        t = pool.do(lambda e: e.tensor_tensor(rr[:, :], rr[:, :], exponent[:, :], ALU.pow))
        dve.wait(t, t_lw)
        for i in range(NT):
            t = dve.do(lambda e, i=i: e.scalar_tensor_tensor(
                Hb[:, i, :], Hb[:, i, :], rr[:, i:i + 1], lw[:, :], ALU.mult, ALU.mult))
        dve.wait(t)
        hm = mem.take("hmax", [P, NT], F32)
        sh = mem.take("h_scale", [P, NT], F32)
        cd = mem.take("c_down", [P, NT], F32)
        t = dve.do(lambda e: e.tensor_reduce(hm[:, :], Hb[:, :, :], AX.X, ALU.max, apply_absolute_value=True))
        dve.wait(t)
        t = dve.do(lambda e: e.tensor_scalar(hm[:, :], hm[:, :], 1e-5, None, ALU.max))
        dve.wait(t)
        t = dve.do(lambda e: e.reciprocal(sh[:, :], hm[:, :]))
        dve.wait(t)
        t = dve.do(lambda e: e.tensor_scalar(sh[:, :], sh[:, :], 127.0, None, ALU.mult))
        t2 = dve.do(lambda e: e.tensor_scalar(cd[:, :], hm[:, :], 1.0 / 127.0, inv[:, 2:3], ALU.mult, ALU.mult))
        dve.wait(t, t2, t_tanh)
        t_cd = dve.do(lambda e: e.tensor_scalar(cd[:, :], cd[:, :], tanh_g[:, 5:6], None, ALU.mult))
        HT_ = mem.take("hqT", [P, I1 // P, T], BF16)
        ring = 0
        for i in range(NT):
            t = quantise(Hb[:, i, :], sh[:, i:i + 1], -128.0, 127.0, Hb[:, i, :])
            for a in range(2):
                bank = ring % 4
                ring += 1
                pe.wait(t, bank_free[bank])
                for k in range(4):
                    t_p = pe.do(lambda e, i=i, a=a, k=k, bank=bank: e.transpose(
                        psum[:, bank, k * P:(k + 1) * P], Hb[:, i, (4 * a + k) * P:(4 * a + k + 1) * P], ident[:, :]))
                act.wait(t_p)
                t_ht = act.do(lambda e, i=i, a=a, bank=bank: e.activation(
                    HT_[:, 4 * a:4 * a + 4, i * P:(i + 1) * P],
                    psum[:, bank, :].rearrange("p (k n) -> p k n", k=4), ACT.Copy))
                bank_free[bank] = t_ht
            bank = 4 + i % 4
            pe.wait(t_ht, bank_free[bank])
            t = product(psum[:, bank, 0:D], [(HT_[:, k, i * P:(i + 1) * P], Wd[:, k, :]) for k in range(I1 // P)])
            dve.wait(t, t_cd)
            t_x = dve.do(lambda e, i=i, bank=bank: e.scalar_tensor_tensor(
                X[:, i, :], psum[:, bank, 0:D], cd[:, i:i + 1], X[:, i, :], ALU.mult, ALU.add))
            bank_free[bank] = t_x
        phase_barrier()
        return t_x

    prepare_context()
    phase_barrier()
    t_now = t_x
    ffns = [ffn0, ffn1, ffn2, ffn3]
    for n in range(4):
        if steps > 2 * n:
            t_now = attention(n, t_now)
        if steps > 2 * n + 1:
            t_now = ffns[n](t_now)
    sp.wait(t_now)
    t_out = dma.start(dsem("out"), out.rearrange("b s d -> (b s) d").rearrange("(i p) d -> p i d", p=P), X[:, :, :])
    sp.wait(t_out)

    with nc.Block() as block:
        for name, stream in (("sync", sp), ("tensor", pe), ("scalar", act), ("vector", dve), ("gpsimd", pool)):
            block.__class__
            {"sync": block.sync, "tensor": block.tensor, "scalar": block.scalar, "vector": block.vector,
             "gpsimd": block.gpsimd}[name](stream.emit)


def layouts(i):
    c = np.ascontiguousarray
    a = {"x": c(i["x"]), "ctx": c(i["ctx_512"]), "g_xattn": c(i["g_xattn"]), "g_ffn": c(i["g_ffn"])}
    heads = lambda w, k, n: c(w.reshape(H, k, n).transpose(1, 0, 2))
    kv = i["L0_xattn_Wkv_expand"]
    a["a0_Wq"] = heads(i["L0_xattn_Wq"], 16, D)
    a["a0_Wk"] = heads(kv[:D], 16, DC)
    a["a0_Wv"] = heads(kv[D:], 16, DC)
    a["a0_WoT"] = heads(c(i["L0_xattn_Wout"].T), 16, D)
    for n in (1, 2, 3):
        w = lambda s: i[f"L{n}_xattn_{s}"]
        a[f"a{n}_Wq"] = heads(w("Wq"), K1, D)
        a[f"a{n}_WoT"] = heads(c(w("Wo").T), K1, D)
        a[f"a{n}_Wv"] = c(w("w_kc_kv").transpose(1, 0, 2))
        a[f"a{n}_WqrT"] = c(w("W_qr").transpose(2, 0, 1))
        a[f"a{n}_WkrT"] = c(w("W_kr").transpose(2, 0, 1))
        if n == 2:
            a["a2_Wc"] = c(w("w_kc_q").transpose(1, 0, 2))
        else:
            a[f"a{n}_WcT"] = c(w("w_kc_q").transpose(0, 2, 1).reshape(H, 2, DQH, K1).transpose(2, 0, 1, 3))

    def chunks(w):
        n = w.shape[0] // P
        return w.reshape(n, P, KD, P).transpose(0, 3, 2, 1).reshape(n, P, KD * P)

    up = np.concatenate([chunks(i["L0_ffn_w1"].reshape(-1, D)), chunks(i["L0_ffn_shared_up_w"])])
    dn = np.concatenate([i["L0_ffn_w2"].transpose(0, 2, 1).reshape(-1, D), i["L0_ffn_shared_down_w"].T]).reshape(-1, P, D)
    a["f0_w"] = c(np.concatenate([up, dn], -1))
    flat = lambda w: w.reshape(-1, D)
    dn = flat(i["L2_ffn_w_down"].transpose(0, 2, 1)).reshape(-1, P, D)
    a["f2_w"] = c(np.concatenate([chunks(flat(i["L2_ffn_w_gate"])), chunks(flat(i["L2_ffn_w_up"])), dn], -1))
    hid = lambda e, s: np.concatenate([flat(i["L3_ffn_" + e].transpose(0, 2, 1)), i["L3_ffn_" + s].T])
    dn = np.concatenate([flat(i["L3_ffn_w_down"]), i["L3_ffn_sw_down"]]).reshape(-1, P, D)
    a["f3_w"] = c(np.concatenate([chunks(hid("w_gate", "sw_gate")), chunks(hid("w_up", "sw_up")), dn], -1))
    rows = lambda w: c(w.reshape(-1, P, w.shape[-1]).transpose(1, 0, 2))
    a["f0_gate"] = rows(i["L0_ffn_gate_w"].T)
    a["f2_gate"] = rows(i["L2_ffn_gate_w"].T)
    a["f3_gate"] = rows(i["L3_ffn_router_w"])
    a["f0_bias"] = c(i["L0_ffn_e_bias"])
    a["f3_rms"] = c(i["L3_ffn_rms_weight"])
    a["f1_ln"] = c(i["L1_ffn_ln_weight"])
    for k in ("gate", "up", "down"):
        w = rows(i[f"L1_ffn_w_{k}"].T)
        a[f"f1_{k}"] = c(w.reshape(P, -1))
    a.update(constants())
    a["blockdiag"] = a["blockdiag"].reshape(NT, T)
    return a


def program(nc, arrays, steps=8):
    io = {k: nc.dram_tensor("in_" + k, v.shape, F32, kind="ExternalInput").ap() for k, v in arrays.items()}
    out = nc.dram_tensor("out", (B, S, D), F32, kind="ExternalOutput").ap()
    build(nc, io, out, steps)


def kernel(**inputs):
    import concourse.bacc as bacc
    from concourse.bass_utils import run_bass_kernel_spmd

    arrays = layouts({k: np.asarray(v) for k, v in inputs.items()})
    nc = bacc.Bacc("TRN2", target_bir_lowering=False, num_devices=1)
    program(nc, arrays)
    r = run_bass_kernel_spmd(nc, [{"in_" + k: v for k, v in arrays.items()}], core_ids=[0])
    return r.results[0]["out"]
```

```python
from collections import namedtuple

import numpy as np

import concourse.bass as bass
from concourse import mybir

F32, F32R, BF16 = mybir.dt.float32, mybir.dt.float32r, mybir.dt.bfloat16
ALU = mybir.AluOpType
ACT = mybir.ActivationFunctionType
AX = mybir.AxisListType

P = 128
B, S, D = 16, 56, 256
T = B * S
NT = T // P
KD = D // P
HT = T // 2
L, DC = 1500, 64
NL, LP = 12, 125
H = 16
K1 = 128
DQ, DQH = 192, 96
E0, TOP0, NG0, TOPG0, CAP0 = 64, 6, 8, 4, 64
I1 = 1024
E2, I2, TOP2 = 16, 176, 6
E3, TOP3 = 8, 2
NB0, NB2, NB3 = E0 + 4, E2 * I2 // P, E3 + 1
BIG = 3.0e38
ROUND = 1.5 * 2.0 ** 23

Tick = namedtuple("Tick", "sem value")


class Stream:

    def __init__(self, sem):
        self.sem, self.count, self.items, self.seen = sem, 0, [], {}

    def wait(self, *ticks):
        for t in ticks:
            if t is not None and self.seen.get(t.sem, 0) < t.value:
                self.seen[t.sem] = t.value
                self.items.append(lambda e, t=t: e.wait_ge(t.sem, t.value))

    def run(self, fn):
        self.items.append(fn)

    def do(self, fn):
        self.count += 1
        self.items.append(lambda e: fn(e).then_inc(self.sem, 1))
        return Tick(self.sem, self.count)

    def tick(self):
        return Tick(self.sem, self.count)

    def emit(self, engine):
        for item in self.items:
            item(engine)


class Loads:

    def __init__(self, stream):
        self.stream, self.counts = stream, {}

    def start(self, sem, out, src, n=1):
        self.counts[sem] = self.counts.get(sem, 0) + 16
        self.stream.items.append(lambda e: e.dma_start(out, src).then_inc(sem, 16))
        return Tick(sem, self.counts[sem])


class Memory:

    def __init__(self, nc):
        self.nc, self.at, self.end, self.n = nc, (nc.sbuf_base + 31) // 32 * 32, nc.sbuf_usable_end, 0

    def take(self, name, shape, dt):
        size = int(np.prod(shape[1:])) * (2 if dt == BF16 else 4)
        self.n += 1
        t = self.nc.alloc_sbuf_tensor_at(f"{name}_{self.n}", list(shape), dt, offset=self.at)
        self.at += (size + 31) // 32 * 32
        assert self.at <= self.end, (name, self.at, self.end)
        return t


def rope_tables(length, dim):
    f = np.float32
    inv = (f(1.0) / np.power(f(10000.0), np.arange(0, dim, 2, dtype=f) / f(dim))).astype(f)
    angle = np.arange(length, dtype=f)[:, None] * inv[None, :]
    return np.repeat(np.sin(angle), 2, axis=-1).astype(f), np.repeat(np.cos(angle), 2, axis=-1).astype(f)


def constants():
    f = np.float32
    c = {}
    c["ident"] = np.eye(P, dtype=f)
    c["before"] = np.triu(np.ones((P, P), f), 1)
    sin, cos = rope_tables(L, DC)
    signed = sin.copy()
    signed[:, :DC // 2] *= -1
    c["cos_k"] = cos.reshape(LP, NL * DC)
    c["sin_k"] = signed.reshape(LP, NL * DC)
    sin, cos = rope_tables(S, DQ)
    halves = [cos[:, :DQH], sin[:, :DQH], cos[:, DQH:], sin[:, DQH:]]
    c["rope_q"] = np.stack([x.T for x in halves], 1).astype(f)
    late = np.where(np.arange(S)[None, :] > np.arange(S)[:, None], f(-1e30), f(0))
    s_of_q = (np.arange(NT * P) % S).reshape(NT, P).T
    c["mask_q"] = late[s_of_q].reshape(P, NT * S).astype(f)
    c["mask_k"] = np.tile(late.T, (1, H // 2)).astype(f)
    bd = np.zeros((64, NT, P), f)
    bd[np.arange(NT), np.arange(NT)] = bd[32 + np.arange(NT), np.arange(NT)] = 1
    c["blockdiag"] = bd
    c["sel0"] = (np.arange(P)[:, None] % E0 == np.arange(E0)[None, :]).astype(f)
    rows = np.arange(64)[:, None] % 32
    c["sel2"] = (rows == np.arange(E2 * I2)[None, :] // I2).astype(f)
    c["sel3"] = (rows == np.arange(E3)[None, :]).astype(f)
    return c


def build(nc, io, out, steps=8):
    mem = Memory(nc)
    sems = {n: nc.alloc_semaphore(n) for n in ("pe_done", "act_done", "dve_done", "pool_done")}
    pe, act, dve, pool = (Stream(sems[n]) for n in ("pe_done", "act_done", "dve_done", "pool_done"))
    sp = Stream(None)
    dma = Loads(sp)
    load_sems = {}

    def dsem(name):
        if name not in load_sems:
            load_sems[name] = nc.alloc_semaphore("dma_" + name)
        return load_sems[name]

    psum = nc.alloc_psum_tensor("psum", [P, 8, 512], F32)
    bank_free = [None] * 8

    def phase_barrier():
        ticks = [s.tick() for s in (pe, act, dve, pool)]
        loads = [Tick(s, n) for s, n in dma.counts.items()]
        for s in (pe, act, dve, pool, sp):
            s.wait(*ticks, *loads)

    def mm(o, lhsT, rhs, start, stop, **kw):
        return lambda e: e.matmul(o, lhsT, rhs, start=start, stop=stop, **kw)

    def product(o, pairs, skip=False):
        for n, (a, b) in enumerate(pairs):
            last = n == len(pairs) - 1
            f = mm(o, a, b, n == 0, last, skip_group_check=skip)
            if last:
                return pe.do(f)
            pe.run(f)

    def split_pairs(ah, al, bh, bl):
        return [(ah, bh), (ah, bl), (al, bh)]

    X = mem.take("X", [P, NT, D], F32)
    YH = mem.take("YH", [P, KD, T], F32R)
    YL = mem.take("YL", [P, KD, T], F32R)
    ident = mem.take("ident", [P, P], F32)
    ones = mem.take("ones", [P, P], F32)
    exponent = mem.take("exponent", [P, NT], F32)
    gates = mem.take("gates", [P, 8], F32)
    tanh_g = mem.take("tanh_g", [P, 8], F32)
    V = mem.take("V", [P, B, NL * DC], F32)
    base = mem.at

    KT = nc.dram_tensor("kt_scratch", (B, P, L), F32, kind="Internal").ap()

    t_ident = dma.start(dsem("ident"), ident[:, :], io["ident"])
    t_x = dma.start(dsem("x"), X[:, :, :], io["x"].rearrange("b s d -> (b s) d").rearrange("(i p) d -> p i d", p=P))
    dma.start(dsem("g"), gates[:, 0:4], io["g_xattn"].rearrange("(a n) -> a n", a=1).broadcast_to([P, 4]))
    t_g = dma.start(dsem("g"), gates[:, 4:8], io["g_ffn"].rearrange("(a n) -> a n", a=1).broadcast_to([P, 4]))
    t_ones = dve.do(lambda e: e.memset(ones[:, :], 1.0))
    t_exponent = dve.do(lambda e: e.memset(exponent[:, :], -0.5))
    act.wait(t_g)
    t_tanh = act.do(lambda e: e.activation(tanh_g[:, :], gates[:, :], ACT.Tanh))

    def dve_barrier_self():
        dve.wait(dve.tick())

    def layer_norm(t_in, Y, stats, mv, rstd):
        dve.wait(t_in)
        for i in range(NT):
            dve.do(lambda e, i=i: e.bn_stats(stats[:, i, :], X[:, i, :]))
        dve.wait(dve.tick())
        for i in range(NT):
            dve.do(lambda e, i=i: e.bn_aggr(mv[:, i, :], stats[:, i, :]))
        dve.wait(dve.tick())
        t = dve.do(lambda e: e.tensor_scalar(rstd[:, :], mv[:, :, 1], 1e-5, None, ALU.add))
        pool.wait(t, t_exponent)
        t = pool.do(lambda e: e.tensor_tensor(rstd[:, :], rstd[:, :], exponent[:, :], ALU.pow))
        dve.wait(t)
        return [dve.do(lambda e, i=i: e.tensor_scalar(Y[:, i, :], X[:, i, :], mv[:, i, 0:1], rstd[:, i:i + 1],
                                                      ALU.subtract, ALU.mult)) for i in range(NT)]

    def transpose_y(Y, t_y):
        pe.wait(t_ident, *t_y)
        t_hi = t_lo = None
        for kd in range(KD):
            for a, tiles in enumerate((range(0, 4), range(4, NT))):
                bank = 4 + (kd * 2 + a) % 4
                pe.wait(bank_free[bank])
                for i in tiles:
                    t = pe.do(lambda e, i=i, kd=kd, bank=bank, a=a: e.transpose(
                        psum[:, bank, (i - 4 * a) * P:(i - 4 * a + 1) * P], Y[:, i, kd * P:(kd + 1) * P], ident[:, :]))
                n = len(tiles) * P
                cols = slice(a * 512, a * 512 + n)
                act.wait(t)
                t_hi = act.do(lambda e, kd=kd, bank=bank, n=n, cols=cols: e.activation(
                    YH[:, kd, cols], psum[:, bank, 0:n], ACT.Copy))
                dve.wait(t_hi)
                t_lo = dve.do(lambda e, kd=kd, bank=bank, n=n, cols=cols: e.tensor_tensor(
                    YL[:, kd, cols], psum[:, bank, 0:n], YH[:, kd, cols].bitcast(F32), ALU.subtract))
                bank_free[bank] = t_lo
        return t_hi, t_lo

    def norm_buffers():
        return (mem.take("Y", [P, NT, D], F32), mem.take("stats", [P, NT, 6], F32),
                mem.take("mv", [P, NT, 2], F32), mem.take("rstd", [P, NT], F32))

    def back_to_tokens(acc_ticks, gate_col, OT):
        ts = []
        for m in range(KD):
            for c in range(2):
                act.wait(acc_ticks)
                ts.append(act.do(lambda e, m=m, c=c: e.activation(
                    OT[:, m, c * HT:(c + 1) * HT], psum[:, m * 2 + c, 0:HT], ACT.Copy)))
        for bank in range(4):
            bank_free[bank] = ts[-1]
        pe.wait(ts[-1])
        t_x = None
        for g in range(4):
            bank = 4 + g
            tiles = [i for i in (2 * g, 2 * g + 1) if i < NT]
            pe.wait(bank_free[bank])
            for i in tiles:
                for m in range(KD):
                    t = pe.do(lambda e, i=i, m=m, bank=bank, g=g: e.transpose(
                        psum[:, bank, (i - 2 * g) * D + m * P:(i - 2 * g) * D + (m + 1) * P],
                        OT[:, m, i * P:(i + 1) * P], ident[:, :]))
            n = len(tiles) * D
            dve.wait(t, t_tanh)
            t_x = dve.do(lambda e, g=g, bank=bank, n=n: e.scalar_tensor_tensor(
                X[:, 2 * g:2 * g + n // D, :].rearrange("p a d -> p (a d)"), psum[:, bank, 0:n],
                tanh_g[:, gate_col:gate_col + 1],
                X[:, 2 * g:2 * g + n // D, :].rearrange("p a d -> p (a d)"), ALU.mult, ALU.add))
            bank_free[bank] = t_x
        return t_x

    def prepare_context():
        mem.at = base
        cos = mem.take("cos_k", [P, NL * DC], F32)
        sin = mem.take("sin_k", [P, NL * DC], F32)
        raw = [mem.take("ctx_raw", [P, NL, DC], F32) for _ in range(3)]
        rot = [mem.take("ctx_rot", [P, NL, DC], F32) for _ in range(2)]
        kt = [mem.take("kt", [P, L], F32R) for _ in range(2)]
        dma.start(dsem("rope"), cos[0:LP, :], io["cos_k"])
        t_tab = dma.start(dsem("rope"), sin[0:LP, :], io["sin_k"])
        t_raw_free, t_rot_free, t_kt_free, t_kt_st = [None] * 3, [None] * 2, [None] * 2, [None] * 2
        loads = []
        half = DC // 2
        cos3 = cos[0:LP, :].rearrange("p (j d) -> p j d", d=DC)
        sin3 = sin[0:LP, :].rearrange("p (j d) -> p j d", d=DC)
        for b in range(B):
            r = raw[b % 3]
            sp.wait(t_raw_free[b % 3])
            t_load = dma.start(dsem(f"raw{b % 3}"), r[0:LP, :, :].rearrange("p j d -> p (j d)"),
                               io["ctx"][b].rearrange("(p j) d -> p (j d)", j=NL))
            q = rot[b % 2]
            Vb = V[0:LP, b, :].rearrange("p (j d) -> p j d", d=DC)
            pool.wait(t_load, t_tab, t_rot_free[b % 2])
            pool.do(lambda e, r=r, q=q: e.tensor_tensor(q[0:LP, :, 0:half], r[0:LP, :, half:DC], sin3[:, :, 0:half], ALU.mult))
            t_q = pool.do(lambda e, r=r, q=q: e.tensor_tensor(q[0:LP, :, half:DC], r[0:LP, :, 0:half], sin3[:, :, half:DC], ALU.mult))
            dve.wait(t_load, t_tab)
            t_c = dve.do(lambda e, r=r, Vb=Vb: e.tensor_tensor(Vb, r[0:LP, :, :], cos3, ALU.mult))
            t_raw_free[b % 3] = t_c
            sp.wait(t_q)
            dve.wait(t_c, t_q)
            t_v = dve.do(lambda e, q=q, Vb=Vb: e.tensor_tensor(Vb, Vb, q[0:LP, :, :], ALU.add))
            t_rot_free[b % 2] = t_v
            k = kt[b % 2]
            for g in range(3):
                bank = (3 * b + g) % 8
                pe.wait(t_v, t_ident, bank_free[bank])
                for j in range(4):
                    t_p = pe.do(lambda e, b=b, g=g, j=j, bank=bank: e.transpose(
                        psum[0:DC, bank, j * LP:(j + 1) * LP],
                        V[0:LP, b, (4 * g + j) * DC:(4 * g + j + 1) * DC], ident[0:LP, 0:LP]))
                cols = slice(g * 4 * LP, (g + 1) * 4 * LP)
                act.wait(t_p, t_kt_free[b % 2])
                t_h = act.do(lambda e, k=k, cols=cols, bank=bank: e.activation(
                    k[0:DC, cols], psum[0:DC, bank, 0:4 * LP], ACT.Copy))
                dve.wait(t_h)
                t_l = dve.do(lambda e, k=k, cols=cols, bank=bank: e.tensor_tensor(
                    k[DC:P, cols], psum[0:DC, bank, 0:4 * LP], k[0:DC, cols].bitcast(F32), ALU.subtract))
                bank_free[bank] = t_l
            sp.wait(t_l)
            t_kt_free[b % 2] = dma.start(dsem(f"kt_st{b % 2}"), KT[b], k[:, :].bitcast(F32))
        return t_kt_free

    def attention(layer, t_in):
        mem.at = base
        first = layer == 0
        KH = 16 if first else K1
        MH = mem.take("MH", [P, H // 2, D], F32R)
        ML = mem.take("ML", [P, H // 2, D], F32R)
        qr_at = mem.at
        QR = mem.take("QR", [P, H // 2, T], F32)
        top = mem.at
        AH = mem.take("AH", [P, KD, H * DC], F32R)
        AL = mem.take("AL", [P, KD, H * DC], F32R)
        a_end = mem.at
        w = lambda n: io[f"a{layer}_{n}"]

        mem.at = qr_at
        WoT = mem.take("WoT", [P, H, D], F32)
        Wv = mem.take("Wv", [P, H, DC], F32)
        mem.at = top if layer == 2 else a_end
        Wq = mem.take("Wq", [P, H, D], F32)
        t_wq = dma.start(dsem("wq"), Wq[0:KH, :, :], w("Wq"))
        t_wo = dma.start(dsem("wo"), WoT[0:KH, :, :], w("WoT"))
        t_wv = dma.start(dsem("wv"), Wv[0:KH, :, :], w("Wv"))
        pe.wait(t_wv, t_wo)
        for g in range(4):
            bank = 4 + g
            pe.wait(bank_free[bank])
            for h in range(4 * g, 4 * g + 4):
                odd, pair = h % 2, (h % 4) // 2
                t = pe.do(mm(psum[odd * DC:(odd + 1) * DC, bank, pair * D:(pair + 1) * D],
                             Wv[0:KH, h, :], WoT[0:KH, h, :], True, True))
            act.wait(t)
            t_MH = act.do(lambda e, g=g, bank=bank: e.activation(
                MH[:, 2 * g:2 * g + 2, :].rearrange("p a d -> p (a d)"), psum[:, bank, :], ACT.Copy))
            dve.wait(t_MH)
            t_ML = dve.do(lambda e, g=g, bank=bank: e.tensor_tensor(
                ML[:, 2 * g:2 * g + 2, :].rearrange("p a d -> p (a d)"), psum[:, bank, :],
                MH[:, 2 * g:2 * g + 2, :].rearrange("p a d -> p (a d)").bitcast(F32), ALU.subtract))
            bank_free[bank] = t_ML

        G = mem.take("G", [P, H, DC], F32)
        t_G = None
        U = None
        if first:
            t_G = dma.start(dsem("wk"), G[0:KH, :, :], w("Wk"))
        else:
            if layer == 2:
                Wc = mem.take("Wc", [P, H, DQ], F32)
            else:
                Wc = mem.take("WcT", [DQH, H, 2, K1], F32)
            U = mem.take("U", [DQH, H, 2, DC], F32)
            wqr_at = mem.at
            Wqr = mem.take("WqrT", [64, H, DQ], F32)
            Wkr = mem.take("WkrT", [64, H, DC], F32)
            t_qr = dma.start(dsem("wqr"), Wqr[:, :, :], w("WqrT"))
            t_kr = dma.start(dsem("wkr"), Wkr[:, :, :], w("WkrT"))
            if layer == 2:
                t_c = dma.start(dsem("wc"), Wc[:, :, :], w("Wc"))
            else:
                t_c = dma.start(dsem("wc"), Wc[:, :, :, :], w("WcT"))
            pe.wait(t_qr, t_kr)
            for g in range(4):
                pe.wait(bank_free[g])
                for h in range(4 * g, 4 * g + 4):
                    for c in range(2):
                        o = psum[0:DQH, g, ((h % 4) * 2 + c) * DC:((h % 4) * 2 + c + 1) * DC]
                        t = pe.do(mm(o, Wqr[:, h, c * DQH:(c + 1) * DQH], Wkr[:, h, :], True, True))
                act.wait(t)
                bank_free[g] = t_U = act.do(lambda e, g=g: e.activation(
                    U[:, 4 * g:4 * g + 4, :, :].rearrange("p h c d -> p (h c d)"), psum[0:DQH, g, :], ACT.Copy))
            if layer != 2:
                pe.wait(t_U, t_c)
                for g in range(2):
                    pe.wait(bank_free[4 + g])
                    for h in range(8 * g, 8 * g + 8):
                        t = product(psum[:, 4 + g, (h % 8) * DC:(h % 8 + 1) * DC],
                                    [(Wc[:, h, c, :], U[:, h, c, :]) for c in range(2)])
                    act.wait(t)
                    bank_free[4 + g] = t_G = act.do(lambda e, g=g: e.activation(
                        G[:, 8 * g:8 * g + 8, :].rearrange("p h d -> p (h d)"), psum[:, 4 + g, :], ACT.Copy))
        t_AL = t_AH = None
        if layer != 2:
            pe.wait(t_wq, t_G)
            for kd in range(KD):
                for g in range(2):
                    bank = kd * 2 + g
                    pe.wait(bank_free[bank])
                    for h in range(8 * g, 8 * g + 8):
                        t = pe.do(mm(psum[:, bank, (h % 8) * DC:(h % 8 + 1) * DC],
                                     Wq[0:KH, h, kd * P:(kd + 1) * P], G[0:KH, h, :], True, True))
                    cols = slice(g * 512, (g + 1) * 512)
                    scale = 1.0 / np.sqrt(16.0) if first else 1.0
                    act.wait(t)
                    t_AH = act.do(lambda e, kd=kd, bank=bank, cols=cols, scale=scale: e.activation(
                        AH[:, kd, cols], psum[:, bank, :], ACT.Copy, scale=float(scale)))
                    dve.wait(t_AH)
                    t_AL = dve.do(lambda e, kd=kd, bank=bank, cols=cols, scale=scale: e.scalar_tensor_tensor(
                        AL[:, kd, cols], psum[:, bank, :], float(scale), AH[:, kd, cols].bitcast(F32),
                        ALU.mult, ALU.subtract))
                    bank_free[bank] = t_AL
        if layer == 2:
            mem.at = wqr_at
            sp.wait(t_U)
            dve.wait(t_U)
        Y, stats, mv, rstd = norm_buffers()
        t_y = layer_norm(t_in, Y, stats, mv, rstd)
        t_yh, t_yl = transpose_y(Y, t_y)

        if layer != 2:
            pe.wait(t_yh, t_yl, t_AH, t_AL)
            for mt in range(H // 2):
                for c in range(2):
                    bank = (mt * 2 + c) % 8
                    pe.wait(bank_free[bank])
                    pairs = []
                    for kd in range(KD):
                        m, n = slice(mt * P, (mt + 1) * P), slice(c * HT, (c + 1) * HT)
                        pairs += split_pairs(AH[:, kd, m], AL[:, kd, m], YH[:, kd, n], YL[:, kd, n])
                    t = product(psum[:, bank, 0:HT], pairs)
                    act.wait(t)
                    bank_free[bank] = act.do(lambda e, mt=mt, c=c, bank=bank: e.activation(
                        QR[:, mt, c * HT:(c + 1) * HT], psum[:, bank, 0:HT], ACT.Copy))
        else:
            rope = mem.take("rope_q", [DQH, 4, S], F32)
            t_rope = dma.start(dsem("rope_q"), rope[:, :, :], io["rope_q"])
            BH = [mem.take("BH", [P, KD, DQ], F32R) for _ in range(2)]
            BL = [mem.take("BL", [P, KD, DQ], F32R) for _ in range(2)]
            terms = [mem.take("rope_term", [DQH, 4, HT], F32) for _ in range(2)]
            turned = [mem.take("turned", [DQH, 2, HT], F32) for _ in range(2)]
            t_turn_free, t_term_free, t_B_free = [None] * 2, [None] * 2, [None] * 2
            unit = 0
            for h in range(H):
                pe.wait(t_wq, t_c, bank_free[0])
                for kd in range(KD):
                    t = pe.do(mm(psum[:, 0, kd * DQ:(kd + 1) * DQ], Wq[:, h, kd * P:(kd + 1) * P],
                                 Wc[:, h, :], True, True))
                bh, bl = BH[h % 2], BL[h % 2]
                act.wait(t, t_B_free[h % 2])
                t_bh = act.do(lambda e, bh=bh: e.activation(
                    bh[:, :, :].rearrange("p k q -> p (k q)"), psum[:, 0, 0:KD * DQ], ACT.Copy))
                dve.wait(t_bh)
                t_bl = dve.do(lambda e, bh=bh, bl=bl: e.tensor_tensor(
                    bl[:, :, :].rearrange("p k q -> p (k q)"), psum[:, 0, 0:KD * DQ],
                    bh[:, :, :].rearrange("p k q -> p (k q)").bitcast(F32), ALU.subtract))
                bank_free[0] = t_bl
                for c in range(2):
                    n = slice(c * HT, (c + 1) * HT)
                    banks = (1 + 2 * (unit % 2), 2 + 2 * (unit % 2))
                    pe.wait(t_bh, t_bl, t_yh, t_yl)
                    for half, bank in enumerate(banks):
                        pe.wait(bank_free[bank])
                        m = slice(half * DQH, (half + 1) * DQH)
                        pairs = []
                        for kd in range(KD):
                            pairs += split_pairs(bh[:, kd, m], bl[:, kd, m], YH[:, kd, n], YL[:, kd, n])
                        t = product(psum[0:DQH, bank, 0:HT], pairs)
                    if c == 1:
                        t_B_free[h % 2] = t
                    tm, tu = terms[unit % 2], turned[unit % 2]
                    dve.wait(t, t_rope, t_term_free[unit % 2])
                    for k, (half, tab) in enumerate(((0, 0), (1, 1), (1, 2), (0, 3))):
                        t_m = dve.do(lambda e, k=k, half=half, tab=tab, tm=tm, banks=banks: e.tensor_tensor(
                            tm[:, k, :].rearrange("p (b s) -> p b s", s=S),
                            psum[0:DQH, banks[half], 0:HT].rearrange("p (b s) -> p b s", s=S),
                            rope[:, tab:tab + 1, :].broadcast_to([DQH, HT // S, S]), ALU.mult))
                    for bank in banks:
                        bank_free[bank] = t_m
                    pool.wait(t_m, t_turn_free[unit % 2])
                    pool.do(lambda e, tm=tm, tu=tu: e.tensor_tensor(tu[:, 0, :], tm[:, 0, :], tm[:, 1, :], ALU.subtract))
                    t_t = pool.do(lambda e, tm=tm, tu=tu: e.tensor_tensor(tu[:, 1, :], tm[:, 2, :], tm[:, 3, :], ALU.add))
                    t_term_free[unit % 2] = t_t
                    bank = 5 + unit % 3
                    odd = h % 2
                    pe.wait(t_t, t_U, bank_free[bank])
                    t = product(psum[odd * DC:(odd + 1) * DC, bank, 0:HT],
                                [(U[:, h, half, :], tu[:, half, :]) for half in range(2)])
                    t_turn_free[unit % 2] = t
                    act.wait(t)
                    bank_free[bank] = act.do(lambda e, h=h, odd=odd, n=n, bank=bank: e.activation(
                        QR[odd * DC:(odd + 1) * DC, h // 2, n], psum[odd * DC:(odd + 1) * DC, bank, 0:HT], ACT.Copy))
                    unit += 1
        t_qr_done = act.tick()
        phase_barrier()

        mem.at = top
        o_rows = 32 + NT
        Q1 = [mem.take("Q1", [P, T], F32R) for _ in range(3 if first else 2)]
        Q2 = [mem.take("Q2", [P, T], F32R) for _ in range(5 if first else 2)]
        bd = mem.take("bd", [64, T], F32)
        RT = mem.take("RT", [64, P], F32R)
        RD = mem.take("RD", [64, T], F32R)
        rden = mem.take("rden", [P, NT], F32)
        ones_r = mem.take("ones_r", [64, P], F32R)
        t_bd = dma.start(dsem("bd"), bd[:, :], io["blockdiag"])
        t_zero = dve.do(lambda e: e.memset(RT[:, :].bitcast(F32), 0.0))
        t_one_r = dve.do(lambda e: e.tensor_copy(ones_r[:, :], ones[0:64, :]))

        def make_queries(b, q1, q2, t_free):
            tok = slice(b * S, (b + 1) * S)

            def copy_hi(odd, copy):
                raw = QR[odd * DC:(odd + 1) * DC, :, tok]
                act.wait(t_qr_done, t_free)
                return act.do(lambda e: e.activation(
                    q1[copy * DC:(copy + 1) * DC, odd * HT:(odd + 1) * HT].rearrange("p (m s) -> p m s", s=S),
                    raw, ACT.Copy))

            def lo(odd, t1):
                raw = QR[odd * DC:(odd + 1) * DC, :, tok]
                part = slice(odd * DC, (odd + 1) * DC)
                dve.wait(t1, t_free)
                return dve.do(lambda e: e.tensor_tensor(
                    q2[0:DC, odd * HT:(odd + 1) * HT].rearrange("p (m s) -> p m s", s=S), raw,
                    q1[part, odd * HT:(odd + 1) * HT].bitcast(F32).rearrange("p (m s) -> p m s", s=S), ALU.subtract))

            return copy_hi, lo

        def spread_max(q2, neg_max, t_max, bank, t_free):
            pe.wait(t_max, t_ident)
            t = pe.do(lambda e: e.transpose(psum[0:NT, bank, 0:P], neg_max, ident[:, :]))
            dve.wait(t, t_bd, t_free)
            t = dve.do(lambda e: e.tensor_tensor(
                q2[DC:DC + NT, :].rearrange("p (j q) -> p j q", q=P),
                psum[0:NT, bank, 0:P].unsqueeze(1).broadcast_to([NT, NT, P]),
                bd[0:NT, :].rearrange("p (j q) -> p j q", q=P), ALU.mult))
            bank_free[bank] = t
            return t

        def sum_keys(tile, rows, t_sums, bank):
            pe.wait(t_sums, t_ones)
            for j in range(NT):
                t = pe.do(mm(psum[:, bank, j:j + P], tile[0:rows, j * P:(j + 1) * P], ones[0:rows, :], True, True))
            dve.wait(t)
            t_r = dve.do(lambda e: e.reciprocal(rden[:, :], psum[:, bank, 0:NT]))
            bank_free[bank] = t_r
            return t, t_r

        state = {"rd_free": None}

        def spread_reciprocals(t_r, bank):
            pe.wait(t_r)
            t = pe.do(lambda e: e.transpose(psum[0:NT, bank, 0:P], rden[:, :], ident[:, :]))
            dve.wait(t, t_zero)
            t = dve.do(lambda e: e.tensor_copy(RT[0:NT, :], psum[0:NT, bank, 0:P]))
            dve.wait(t)
            t = dve.do(lambda e: e.tensor_tensor(RT[32:o_rows, :], psum[0:NT, bank, 0:P],
                                                 RT[0:NT, :].bitcast(F32), ALU.subtract))
            bank_free[bank] = t
            dve.wait(t, t_bd, state["rd_free"])
            return dve.do(lambda e: e.tensor_tensor(
                RD[0:o_rows, :].rearrange("p (j q) -> p j q", q=P),
                RT[0:o_rows, :].bitcast(F32).unsqueeze(1).broadcast_to([o_rows, NT, P]),
                bd[0:o_rows, :].rearrange("p (j q) -> p j q", q=P), ALU.mult))

        def divide(b, odd, o1, t_o1, t_rd, bank):
            pe.wait(t_rd, t_one_r)
            cols = slice(odd * HT, (odd + 1) * HT)
            t = pe.do(mm(psum[:, bank, 0:HT], ones_r[0:o_rows, :], RD[0:o_rows, cols], True, True))
            state["rd_free"] = t
            dve.wait(t, t_o1)
            t = dve.do(lambda e: e.tensor_tensor(
                QR[odd * DC:(odd + 1) * DC, :, b * S:(b + 1) * S],
                o1[:, cols].rearrange("p (m s) -> p m s", s=S),
                psum[0:DC, bank, 0:HT].rearrange("p (m s) -> p m s", s=S), ALU.mult))
            bank_free[bank] = t
            return t

        if first:
            K1t = mem.take("K1", [P, T], F32R)
            K2t = mem.take("K2", [P, T], F32R)
            V0 = mem.take("V0", [S, B, DC], F32)
            mqf = mem.take("mask_q", [P, NT * S], F32)
            mkf = mem.take("mask_k", [S, HT], F32)
            mq = mem.take("mask_q_bf", [P, NT * S], BF16)
            mk = mem.take("mask_k_bf", [S, HT], BF16)
            ident_b = mem.take("ident_bf", [P, P], BF16)
            E = [mem.take("E", [S, T], F32) for _ in range(2)]
            O1 = [mem.take("O1", [DC, T], F32) for _ in range(4)]
            nm = [mem.take("nm", [P, NT], F32) for _ in range(2)]
            t_v0 = dma.start(dsem("v0"), V0[:, :, :], io["ctx"][:, 0:S, :].rearrange("b l d -> l b d"))
            dma.start(dsem("masks"), mqf[:, :], io["mask_q"])
            t_masks = dma.start(dsem("masks"), mkf[:, :], io["mask_k"])
            t_k2 = dve.do(lambda e: e.memset(K2t[DC:DC + NT, :].bitcast(F32), 1.0))
            dve.wait(t_masks, t_ident)
            dve.do(lambda e: e.tensor_copy(mq[:, :], mqf[:, :]))
            dve.do(lambda e: e.tensor_copy(mk[:, :], mkf[:, :]))
            t_masks = dve.do(lambda e: e.tensor_copy(ident_b[:, :], ident[:, :]))
            for c in range(2):
                pe.wait(t_v0, bank_free[c])
                for b in range(8 * c, 8 * c + 8):
                    t = pe.do(lambda e, b=b, c=c: e.transpose(psum[0:DC, c, (b % 8) * S:(b % 8 + 1) * S], V0[:, b, :],
                                                              ident[0:S, 0:S]))
                n = slice(c * HT, (c + 1) * HT)
                act.wait(t)
                act.do(lambda e, c=c, n=n: e.activation(K1t[0:DC, n], psum[0:DC, c, 0:HT], ACT.Copy))
                t_h = act.do(lambda e, c=c, n=n: e.activation(K2t[0:DC, n], psum[0:DC, c, 0:HT], ACT.Copy))
                dve.wait(t_h)
                t_keys = dve.do(lambda e, c=c, n=n: e.tensor_tensor(
                    K1t[DC:P, n], psum[0:DC, c, 0:HT], K1t[0:DC, n].bitcast(F32), ALU.subtract))
                bank_free[c] = t_keys
            tk = {}
            at = [2]

            def next_bank():
                at[0] += 1
                bank = at[0] % 8
                pe.wait(bank_free[bank])
                return bank

            def queries0(b):
                copy_hi, lo = make_queries(b, Q1[b % 3], Q2[b % 5], tk.get(("scored", b - 3)))
                for odd in range(2):
                    for copy in range(2):
                        tk["q1", b] = copy_hi(odd, copy)
                    tk["q2", b] = lo(odd, tk["q1", b])

            def maxima0(b):
                bank = next_bank()
                pe.wait(tk["q1", b], t_keys, t_masks)
                pe.run(mm(psum[:, bank, 0:NT * S], ident_b[:, :], mq[:, :], True, False, skip_group_check=True))
                for j in range(NT):
                    t = pe.do(mm(psum[:, bank, j * S:(j + 1) * S], Q1[b % 3][:, j * P:(j + 1) * P],
                                 K1t[:, b * S:(b + 1) * S], False, j == NT - 1, skip_group_check=True))
                dve.wait(t, tk.get(("spread", b - 2)))
                tk["max", b] = t = dve.do(lambda e: e.tensor_reduce(
                    nm[b % 2][:, :], psum[:, bank, 0:NT * S].rearrange("p (j l) -> p j l", l=S), AX.X, ALU.max, negate=True))
                bank_free[bank] = t

            def spread0(b):
                tk["spread", b] = spread_max(Q2[b % 5], nm[b % 2][:, :], tk["max", b], next_bank(), tk.get(("scored", b - 5)))

            def scores0(b):
                cols = slice(b * S, (b + 1) * S)
                for c in range(2):
                    bank = next_bank()
                    n = slice(c * HT, (c + 1) * HT)
                    o = psum[0:S, bank, 0:HT]
                    pe.wait(tk["q1", b], tk["q2", b], tk["spread", b], t_k2)
                    pe.run(mm(o, ident_b[0:S, 0:S], mk[:, :], True, False))
                    pe.run(mm(o, K1t[:, cols], Q1[b % 3][:, n], False, False))
                    t = pe.do(mm(o, K2t[0:DC + NT, cols], Q2[b % 5][0:DC + NT, n], False, True))
                    act.wait(t, tk.get(("summed", b - 2)), tk.get(("valued", b - 2)))
                    t_e = act.do(lambda e, o=o, n=n: e.activation(E[b % 2][:, n], o, ACT.Exp))
                    bank_free[bank] = t_e
                tk["scored", b], tk["exp", b] = t, t_e

            def values0(b):
                for c in range(2):
                    bank = next_bank()
                    pe.wait(tk["exp", b])
                    n = slice(c * HT, (c + 1) * HT)
                    t = pe.do(mm(psum[0:DC, bank, 0:HT], V0[:, b, :], E[b % 2][:, n], True, True))
                    act.wait(t, tk.get(("divided", b - 4)))
                    t_o = act.do(lambda e, bank=bank, n=n: e.activation(O1[b % 4][:, n], psum[0:DC, bank, 0:HT], ACT.Copy))
                    bank_free[bank] = t_o
                tk["valued", b], tk["o1", b] = t, t_o
                dve.wait(tk.get(("rt", b - 1)))
                tk["summed", b], tk["recip", b] = sum_keys(E[b % 2], S, tk["exp", b], next_bank())

            def reciprocals0(b):
                tk["rd", b] = tk["rt", b] = spread_reciprocals(tk["recip", b], next_bank())

            def divide0(b):
                for odd in range(2):
                    t = divide(b, odd, O1[b % 4], tk["o1", b], tk["rd", b], next_bank())
                tk["divided", b] = t

            stages = [queries0, maxima0, spread0, scores0, values0, reciprocals0, divide0]
            for step in range(B + len(stages) - 1):
                for n in reversed(range(len(stages))):
                    if 0 <= step - n < B:
                        stages[n](step - n)
            t_out_last = tk["divided", B - 1]
        else:
            NE = 6
            CW = L // 3
            K1t = [mem.take("K1", [P, L], F32R) for _ in range(3)]
            K2t = [mem.take("K2", [P, L], F32R) for _ in range(2)]
            E = [mem.take("E", [P, T], F32) for _ in range(NE)]
            SA = [mem.take("SA", [P, T], F32) for _ in range(2)]
            O1 = mem.take("O1", [DC, T], F32)
            mx = mem.take("mx", [P, 2, NT * 3], F32)
            nm = mem.take("nm", [P, 2, NT], F32)
            for k in K2t:
                t_k2 = dve.do(lambda e, k=k: e.memset(k[DC:DC + NT, :].bitcast(F32), 1.0))
            tk = {}
            at = [0]

            def small_bank():
                at[0] += 1
                bank = 6 + at[0] % 2
                pe.wait(bank_free[bank])
                return bank

            def load_keys(b):
                sp.wait(tk.get(("scored", b - 3)))
                tk["k1", b] = dma.start(dsem(f"k1{b % 3}"), K1t[b % 3][:, :].bitcast(F32), KT[b])

            def copy_keys(b, n):
                act.wait(tk["k1", b], tk.get(("scored", b - 2)))
                cols = slice(n * CW, (n + 1) * CW)
                tk["k2", b] = act.do(lambda e: e.activation(
                    K2t[b % 2][0:DC, cols], K1t[b % 3][0:DC, cols].bitcast(F32), ACT.Copy))

            def queries(b, n):
                copy_hi, lo = make_queries(b, Q1[b % 2], Q2[b % 2], tk.get(("scored", b - 2)))
                if n < 4:
                    tk["q1", b] = copy_hi(n // 2, n % 2)
                else:
                    tk["q2", b] = lo(n - 4, tk["q1", b])

            def max_unit(b, j, c):
                bank = small_bank()
                pe.wait(tk["q1", b], tk["k1", b])
                t = pe.do(mm(psum[:, bank, 0:CW], Q1[b % 2][:, j * P:(j + 1) * P], K1t[b % 3][:, c * CW:(c + 1) * CW],
                             True, True))
                dve.wait(t)
                bank_free[bank] = tk["mx", b] = dve.do(lambda e: e.tensor_reduce(
                    mx[:, b % 2, j * 3 + c:j * 3 + c + 1], psum[:, bank, 0:CW], AX.X, ALU.max))

            def max_total(b):
                dve.wait(tk["mx", b])
                tk["max", b] = dve.do(lambda e: e.tensor_reduce(
                    nm[:, b % 2, :], mx[:, b % 2, :].rearrange("p (j c) -> p j c", c=3), AX.X, ALU.max, negate=True))

            def max_spread(b):
                tk["spread", b] = spread_max(Q2[b % 2], nm[:, b % 2, :], tk["max", b], small_bank(),
                                             tk.get(("scored", b - 2)))

            def ring(b, k):
                return (b * NL + k) % NE

            readers = {}

            def scores(b, k):
                pair = (0, 1) if k % 2 == 0 else (2, 3)
                cols = slice(k * LP, (k + 1) * LP)
                pe.wait(tk["k1", b], tk["k2", b], tk["q1", b], tk["q2", b], tk["spread", b], t_k2, bank_free[pair[0]])
                for c in range(2):
                    pe.run(mm(psum[0:LP, pair[c], 0:HT], K1t[b % 3][:, cols], Q1[b % 2][:, c * HT:(c + 1) * HT], True, False))
                for c in range(2):
                    t = pe.do(mm(psum[0:LP, pair[c], 0:HT], K2t[b % 2][0:DC + NT, cols],
                                 Q2[b % 2][0:DC + NT, c * HT:(c + 1) * HT], False, True))
                if k == NL - 1:
                    tk["scored", b] = t
                n = ring(b, k)
                act.wait(t, *readers.get(n, ()))
                t = act.do(lambda e: e.activation(E[n][0:LP, :].rearrange("p (c q) -> p c q", c=2),
                                                  psum[0:LP, pair[0]:pair[0] + 2, 0:HT], ACT.Exp))
                bank_free[pair[0]] = bank_free[pair[1]] = t
                tk["exp", b, k] = t
                readers[n] = []
                if k == 0:
                    return
                eng = pool
                a = SA[b % 2][0:LP, :]
                prev = E[ring(b, 0)][0:LP, :] if k == 1 else a
                eng.wait(t, tk.get(("summed", b - 2)) if k == 1 else tk["sum", b])
                t = eng.do(lambda e: e.tensor_tensor(a, prev, E[n][0:LP, :], ALU.add))
                tk["sum", b] = t
                readers[n].append(t)
                if k == 1:
                    readers[ring(b, 0)].append(t)

            def values(b, pair, c):
                ks = (2 * pair, 2 * pair + 1)
                pe.wait(tk["exp", b, ks[1]], bank_free[4 + c])
                for k in ks:
                    t = pe.do(mm(psum[(k % 2) * DC:(k % 2 + 1) * DC, 4 + c, 0:HT], V[0:LP, b, k * DC:(k + 1) * DC],
                                 E[ring(b, k)][0:LP, c * HT:(c + 1) * HT], pair == 0, pair == NL // 2 - 1))
                for k in ks:
                    readers[ring(b, k)].append(t)
                if pair == NL // 2 - 1:
                    cols = slice(c * HT, (c + 1) * HT)
                    act.wait(t, tk.get(("divided", b - 1)))
                    t = act.do(lambda e: e.activation(O1[:, cols], psum[DC:P, 4 + c, 0:HT], ACT.Copy))
                    dve.wait(t)
                    t = dve.do(lambda e: e.tensor_tensor(O1[:, cols], psum[0:DC, 4 + c, 0:HT], O1[:, cols], ALU.add))
                    bank_free[4 + c] = tk["o1", b] = t

            def total(b):
                dve.wait(tk.get(("rt", b - 1)))
                tk["summed", b], tk["recip", b] = sum_keys(SA[b % 2], LP, tk["sum", b], small_bank())

            def reciprocals(b):
                tk["rd", b] = tk["rt", b] = spread_reciprocals(tk["recip", b], small_bank())

            def division(b, odd):
                tk["divided", b] = divide(b, odd, O1, tk["o1", b], tk["rd", b], small_bank())

            units = [(j, c) for j in range(NT) for c in range(3)]
            load_keys(0)
            load_keys(1)
            for n in range(3):
                copy_keys(0, n)
            for n in range(6):
                queries(0, n)
            for j, c in units:
                max_unit(0, j, c)
            max_total(0)
            max_spread(0)
            for b in range(B):
                todo = list(units) if b + 1 < B else []
                if b + 2 < B:
                    load_keys(b + 2)
                for slot in range(2 * NL):
                    if slot % 2 == 0:
                        scores(b, slot // 2)
                    elif slot >= 4:
                        values(b, slot // 4 - 1, (slot % 4) // 2)
                    elif b > 0:
                        values(b - 1, NL // 2 - 1, (slot % 4) // 2)
                    if b + 1 < B:
                        if slot < 4:
                            queries(b + 1, slot)
                        if slot in (12, 15):
                            queries(b + 1, 4 + (slot - 12) // 3)
                        if slot in (7, 13, 17):
                            copy_keys(b + 1, (7, 13, 17).index(slot))
                        if slot >= 4:
                            for _ in range(2 if slot % 3 == 0 and slot < 20 else 1):
                                if todo:
                                    max_unit(b + 1, *todo.pop(0))
                                    if not todo:
                                        max_total(b + 1)
                        if slot == 21:
                            max_spread(b + 1)
                    if b > 0:
                        if slot == 7:
                            total(b - 1)
                        if slot == 11:
                            reciprocals(b - 1)
                        if slot == 16:
                            division(b - 1, 0)
                        if slot == 18:
                            division(b - 1, 1)
            for c in range(2):
                values(B - 1, NL // 2 - 1, c)
            total(B - 1)
            reciprocals(B - 1)
            for odd in range(2):
                division(B - 1, odd)
            t_out_last = tk["divided", B - 1]
        phase_barrier()

        mem.at = top
        CHh = mem.take("CH", [P, H // 2, T], F32R)
        CL = mem.take("CL", [P, H // 2, T], F32R)
        for m in range(H // 2):
            act.wait(t_out_last)
            t_h = act.do(lambda e, m=m: e.activation(CHh[:, m, :], QR[:, m, :], ACT.Copy))
            dve.wait(t_h)
            t_l2 = dve.do(lambda e, m=m: e.tensor_tensor(CL[:, m, :], QR[:, m, :], CHh[:, m, :].bitcast(F32), ALU.subtract))
        pe.wait(t_h, t_l2)
        t_x = None
        for i in range(NT):
            bank = i
            pe.wait(bank_free[bank])
            tok = slice(i * P, (i + 1) * P)
            pairs = []
            for m in range(H // 2):
                pairs += split_pairs(CHh[:, m, tok], CL[:, m, tok], MH[:, m, :], ML[:, m, :])
            t = product(psum[:, bank, 0:D], pairs)
            dve.wait(t, t_tanh)
            t_x = dve.do(lambda e, i=i, bank=bank: e.scalar_tensor_tensor(
                X[:, i, :], psum[:, bank, 0:D], tanh_g[:, layer:layer + 1], X[:, i, :], ALU.mult, ALU.add))
            bank_free[bank] = t_x
        phase_barrier()
        return t_x

    def logits(gate, n_exp, t_yh, t_yl):
        GW = mem.take("gate_w", [P, KD, n_exp], F32)
        GH = mem.take("gate_hi", [P, KD, n_exp], F32R)
        GL = mem.take("gate_lo", [P, KD, n_exp], F32R)
        t = dma.start(dsem("gate_w"), GW[:, :, :], gate)
        dve.wait(t)
        t = dve.do(lambda e: e.tensor_copy(GH[:, :, :], GW[:, :, :]))
        dve.wait(t)
        t = dve.do(lambda e: e.tensor_tensor(GL[:, :, :], GW[:, :, :], GH[:, :, :].bitcast(F32), ALU.subtract))
        pe.wait(t, t_yh, t_yl, bank_free[4])
        for i in range(NT):
            tok = slice(i * P, (i + 1) * P)
            pairs = []
            for kd in range(KD):
                pairs += split_pairs(YH[:, kd, tok], YL[:, kd, tok], GH[:, kd, :], GL[:, kd, :])
            t = product(psum[:, 4, i * n_exp:(i + 1) * n_exp], pairs)
        return t, psum[:, 4, 0:NT * n_exp].rearrange("p (i n) -> p i n", n=n_exp)

    def choose(values, t_in, n, top, name):
        wide = n + 8 - top
        v8 = mem.take(name + "_top8", [P, NT, 8], F32)
        left = mem.take(name + "_left", [P, NT, wide], F32)
        mask = mem.take(name + "_mask", [P, NT, n], F32)
        dve.wait(t_in)
        for i in range(NT):
            t = dve.do(lambda e, i=i: e.max(v8[:, i, :], values[:, i, :]))
        dve.wait(t)
        for i in range(NT):
            t = dve.do(lambda e, i=i: e.match_replace(left[:, i, :], v8[:, i, :], values[:, i, :], -BIG))
        dve.wait(t)
        t = dve.do(lambda e: e.tensor_tensor(mask[:, :, :], values[:, :, 0:n], left[:, :, 0:n], ALU.not_equal))
        return mask, t

    def softmax_rows(src, n, t_in, wide):
        m = mem.take("lmax", [P, NT], F32)
        ex = mem.take("lexp", [P, NT, n], F32)
        sm = mem.take("lsum", [P, NT], F32)
        pr = mem.take("probs", [P, NT, wide], F32)
        t0 = dve.do(lambda e: e.memset(pr[:, :, :], BIG))
        dve.wait(t_in)
        t = dve.do(lambda e: e.tensor_reduce(m[:, :], src, AX.X, ALU.max))
        dve.wait(t)
        t = dve.do(lambda e: e.tensor_tensor(ex[:, :, :], src, m[:, :].unsqueeze(2).broadcast_to([P, NT, n]), ALU.subtract))
        bank_free[4] = t
        act.wait(t)
        t = act.do(lambda e: e.activation(ex[:, :, :], ex[:, :, :], ACT.Exp))
        dve.wait(t)
        t = dve.do(lambda e: e.tensor_reduce(sm[:, :], ex[:, :, :], AX.X, ALU.add))
        dve.wait(t)
        t = dve.do(lambda e: e.reciprocal(sm[:, :], sm[:, :]))
        dve.wait(t, t0)
        t = dve.do(lambda e: e.tensor_tensor(pr[:, :, 0:n], ex[:, :, :], sm[:, :].unsqueeze(2).broadcast_to([P, NT, n]), ALU.mult))
        return pr, t

    def gates_transposed(Gt, n, lo_row, t_in):
        GT = mem.take("GT", [P, T], F32R)
        t0 = None
        if lo_row != n:
            t0 = dve.do(lambda e: e.memset(GT[:, :].bitcast(F32), 0.0))
        pe.wait(t_in)
        for a, tiles in enumerate((range(0, 4), range(4, NT))):
            bank = 5 + a
            pe.wait(bank_free[bank])
            for i in tiles:
                t = pe.do(lambda e, i=i, a=a, bank=bank: e.transpose(
                    psum[0:n, bank, (i - 4 * a) * P:(i - 4 * a + 1) * P], Gt[:, i, :], ident[:, :]))
            w = len(tiles) * P
            cols = slice(a * 512, a * 512 + w)
            dve.wait(t, t0)
            t = dve.do(lambda e, cols=cols, bank=bank, w=w: e.tensor_copy(GT[0:n, cols], psum[0:n, bank, 0:w]))
            dve.wait(t)
            t = dve.do(lambda e, cols=cols, bank=bank, w=w: e.tensor_tensor(
                GT[lo_row:lo_row + n, cols], psum[0:n, bank, 0:w], GT[0:n, cols].bitcast(F32), ALU.subtract))
            bank_free[bank] = t
        return GT, t

    def expert_blocks(weights, nblk, swiglu, selector, sel_rows, n_gated, GT, t_gt, t_yh, t_yl):
        WID = 768 if swiglu else 512
        NW = 4
        WS = [mem.take("WS", [P, WID], F32) for _ in range(NW)]
        WH = [mem.take("WH", [P, WID], F32R) for _ in range(NW)]
        WL = [mem.take("WL", [P, WID], F32R) for _ in range(NW)]
        NH = 4
        R = [mem.take("R", [P, HT], F32) for _ in range(NH)]
        G1 = [mem.take("G1", [P, HT], F32) for _ in range(NH)]
        HF = [mem.take("HF", [P, HT], F32) for _ in range(NH)]
        HH = [mem.take("HH", [P, HT], F32R) for _ in range(NH)]
        HL = [mem.take("HL", [P, HT], F32R) for _ in range(NH)]
        ws_free, w_free = [None] * NW, [None] * NW
        r_free, h_free, hf_free = [None] * NH, [None] * NH, [None] * NH
        ring = [0]
        t_w = {}

        def next_bank():
            bank = 4 + ring[0] % 4
            ring[0] += 1
            pe.wait(bank_free[bank])
            return bank

        t_load = {}

        def fetch(n):
            k = n % NW
            sp.wait(*(ws_free[k] or ()))
            t_load[n] = dma.start(dsem(f"ws{k}"), WS[k][:, :], weights[n])

        def split(n):
            k = n % NW
            act.wait(t_load[n], w_free[k])
            t_h = act.do(lambda e: e.activation(WH[k][:, :], WS[k][:, :], ACT.Copy))
            pool.wait(t_h, w_free[k])
            t_l = pool.do(lambda e: e.tensor_tensor(WL[k][:, :], WS[k][:, :], WH[k][:, :].bitcast(F32), ALU.subtract))
            ws_free[k] = (t_h, t_l)
            t_w[n] = (t_h, t_l)

        def up(n, c):
            k, u = n % NW, (2 * n + c) % NH
            cols = slice(c * HT, (c + 1) * HT)
            pe.wait(*t_w[n], t_yh, t_yl)
            outs = []
            for part in range(2 if swiglu else 1):
                bank = next_bank()
                pairs = []
                for kd in range(KD):
                    m = slice(part * D + kd * P, part * D + (kd + 1) * P)
                    pairs += split_pairs(WH[k][:, m], WL[k][:, m], YH[:, kd, cols], YL[:, kd, cols])
                t = product(psum[:, bank, 0:HT], pairs)
                outs.append((bank, t))
            gated = n < n_gated
            if gated:
                gb = next_bank()
                pe.wait(t_gt)
                t_g = pe.do(mm(psum[:, gb, 0:HT], selector(n), GT[0:sel_rows, cols], True, True))
            r, g1, hf, hh, hl = R[u], G1[u], HF[u], HH[u], HL[u]
            bank, t = outs[0]
            act.wait(t, *(r_free[u] or ()))
            t_r = act.do(lambda e: e.activation(r[:, :], psum[:, bank, 0:HT], ACT.Silu if swiglu else ACT.Relu))
            bank_free[bank] = t_r
            dve.wait(t_r)
            if swiglu:
                b2, t2 = outs[1]
                dve.wait(t2)
                first_out = g1 if gated else hf
                if not gated:
                    dve.wait(hf_free[u])
                t = dve.do(lambda e: e.tensor_tensor(first_out[:, :], r[:, :], psum[:, b2, 0:HT], ALU.mult))
                bank_free[b2] = t
                if gated:
                    dve.wait(t, t_g, hf_free[u])
                    t = dve.do(lambda e: e.tensor_tensor(hf[:, :], g1[:, :], psum[:, gb, 0:HT], ALU.mult))
                    bank_free[gb] = t
            else:
                if gated:
                    dve.wait(t_g)
                    t = dve.do(lambda e: e.tensor_tensor(g1[:, :], r[:, :], psum[:, gb, 0:HT], ALU.mult))
                    bank_free[gb] = t
                    dve.wait(t)
                src = g1 if gated else r
                dve.wait(hf_free[u])
                t = dve.do(lambda e: e.tensor_tensor(hf[:, :], src[:, :], r[:, :], ALU.mult))
            r_free[u] = (t,)
            dve.wait(t, h_free[u])
            t_hh = dve.do(lambda e: e.tensor_copy(hh[:, :], hf[:, :]))
            pool.wait(t_hh, h_free[u])
            t_hl = pool.do(lambda e: e.tensor_tensor(hl[:, :], hf[:, :], hh[:, :].bitcast(F32), ALU.subtract))
            hf_free[u] = t_hl
            return t_hh, t_hl

        def down(n, c, ticks):
            k, u = n % NW, (2 * n + c) % NH
            off = WID - D
            pe.wait(*ticks)
            for m in range(KD):
                mcol = slice(off + m * P, off + (m + 1) * P)
                if n == 0:
                    pe.wait(bank_free[m * 2 + c])
                prs = split_pairs(WH[k][:, mcol], WL[k][:, mcol], HH[u][:, :], HL[u][:, :])
                for q, (a, bb) in enumerate(prs):
                    f = mm(psum[:, m * 2 + c, 0:HT], a, bb, n == 0 and q == 0, n == nblk - 1 and q == 2)
                    if q == 2:
                        t = pe.do(f)
                    else:
                        pe.run(f)
            h_free[u] = t
            if c == 1:
                w_free[k] = t
            return t

        for n in range(3):
            fetch(n)
        split(0)
        split(1)
        pending = []
        for n in range(nblk):
            if n + 3 < nblk:
                fetch(n + 3)
            for c in range(2):
                pending.append((n, c, up(n, c)))
                if len(pending) > 2:
                    down(*pending.pop(0))
            if n + 2 < nblk:
                split(n + 2)
        while pending:
            t = down(*pending.pop(0))
        return t

    def begin_ffn(t_in):
        mem.at = base
        Y, stats, mv, rstd = norm_buffers()
        t_y = layer_norm(t_in, Y, stats, mv, rstd)
        return Y, t_y

    def ffn0(t_in):
        Y, t_y = begin_ffn(t_in)
        t_yh, t_yl = transpose_y(Y, t_y)
        t, lg = logits(io["f0_gate"], E0, t_yh, t_yl)
        sc = mem.take("scores", [P, NT, E0], F32)
        sb = mem.take("biased", [P, NT, E0], F32)
        eb = mem.take("e_bias", [P, E0], F32)
        t_eb = dma.start(dsem("eb"), eb[:, :], io["f0_bias"].rearrange("(a n) -> a n", a=1).broadcast_to([P, E0]))
        act.wait(t)
        t_sc = act.do(lambda e: e.activation(sc[:, :, :], lg, ACT.Sigmoid))
        bank_free[4] = t_sc
        dve.wait(t_sc, t_eb)
        t = dve.do(lambda e: e.tensor_tensor(sb[:, :, :], sc[:, :, :], eb[:, :].unsqueeze(1).broadcast_to([P, NT, E0]), ALU.add))
        g8 = mem.take("group_top8", [P, NT, NG0, 8], F32)
        gs = mem.take("group_score", [P, NT, NG0 + 8 - TOPG0], F32)
        t0 = dve.do(lambda e: e.memset(gs[:, :, :], BIG))
        dve.wait(t, t0)
        for i in range(NT):
            for g in range(NG0):
                t = dve.do(lambda e, i=i, g=g: e.max(g8[:, i, g, :], sb[:, i, g * 8:(g + 1) * 8]))
        dve.wait(t)
        t = dve.do(lambda e: e.tensor_tensor(gs[:, :, 0:NG0], g8[:, :, :, 0], g8[:, :, :, 1], ALU.add))
        gm, t = choose(gs, t, NG0, TOPG0, "group")
        low = mem.take("low", [P, NT, NG0], F32)
        ms = mem.take("masked", [P, NT, E0 + 8 - TOP0], F32)
        dve.wait(t)
        t0 = dve.do(lambda e: e.memset(ms[:, :, :], BIG))
        t = dve.do(lambda e: e.tensor_scalar(low[:, :, :], gm[:, :, :], 1.0, 1e30, ALU.subtract, ALU.mult))
        dve.wait(t0, t)
        for i in range(NT):
            out3 = ms[:, i, 0:E0].rearrange("p (g k) -> p g k", k=8)
            t = dve.do(lambda e, i=i, out3=out3: e.tensor_tensor(
                out3, sb[:, i, :].rearrange("p (g k) -> p g k", k=8),
                gm[:, i, :].unsqueeze(2).broadcast_to([P, NG0, 8]), ALU.mult))
        dve.wait(t)
        for i in range(NT):
            out3 = ms[:, i, 0:E0].rearrange("p (g k) -> p g k", k=8)
            t = dve.do(lambda e, i=i, out3=out3: e.tensor_tensor(
                out3, out3, low[:, i, :].unsqueeze(2).broadcast_to([P, NG0, 8]), ALU.add))
        mask, t = choose(ms, t, E0, TOP0, "expert")
        mb = mem.take("mask_bf", [P, NT, E0], BF16)
        tri = mem.take("before", [P, P], F32)
        trib = mem.take("before_bf", [P, P], BF16)
        onesb = mem.take("ones_bf", [P, P], BF16)
        t_tri = dma.start(dsem("tri"), tri[:, :], io["before"])
        dve.wait(t_tri, t)
        dve.do(lambda e: e.memset(onesb[:, :], 1.0))
        dve.do(lambda e: e.tensor_copy(trib[:, :], tri[:, :]))
        t_mb = dve.do(lambda e: e.tensor_copy(mb[:, :, :], mask[:, :, :]))
        pe.wait(t_mb, bank_free[7])
        for i in range(NT):
            t_pos = product(psum[:, 7, i * E0:(i + 1) * E0],
                            [(trib[:, :], mb[:, i, :])] + [(onesb[:, :], mb[:, j, :]) for j in range(i)])
        w = mem.take("w", [P, NT, E0], F32)
        keep = mem.take("keep", [P, NT, E0], F32)
        ws = mem.take("wsum", [P, NT], F32)
        t = dve.do(lambda e: e.tensor_tensor(w[:, :, :], sc[:, :, :], mask[:, :, :], ALU.mult))
        dve.wait(t)
        t = dve.do(lambda e: e.tensor_reduce(ws[:, :], w[:, :, :], AX.X, ALU.add))
        dve.wait(t)
        t = dve.do(lambda e: e.tensor_scalar(ws[:, :], ws[:, :], 1e-20, None, ALU.add))
        dve.wait(t)
        t = dve.do(lambda e: e.reciprocal(ws[:, :], ws[:, :]))
        dve.wait(t)
        t = dve.do(lambda e: e.tensor_tensor(w[:, :, :], w[:, :, :], ws[:, :].unsqueeze(2).broadcast_to([P, NT, E0]), ALU.mult))
        dve.wait(t, t_pos)
        pos = psum[:, 7, 0:NT * E0].rearrange("p (i n) -> p i n", n=E0)
        t = dve.do(lambda e: e.tensor_scalar(keep[:, :, :], pos, float(CAP0), 2.5, ALU.is_lt, ALU.mult))
        bank_free[7] = t
        dve.wait(t)
        t = dve.do(lambda e: e.tensor_tensor(w[:, :, :], w[:, :, :], keep[:, :, :], ALU.mult))
        GT, t_gt = gates_transposed(w, E0, E0, t)
        sel = mem.take("sel", [P, E0], F32)
        selr = mem.take("selr", [P, E0], F32R)
        t = dma.start(dsem("sel"), sel[:, :], io["sel0"])
        dve.wait(t)
        t_sel = dve.do(lambda e: e.tensor_copy(selr[:, :], sel[:, :]))
        pe.wait(t_sel)
        t = expert_blocks(io["f0_w"], NB0, False, lambda n: selr[:, n:n + 1].broadcast_to([P, P]), P, E0,
                          GT, t_gt, t_yh, t_yl)
        OT = mem.take("OT", [P, KD, T], F32)
        t = back_to_tokens(t, 4, OT)
        phase_barrier()
        return t

    def ffn2(t_in):
        Y, t_y = begin_ffn(t_in)
        t_yh, t_yl = transpose_y(Y, t_y)
        t, lg = logits(io["f2_gate"], E2, t_yh, t_yl)
        pr, t = softmax_rows(lg, E2, t, E2 + 8 - TOP2)
        mask, t = choose(pr, t, E2, TOP2, "expert")
        w = mem.take("w", [P, NT, E2], F32)
        dve.wait(t)
        t = dve.do(lambda e: e.tensor_tensor(w[:, :, :], pr[:, :, 0:E2], mask[:, :, :], ALU.mult))
        GT, t_gt = gates_transposed(w, E2, 32, t)
        sel = mem.take("sel", [64, E2 * I2], F32)
        selr = mem.take("selr", [64, E2 * I2], F32R)
        t = dma.start(dsem("sel"), sel[:, :], io["sel2"])
        dve.wait(t)
        t_sel = dve.do(lambda e: e.tensor_copy(selr[:, :], sel[:, :]))
        pe.wait(t_sel)
        rows = 32 + E2
        t = expert_blocks(io["f2_w"], NB2, True, lambda n: selr[0:rows, n * P:(n + 1) * P], rows, NB2,
                          GT, t_gt, t_yh, t_yl)
        OT = mem.take("OT", [P, KD, T], F32)
        t = back_to_tokens(t, 6, OT)
        phase_barrier()
        return t

    def ffn3(t_in):
        Y, t_y = begin_ffn(t_in)
        rw = mem.take("rms_w", [P, D], F32)
        t_rw = dma.start(dsem("rms_w"), rw[:, :], io["f3_rms"].rearrange("(a n) -> a n", a=1).broadcast_to([P, D]))
        sq = mem.take("sq", [P, D], F32)
        ss = mem.take("ss", [P, NT], F32)
        act.wait(*t_y)
        for i in range(NT):
            t = act.do(lambda e, i=i: e.activation(sq[:, :], Y[:, i, :], ACT.Square, accum_out=ss[:, i:i + 1]))
            act.wait(t)
        rr = mem.take("rr", [P, NT], F32)
        dve.wait(t)
        t = dve.do(lambda e: e.tensor_scalar(rr[:, :], ss[:, :], 1.0 / D, 1e-6, ALU.mult, ALU.add))
        dve.wait(t)
        pool.wait(t)
        t = pool.do(lambda e: e.tensor_tensor(rr[:, :], rr[:, :], exponent[:, :], ALU.pow))
        dve.wait(t, t_rw)
        t_y = [dve.do(lambda e, i=i: e.scalar_tensor_tensor(
            Y[:, i, :], Y[:, i, :], rr[:, i:i + 1], rw[:, :], ALU.mult, ALU.mult)) for i in range(NT)]
        t_yh, t_yl = transpose_y(Y, t_y)
        t, lg = logits(io["f3_gate"], E3, t_yh, t_yl)
        pr, t = softmax_rows(lg, E3, t, E3 + 8 - TOP3)
        mask, t = choose(pr, t, E3, TOP3, "expert")
        w = mem.take("w", [P, NT, E3], F32)
        ws = mem.take("wsum", [P, NT], F32)
        dve.wait(t)
        t = dve.do(lambda e: e.tensor_tensor(w[:, :, :], pr[:, :, 0:E3], mask[:, :, :], ALU.mult))
        dve.wait(t)
        t = dve.do(lambda e: e.tensor_reduce(ws[:, :], w[:, :, :], AX.X, ALU.add))
        dve.wait(t)
        t = dve.do(lambda e: e.reciprocal(ws[:, :], ws[:, :]))
        dve.wait(t)
        t = dve.do(lambda e: e.tensor_tensor(w[:, :, :], w[:, :, :], ws[:, :].unsqueeze(2).broadcast_to([P, NT, E3]), ALU.mult))
        GT, t_gt = gates_transposed(w, E3, 32, t)
        sel = mem.take("sel", [64, E3], F32)
        selr = mem.take("selr", [64, E3], F32R)
        t = dma.start(dsem("sel"), sel[:, :], io["sel3"])
        dve.wait(t)
        t_sel = dve.do(lambda e: e.tensor_copy(selr[:, :], sel[:, :]))
        pe.wait(t_sel)
        rows = 32 + E3
        t = expert_blocks(io["f3_w"], NB3, True, lambda n: selr[0:rows, n:n + 1].broadcast_to([rows, P]), rows, E3,
                          GT, t_gt, t_yh, t_yl)
        OT = mem.take("OT", [P, KD, T], F32)
        t = back_to_tokens(t, 7, OT)
        phase_barrier()
        return t

    def ffn1(t_in):
        Y, t_y = begin_ffn(t_in)
        NW = [I1 * KD, I1 * KD, D * I1 // P]
        raws = [mem.take("wraw", [P, n], F32) for n in NW]
        qs = [mem.take("wq", [P, n], BF16) for n in NW]
        part = mem.take("wpart", [P, 3], F32)
        for k, name in enumerate(("f1_gate", "f1_up", "f1_down")):
            t = dma.start(dsem(f"w1_{k}"), raws[k][:, :], io[name])
            dve.wait(t)
            t = dve.do(lambda e, k=k: e.tensor_reduce(part[:, k:k + 1], raws[k][:, :], AX.X, ALU.add,
                                                      apply_absolute_value=True))
        lw = mem.take("ln_w", [P, I1], F32)
        t_lw = dma.start(dsem("ln_w"), lw[:, :], io["f1_ln"].rearrange("(a n) -> a n", a=1).broadcast_to([P, I1]))
        pe.wait(t, t_ones, bank_free[0])
        t = pe.do(mm(psum[:, 0, 0:3], ones[:, :], part[:, :], True, True))
        inv = mem.take("w_unit", [P, 3], F32)
        sw = mem.take("w_scale", [P, 3], F32)
        dve.wait(t)
        t = dve.do(lambda e: e.tensor_scalar(inv[:, :], psum[:, 0, 0:3], 1.0 / (I1 * D), 1e-5, ALU.mult, ALU.max))
        bank_free[0] = t
        dve.wait(t)
        t = dve.do(lambda e: e.reciprocal(sw[:, :], inv[:, :]))
        dve.wait(t)

        def quantise(raw, scale, low, high, last_out):
            t = dve.do(lambda e: e.tensor_scalar(raw, raw, scale, ROUND, ALU.mult, ALU.add))
            dve.wait(t)
            t = dve.do(lambda e: e.tensor_scalar(raw, raw, ROUND, high, ALU.subtract, ALU.min))
            dve.wait(t)
            return dve.do(lambda e: e.tensor_scalar(last_out, raw, low, None, ALU.max))

        for k in range(3):
            t_wq = quantise(raws[k][:, :], sw[:, k:k + 1], -1.0, 1.0, qs[k][:, :])
        am = mem.take("amax", [P, NT], F32)
        sx = mem.take("x_scale", [P, NT], F32)
        ux = mem.take("x_unit", [P, NT], F32)
        cg = mem.take("c_gate", [P, NT], F32)
        cu = mem.take("c_up", [P, NT], F32)
        t = dve.do(lambda e: e.tensor_reduce(am[:, :], Y[:, :, :], AX.X, ALU.max, apply_absolute_value=True))
        dve.wait(t)
        t = dve.do(lambda e: e.tensor_scalar(am[:, :], am[:, :], 1e-5, None, ALU.max))
        dve.wait(t)
        t = dve.do(lambda e: e.reciprocal(sx[:, :], am[:, :]))
        dve.wait(t)
        t = dve.do(lambda e: e.tensor_scalar(sx[:, :], sx[:, :], 127.0, None, ALU.mult))
        t = dve.do(lambda e: e.tensor_scalar(ux[:, :], am[:, :], 1.0 / 127.0, None, ALU.mult))
        dve.wait(t)
        dve.do(lambda e: e.tensor_scalar(cg[:, :], ux[:, :], inv[:, 0:1], None, ALU.mult))
        t_cu = dve.do(lambda e: e.tensor_scalar(cu[:, :], ux[:, :], inv[:, 1:2], None, ALU.mult))
        t_q = [quantise(Y[:, i, :], sx[:, i:i + 1], -128.0, 127.0, Y[:, i, :]) for i in range(NT)]
        XT = mem.take("xqT", [P, KD, T], BF16)
        pe.wait(*t_q)
        for kd in range(KD):
            for a, tiles in enumerate((range(0, 4), range(4, NT))):
                bank = 4 + kd * 2 + a
                pe.wait(bank_free[bank])
                for i in tiles:
                    t = pe.do(lambda e, i=i, a=a, bank=bank, kd=kd: e.transpose(
                        psum[:, bank, (i - 4 * a) * P:(i - 4 * a + 1) * P], Y[:, i, kd * P:(kd + 1) * P], ident[:, :]))
                n = len(tiles) * P
                act.wait(t)
                t_xt = act.do(lambda e, kd=kd, a=a, n=n, bank=bank: e.activation(
                    XT[:, kd, a * 512:a * 512 + n], psum[:, bank, 0:n], ACT.Copy))
                bank_free[bank] = t_xt
        Wg = qs[0][:, :].rearrange("p (k n) -> p k n", k=KD)
        Wu = qs[1][:, :].rearrange("p (k n) -> p k n", k=KD)
        Wd = qs[2][:, :].rearrange("p (k n) -> p k n", k=I1 // P)
        Hb = mem.take("h", [P, NT, I1], F32)
        SG = [mem.take("sg", [P, I1], F32) for _ in range(2)]
        ss = mem.take("ss", [P, NT], F32)
        sg_free = [None] * 2
        pe.wait(t_xt, t_wq)
        t_sq = None
        for i in range(NT):
            b0 = 4 * (i % 2)
            for which, W in ((0, Wg), (1, Wu)):
                for n in range(2):
                    bank = b0 + 2 * which + n
                    pe.wait(bank_free[bank])
                    t = product(psum[:, bank, :], [(XT[:, kd, i * P:(i + 1) * P], W[:, kd, n * 512:(n + 1) * 512])
                                                   for kd in range(KD)])
                if which == 0:
                    t_gm = t
            sg = SG[i % 2]
            act.wait(t_gm, t_cu, sg_free[i % 2])
            t_s = act.do(lambda e, i=i, b0=b0, sg=sg: e.activation(
                sg[:, :].rearrange("p (a n) -> p a n", a=2), psum[:, b0:b0 + 2, :], ACT.Silu, scale=cg[:, i:i + 1]))
            bank_free[b0] = bank_free[b0 + 1] = t_s
            dve.wait(t_s, t)
            t_h = dve.do(lambda e, i=i, b0=b0, sg=sg: e.scalar_tensor_tensor(
                Hb[:, i, :].rearrange("p (a n) -> p a n", a=2), psum[:, b0 + 2:b0 + 4, :], cu[:, i:i + 1],
                sg[:, :].rearrange("p (a n) -> p a n", a=2), ALU.mult, ALU.mult))
            bank_free[b0 + 2] = bank_free[b0 + 3] = t_h
            act.wait(t_h)
            t_sq = act.do(lambda e, i=i, sg=sg: e.activation(sg[:, :], Hb[:, i, :], ACT.Square, accum_out=ss[:, i:i + 1]))
            sg_free[i % 2] = t_sq
            act.wait(t_sq)
        rr = mem.take("rr", [P, NT], F32)
        dve.wait(t_sq)
        t = dve.do(lambda e: e.tensor_scalar(rr[:, :], ss[:, :], 1.0 / I1, 1e-6, ALU.mult, ALU.add))
        dve.wait(t)
        pool.wait(t)
        t = pool.do(lambda e: e.tensor_tensor(rr[:, :], rr[:, :], exponent[:, :], ALU.pow))
        dve.wait(t, t_lw)
        for i in range(NT):
            t = dve.do(lambda e, i=i: e.scalar_tensor_tensor(
                Hb[:, i, :], Hb[:, i, :], rr[:, i:i + 1], lw[:, :], ALU.mult, ALU.mult))
        dve.wait(t)
        hm = mem.take("hmax", [P, NT], F32)
        sh = mem.take("h_scale", [P, NT], F32)
        cd = mem.take("c_down", [P, NT], F32)
        t = dve.do(lambda e: e.tensor_reduce(hm[:, :], Hb[:, :, :], AX.X, ALU.max, apply_absolute_value=True))
        dve.wait(t)
        t = dve.do(lambda e: e.tensor_scalar(hm[:, :], hm[:, :], 1e-5, None, ALU.max))
        dve.wait(t)
        t = dve.do(lambda e: e.reciprocal(sh[:, :], hm[:, :]))
        dve.wait(t)
        t = dve.do(lambda e: e.tensor_scalar(sh[:, :], sh[:, :], 127.0, None, ALU.mult))
        t2 = dve.do(lambda e: e.tensor_scalar(cd[:, :], hm[:, :], 1.0 / 127.0, inv[:, 2:3], ALU.mult, ALU.mult))
        dve.wait(t, t2, t_tanh)
        t_cd = dve.do(lambda e: e.tensor_scalar(cd[:, :], cd[:, :], tanh_g[:, 5:6], None, ALU.mult))
        HT_ = mem.take("hqT", [P, I1 // P, T], BF16)
        ring = 0
        for i in range(NT):
            t = quantise(Hb[:, i, :], sh[:, i:i + 1], -128.0, 127.0, Hb[:, i, :])
            for a in range(2):
                bank = ring % 4
                ring += 1
                pe.wait(t, bank_free[bank])
                for k in range(4):
                    t_p = pe.do(lambda e, i=i, a=a, k=k, bank=bank: e.transpose(
                        psum[:, bank, k * P:(k + 1) * P], Hb[:, i, (4 * a + k) * P:(4 * a + k + 1) * P], ident[:, :]))
                act.wait(t_p)
                t_ht = act.do(lambda e, i=i, a=a, bank=bank: e.activation(
                    HT_[:, 4 * a:4 * a + 4, i * P:(i + 1) * P],
                    psum[:, bank, :].rearrange("p (k n) -> p k n", k=4), ACT.Copy))
                bank_free[bank] = t_ht
            bank = 4 + i % 4
            pe.wait(t_ht, bank_free[bank])
            t = product(psum[:, bank, 0:D], [(HT_[:, k, i * P:(i + 1) * P], Wd[:, k, :]) for k in range(I1 // P)])
            dve.wait(t, t_cd)
            t_x = dve.do(lambda e, i=i, bank=bank: e.scalar_tensor_tensor(
                X[:, i, :], psum[:, bank, 0:D], cd[:, i:i + 1], X[:, i, :], ALU.mult, ALU.add))
            bank_free[bank] = t_x
        phase_barrier()
        return t_x

    prepare_context()
    phase_barrier()
    t_now = t_x
    ffns = [ffn0, ffn1, ffn2, ffn3]
    for n in range(4):
        if steps > 2 * n:
            t_now = attention(n, t_now)
        if steps > 2 * n + 1:
            t_now = ffns[n](t_now)
    sp.wait(t_now)
    t_out = dma.start(dsem("out"), out.rearrange("b s d -> (b s) d").rearrange("(i p) d -> p i d", p=P), X[:, :, :])
    sp.wait(t_out)

    with nc.Block() as block:
        for name, stream in (("sync", sp), ("tensor", pe), ("scalar", act), ("vector", dve), ("gpsimd", pool)):
            block.__class__
            {"sync": block.sync, "tensor": block.tensor, "scalar": block.scalar, "vector": block.vector,
             "gpsimd": block.gpsimd}[name](stream.emit)


def layouts(i):
    c = np.ascontiguousarray
    a = {"x": c(i["x"]), "ctx": c(i["ctx_512"]), "g_xattn": c(i["g_xattn"]), "g_ffn": c(i["g_ffn"])}
    heads = lambda w, k, n: c(w.reshape(H, k, n).transpose(1, 0, 2))
    kv = i["L0_xattn_Wkv_expand"]
    a["a0_Wq"] = heads(i["L0_xattn_Wq"], 16, D)
    a["a0_Wk"] = heads(kv[:D], 16, DC)
    a["a0_Wv"] = heads(kv[D:], 16, DC)
    a["a0_WoT"] = heads(c(i["L0_xattn_Wout"].T), 16, D)
    for n in (1, 2, 3):
        w = lambda s: i[f"L{n}_xattn_{s}"]
        a[f"a{n}_Wq"] = heads(w("Wq"), K1, D)
        a[f"a{n}_WoT"] = heads(c(w("Wo").T), K1, D)
        a[f"a{n}_Wv"] = c(w("w_kc_kv").transpose(1, 0, 2))
        a[f"a{n}_WqrT"] = c(w("W_qr").transpose(2, 0, 1))
        a[f"a{n}_WkrT"] = c(w("W_kr").transpose(2, 0, 1))
        if n == 2:
            a["a2_Wc"] = c(w("w_kc_q").transpose(1, 0, 2))
        else:
            a[f"a{n}_WcT"] = c(w("w_kc_q").transpose(0, 2, 1).reshape(H, 2, DQH, K1).transpose(2, 0, 1, 3))

    def chunks(w):
        n = w.shape[0] // P
        return w.reshape(n, P, KD, P).transpose(0, 3, 2, 1).reshape(n, P, KD * P)

    up = np.concatenate([chunks(i["L0_ffn_w1"].reshape(-1, D)), chunks(i["L0_ffn_shared_up_w"])])
    dn = np.concatenate([i["L0_ffn_w2"].transpose(0, 2, 1).reshape(-1, D), i["L0_ffn_shared_down_w"].T]).reshape(-1, P, D)
    a["f0_w"] = c(np.concatenate([up, dn], -1))
    flat = lambda w: w.reshape(-1, D)
    dn = flat(i["L2_ffn_w_down"].transpose(0, 2, 1)).reshape(-1, P, D)
    a["f2_w"] = c(np.concatenate([chunks(flat(i["L2_ffn_w_gate"])), chunks(flat(i["L2_ffn_w_up"])), dn], -1))
    hid = lambda e, s: np.concatenate([flat(i["L3_ffn_" + e].transpose(0, 2, 1)), i["L3_ffn_" + s].T])
    dn = np.concatenate([flat(i["L3_ffn_w_down"]), i["L3_ffn_sw_down"]]).reshape(-1, P, D)
    a["f3_w"] = c(np.concatenate([chunks(hid("w_gate", "sw_gate")), chunks(hid("w_up", "sw_up")), dn], -1))
    rows = lambda w: c(w.reshape(-1, P, w.shape[-1]).transpose(1, 0, 2))
    a["f0_gate"] = rows(i["L0_ffn_gate_w"].T)
    a["f2_gate"] = rows(i["L2_ffn_gate_w"].T)
    a["f3_gate"] = rows(i["L3_ffn_router_w"])
    a["f0_bias"] = c(i["L0_ffn_e_bias"])
    a["f3_rms"] = c(i["L3_ffn_rms_weight"])
    a["f1_ln"] = c(i["L1_ffn_ln_weight"])
    for k in ("gate", "up", "down"):
        w = rows(i[f"L1_ffn_w_{k}"].T)
        a[f"f1_{k}"] = c(w.reshape(P, -1))
    a.update(constants())
    a["blockdiag"] = a["blockdiag"].reshape(64, T)
    return a


def program(nc, arrays, steps=8):
    io = {k: nc.dram_tensor("in_" + k, v.shape, F32, kind="ExternalInput").ap() for k, v in arrays.items()}
    out = nc.dram_tensor("out", (B, S, D), F32, kind="ExternalOutput").ap()
    build(nc, io, out, steps)


def kernel(**inputs):
    import concourse.bacc as bacc
    from concourse.bass_utils import run_bass_kernel_spmd

    arrays = layouts({k: np.asarray(v) for k, v in inputs.items()})
    nc = bacc.Bacc("TRN2", target_bir_lowering=False, num_devices=1)
    program(nc, arrays)
    r = run_bass_kernel_spmd(nc, [{"in_" + k: v for k, v in arrays.items()}], core_ids=[0])
    return r.results[0]["out"]
```

```python
from collections import namedtuple

import numpy as np

import concourse.bass as bass
from concourse import mybir

F32, F32R, BF16 = mybir.dt.float32, mybir.dt.float32r, mybir.dt.bfloat16
ALU = mybir.AluOpType
ACT = mybir.ActivationFunctionType
AX = mybir.AxisListType

P = 128
B, S, D = 16, 56, 256
T = B * S
NT = T // P
KD = D // P
HT = T // 2
L, DC = 1500, 64
NL, LP = 12, 125
H = 16
K1 = 128
DQ, DQH = 192, 96
E0, TOP0, NG0, TOPG0, CAP0 = 64, 6, 8, 4, 64
I1 = 1024
E2, I2, TOP2 = 16, 176, 6
E3, TOP3 = 8, 2
NB0, NB2, NB3 = E0 + 4, E2 * I2 // P, E3 + 1
BIG = 3.0e38
ROUND = 1.5 * 2.0 ** 23

Tick = namedtuple("Tick", "sem value")


class Stream:

    def __init__(self, sem):
        self.sem, self.count, self.items, self.seen = sem, 0, [], {}

    def wait(self, *ticks):
        for t in ticks:
            if t is not None and self.seen.get(t.sem, 0) < t.value:
                self.seen[t.sem] = t.value
                self.items.append(lambda e, t=t: e.wait_ge(t.sem, t.value))

    def run(self, fn):
        self.items.append(fn)

    def do(self, fn):
        self.count += 1
        self.items.append(lambda e: fn(e).then_inc(self.sem, 1))
        return Tick(self.sem, self.count)

    def tick(self):
        return Tick(self.sem, self.count)

    def emit(self, engine):
        for item in self.items:
            item(engine)


class Loads:

    def __init__(self, stream):
        self.stream, self.counts = stream, {}

    def start(self, sem, out, src):
        self.counts[sem] = self.counts.get(sem, 0) + 16
        self.stream.items.append(lambda e: e.dma_start(out, src).then_inc(sem, 16))
        return Tick(sem, self.counts[sem])


class Memory:

    def __init__(self, nc):
        self.nc, self.at, self.end, self.n = nc, (nc.sbuf_base + 31) // 32 * 32, nc.sbuf_usable_end, 0

    def take(self, name, shape, dt):
        size = int(np.prod(shape[1:])) * (2 if dt == BF16 else 4)
        self.n += 1
        t = self.nc.alloc_sbuf_tensor_at(f"{name}_{self.n}", list(shape), dt, offset=self.at)
        self.at += (size + 31) // 32 * 32
        assert self.at <= self.end, (name, self.at, self.end)
        return t


def rope_tables(length, dim):
    f = np.float32
    inv = (f(1.0) / np.power(f(10000.0), np.arange(0, dim, 2, dtype=f) / f(dim))).astype(f)
    angle = np.arange(length, dtype=f)[:, None] * inv[None, :]
    return np.repeat(np.sin(angle), 2, axis=-1).astype(f), np.repeat(np.cos(angle), 2, axis=-1).astype(f)


def constants():
    f = np.float32
    c = {}
    c["ident"] = np.eye(P, dtype=f)
    c["before"] = np.triu(np.ones((P, P), f), 1)
    sin, cos = rope_tables(L, DC)
    signed = sin.copy()
    signed[:, :DC // 2] *= -1
    c["cos_k"] = cos.reshape(LP, NL * DC)
    c["sin_k"] = signed.reshape(LP, NL * DC)
    sin, cos = rope_tables(S, DQ)
    halves = [cos[:, :DQH], sin[:, :DQH], cos[:, DQH:], sin[:, DQH:]]
    c["rope_q"] = np.stack([x.T for x in halves], 1).astype(f)
    late = np.where(np.arange(S)[None, :] > np.arange(S)[:, None], f(-1e30), f(0))
    s_of_q = (np.arange(NT * P) % S).reshape(NT, P).T
    c["mask_q"] = late[s_of_q].reshape(P, NT * S).astype(f)
    c["mask_k"] = np.tile(late.T, (1, H // 2)).astype(f)
    bd = np.zeros((64, NT, P), f)
    bd[np.arange(NT), np.arange(NT)] = bd[32 + np.arange(NT), np.arange(NT)] = 1
    c["blockdiag"] = bd
    bd = np.zeros((64, NT, P), f)
    pick = np.zeros((64, P), f)
    for n in range(2 * NT):
        bd[[n, 32 + n], n // 2] = 1
        pick[[n, 32 + n], n % 2 * DC:(n % 2 + 1) * DC] = 1
    c["blockdiag2"], c["pick2"] = bd, pick
    ones = np.zeros((P, P), f)
    ones[0:S, 0] = ones[DC:DC + S, 1] = 1
    c["ones2"] = ones
    c["sel0"] = (np.arange(P)[:, None] % E0 == np.arange(E0)[None, :]).astype(f)
    rows = np.arange(64)[:, None] % 32
    c["sel2"] = (rows == np.arange(E2 * I2)[None, :] // I2).astype(f)
    c["sel3"] = (rows == np.arange(E3)[None, :]).astype(f)
    return c


def build(nc, io, out, steps=8):
    mem = Memory(nc)
    sems = {n: nc.alloc_semaphore(n) for n in ("pe_done", "act_done", "dve_done", "pool_done")}
    pe, act, dve, pool = (Stream(sems[n]) for n in ("pe_done", "act_done", "dve_done", "pool_done"))
    sp = Stream(None)
    dma = Loads(sp)
    load_sems = {}

    def dsem(name):
        if name not in load_sems:
            load_sems[name] = nc.alloc_semaphore("dma_" + name)
        return load_sems[name]

    psum = nc.alloc_psum_tensor("psum", [P, 8, 512], F32)
    bank_free = [None] * 8

    def phase_barrier():
        ticks = [s.tick() for s in (pe, act, dve, pool)]
        loads = [Tick(s, n) for s, n in dma.counts.items()]
        for s in (pe, act, dve, pool, sp):
            s.wait(*ticks, *loads)

    upper = [0]

    def upper_bank():
        bank = 4 + upper[0] % 4
        upper[0] += 1
        pe.wait(bank_free[bank])
        return bank

    def mm(o, lhsT, rhs, start, stop, **kw):
        return lambda e: e.matmul(o, lhsT, rhs, start=start, stop=stop, **kw)

    def product(o, pairs):
        for n, (a, b) in enumerate(pairs):
            last = n == len(pairs) - 1
            f = mm(o, a, b, n == 0, last)
            if last:
                return pe.do(f)
            pe.run(f)

    def split_pairs(ah, al, bh, bl):
        return [(ah, bh), (ah, bl), (al, bh)]

    X = mem.take("X", [P, NT, D], F32)
    YH = mem.take("YH", [P, KD, T], F32R)
    YL = mem.take("YL", [P, KD, T], F32R)
    ident = mem.take("ident", [P, P], F32)
    ones = mem.take("ones", [P, P], F32)
    exponent = mem.take("exponent", [P, NT], F32)
    gates = mem.take("gates", [P, 8], F32)
    tanh_g = mem.take("tanh_g", [P, 8], F32)
    V = mem.take("V", [P, B, NL * DC], F32)
    MH = mem.take("MH", [P, H // 2, D], F32R)
    ML = mem.take("ML", [P, H // 2, D], F32R)
    norm_at = mem.at
    Y = mem.take("Y", [P, NT, D], F32)
    norm_end = mem.at
    stats = mem.take("stats", [P, NT, 6], F32)
    mv = mem.take("mv", [P, NT, 2], F32)
    rstd = mem.take("rstd", [P, NT], F32)
    folded_at = mem.at
    AH = mem.take("AH", [P, KD, H * DC], F32R)
    AL = mem.take("AL", [P, KD, H * DC], F32R)
    base = mem.at
    mem.at = folded_at
    U2 = mem.take("U2", [DQH, H, 2, DC], F32)
    mem.at = base

    KT = nc.dram_tensor("kt_scratch", (B, P, L), F32, kind="Internal").ap()

    t_ident = dma.start(dsem("ident"), ident[:, :], io["ident"])
    t_x = dma.start(dsem("x"), X[:, :, :], io["x"].rearrange("b s d -> (b s) d").rearrange("(i p) d -> p i d", p=P))
    dma.start(dsem("g"), gates[:, 0:4], io["g_xattn"].rearrange("(a n) -> a n", a=1).broadcast_to([P, 4]))
    t_g = dma.start(dsem("g"), gates[:, 4:8], io["g_ffn"].rearrange("(a n) -> a n", a=1).broadcast_to([P, 4]))
    t_ones = dve.do(lambda e: e.memset(ones[:, :], 1.0))
    t_exponent = dve.do(lambda e: e.memset(exponent[:, :], -0.5))
    act.wait(t_g)
    t_tanh = act.do(lambda e: e.activation(tanh_g[:, :], gates[:, :], ACT.Tanh))

    norm = {}

    def norm_stats(i, t_in):
        dve.wait(t_in)
        t = dve.do(lambda e: e.bn_stats(stats[:, i, :], X[:, i, :]))
        dve.wait(t)
        t = dve.do(lambda e: e.bn_aggr(mv[:, i, :], stats[:, i, :]))
        dve.wait(t)
        t = dve.do(lambda e: e.tensor_scalar(rstd[:, i:i + 1], mv[:, i, 1:2], 1e-5, None, ALU.add))
        pool.wait(t, t_exponent)
        norm["rstd", i] = pool.do(lambda e: e.tensor_tensor(rstd[:, i:i + 1], rstd[:, i:i + 1], exponent[:, 0:1], ALU.pow))

    def norm_apply(i):
        dve.wait(norm["rstd", i])
        norm["y", i] = dve.do(lambda e: e.tensor_scalar(Y[:, i, :], X[:, i, :], mv[:, i, 0:1], rstd[:, i:i + 1],
                                                        ALU.subtract, ALU.mult))

    def norm_transpose(i):
        bank = upper_bank()
        pe.wait(t_ident, norm["y", i])
        for kd in range(KD):
            t = pe.do(lambda e, kd=kd: e.transpose(psum[:, bank, kd * P:(kd + 1) * P],
                                                   Y[:, i, kd * P:(kd + 1) * P], ident[:, :]))
        src = psum[:, bank, 0:KD * P].rearrange("p (k n) -> p k n", k=KD)
        cols = slice(i * P, (i + 1) * P)
        act.wait(t)
        norm["yh"] = t = act.do(lambda e: e.activation(YH[:, :, cols], src, ACT.Copy))
        dve.wait(t)
        norm["yl"] = bank_free[bank] = dve.do(lambda e: e.tensor_tensor(
            YL[:, :, cols], src, YH[:, :, cols].bitcast(F32), ALU.subtract))

    def back_to_tokens(c, t_acc, gate_col, OT, last=False):
        for m in range(KD):
            act.wait(t_acc)
            t = act.do(lambda e, m=m: e.activation(OT[:, m, c * HT:(c + 1) * HT], psum[:, m * 2 + c, 0:HT], ACT.Copy))
            bank_free[m * 2 + c] = t
        t_copied = t
        before = (0, 1, 2) if c == 1 else ()
        for tiles in (((0, 1), (2,)) if c == 0 else ((3, 4), (5, 6))):
            bank = upper_bank()
            pe.wait(t_copied)
            for k, i in enumerate(tiles):
                for m in range(KD):
                    t = pe.do(lambda e, i=i, k=k, m=m, bank=bank: e.transpose(
                        psum[:, bank, k * D + m * P:k * D + (m + 1) * P], OT[:, m, i * P:(i + 1) * P], ident[:, :]))
            n = len(tiles)
            rows = X[:, tiles[0]:tiles[0] + n, :].rearrange("p a d -> p (a d)")
            dve.wait(t, t_tanh)
            t_x = dve.do(lambda e, rows=rows, bank=bank, n=n: e.scalar_tensor_tensor(
                rows, psum[:, bank, 0:n * D], tanh_g[:, gate_col:gate_col + 1], rows, ALU.mult, ALU.add))
            bank_free[bank] = t_x
            if not last:
                for i in tiles:
                    norm_stats(i, t_x)
                for i in tiles:
                    norm_apply(i)
                if c == 1:
                    for i in before:
                        norm_transpose(i)
                    before = tiles
        if not last and c == 1:
            for i in before:
                norm_transpose(i)
        return t_x

    def prepare_context():
        cos = mem.take("cos_k", [P, NL * DC], F32)
        sin = mem.take("sin_k", [P, NL * DC], F32)
        raw = [mem.take("ctx_raw", [P, NL, DC], F32) for _ in range(2)]
        rot = mem.take("ctx_rot", [P, NL, DC], F32)
        kt = [mem.take("kt", [P, L], F32R) for _ in range(2)]
        half = DC // 2
        cos3 = cos[0:LP, :].rearrange("p (j d) -> p j d", d=DC)
        sin3 = sin[0:LP, :].rearrange("p (j d) -> p j d", d=DC)
        t_load, t_terms, t_v, t_stored = {}, {}, {}, {}

        def load(b):
            sp.wait(t_v.get(b - 2))
            t_load[b] = dma.start(dsem(f"raw{b % 2}"), raw[b % 2][0:LP, :, :].rearrange("p j d -> p (j d)"),
                                  io["ctx"][b].rearrange("(p j) d -> p (j d)", j=NL))

        def rotate(b):
            r = raw[b % 2]
            Vb = V[0:LP, b, :].rearrange("p (j d) -> p j d", d=DC)
            pool.wait(t_load[b], t_tab, t_v.get(b - 1))
            pool.do(lambda e: e.tensor_tensor(rot[0:LP, :, 0:half], r[0:LP, :, half:DC], sin3[:, :, 0:half], ALU.mult))
            t_q = pool.do(lambda e: e.tensor_tensor(rot[0:LP, :, half:DC], r[0:LP, :, 0:half], sin3[:, :, half:DC], ALU.mult))
            dve.wait(t_load[b], t_tab)
            t_c = dve.do(lambda e: e.tensor_tensor(Vb, r[0:LP, :, :], cos3, ALU.mult))
            t_terms[b] = (t_c, t_q)

        def add_terms(b):
            Vb = V[0:LP, b, :].rearrange("p (j d) -> p j d", d=DC)
            dve.wait(*t_terms[b])
            t_v[b] = dve.do(lambda e: e.tensor_tensor(Vb, Vb, rot[0:LP, :, :], ALU.add))

        def transpose(b, g):
            k = kt[b % 2]
            bank = upper_bank()
            pe.wait(t_v[b], t_ident)
            for j in range(4):
                t = pe.do(lambda e, j=j: e.transpose(
                    psum[0:DC, bank, j * LP:(j + 1) * LP], V[0:LP, b, (4 * g + j) * DC:(4 * g + j + 1) * DC],
                    ident[0:LP, 0:LP]))
            cols = slice(g * 4 * LP, (g + 1) * 4 * LP)
            act.wait(t, t_stored.get(b - 2))
            t = act.do(lambda e: e.activation(k[0:DC, cols], psum[0:DC, bank, 0:4 * LP], ACT.Copy))
            dve.wait(t)
            bank_free[bank] = dve.do(lambda e: e.tensor_tensor(
                k[DC:P, cols], psum[0:DC, bank, 0:4 * LP], k[0:DC, cols].bitcast(F32), ALU.subtract))
            return bank_free[bank]

        def store(b, t):
            sp.wait(t)
            t_stored[b] = dma.start(dsem(f"kt_st{b % 2}"), KT[b], kt[b % 2][:, :].bitcast(F32))

        dma.start(dsem("rope"), cos[0:LP, :], io["cos_k"])
        t_tab = dma.start(dsem("rope"), sin[0:LP, :], io["sin_k"])
        load(0)
        load(1)
        yield
        rotate(0)
        yield
        add_terms(0)
        yield
        t_kt = None
        for b in range(B):
            for g in range(3):
                if g == 0 and b > 0:
                    store(b - 1, t_kt)
                if g == 0 and b + 2 < B:
                    load(b + 2)
                if g == 0 and b + 1 < B:
                    rotate(b + 1)
                if g == 2 and b + 1 < B:
                    add_terms(b + 1)
                t_kt = transpose(b, g)
                yield
                if g < 2:
                    yield
        store(B - 1, t_kt)
        after_context.extend([t_stored[B - 2], t_stored[B - 1], t_v[B - 1], t_kt])

    after_context = []

    def fold_weights(layer, nbuf, after=()):
        first = layer == 0
        KH = 16 if first else K1
        w = lambda n: io[f"a{layer}_{n}"]
        bufs = []
        for _ in range(nbuf):
            wo = mem.take("WoT", [P, 2, D], F32)
            wv = mem.take("Wv", [P, 2, DC], F32)
            wq = mem.take("Wq", [P, 2, D], F32) if layer != 2 else None
            G = mem.take("G", [P, 2, DC], F32) if layer != 2 else None
            wc = mem.take("WcT", [DQH, 2, 2, K1], F32) if layer in (1, 3) else None
            wr = mem.take("WqrT", [64, 2, DQ + DC], F32) if not first else None
            U = mem.take("U", [DQH, 2, 2, DC], F32) if layer in (1, 3) else None
            bufs.append((wo, wv, wq, G, wc, wr, U))
        t_m, t_a, t_r = {}, {}, {}
        used_m, used_a, used_r, t_G, t_U = {}, {}, {}, {}, {}

        def load(p):
            wo, wv, wq, G, wc, wr, U = bufs[p % nbuf]
            heads, k = slice(2 * p, 2 * p + 2), p % nbuf
            sp.wait(*after, used_r.get(p - nbuf))
            if not first:
                t_r[p] = dma.start(dsem(f"fold_r{k}"), wr[:, :, :], w("WrT")[:, heads, :])
            sp.wait(used_m.get(p - nbuf))
            dma.start(dsem(f"fold_m{k}"), wo[0:KH, :, :], w("WoT")[:, heads, :])
            t_m[p] = dma.start(dsem(f"fold_m{k}"), wv[0:KH, :, :], w("Wv")[:, heads, :])
            if layer == 2:
                return
            sp.wait(used_a.get(p - nbuf))
            dma.start(dsem(f"fold_a{k}"), wq[0:KH, :, :], w("Wq")[:, heads, :])
            t_a[p] = (dma.start(dsem(f"fold_a{k}"), G[0:KH, :, :], w("Wk")[:, heads, :]) if first else
                      dma.start(dsem(f"fold_a{k}"), wc[:, :, :, :], w("WcT")[:, heads, :, :]))

        def fold_u(p):
            wr, U = bufs[p % nbuf][5:7]
            bank = upper_bank()
            pe.wait(t_r[p])
            for odd in range(2):
                for c in range(2):
                    n = (odd * 2 + c) * DC
                    t = pe.do(mm(psum[0:DQH, bank, n:n + DC], wr[:, odd, c * DQH:(c + 1) * DQH],
                                 wr[:, odd, DQ:DQ + DC], True, True))
            used_r[p] = t
            act.wait(t, used_a.get(p - nbuf))
            o = U2[:, 2 * p:2 * p + 2, :, :] if layer == 2 else U[:, :, :, :]
            bank_free[bank] = t_U[p] = act.do(lambda e: e.activation(
                o.rearrange("p h c d -> p (h c d)"), psum[0:DQH, bank, 0:4 * DC], ACT.Copy))

        def fold_m(p):
            wo, wv = bufs[p % nbuf][0:2]
            bank = upper_bank()
            pe.wait(t_m[p])
            for odd in range(2):
                t = pe.do(mm(psum[odd * DC:(odd + 1) * DC, bank, 0:D], wv[0:KH, odd, :], wo[0:KH, odd, :], True, True))
            used_m[p] = t
            act.wait(t)
            t = act.do(lambda e: e.activation(MH[:, p, :], psum[:, bank, 0:D], ACT.Copy))
            dve.wait(t)
            bank_free[bank] = dve.do(lambda e: e.tensor_tensor(
                ML[:, p, :], psum[:, bank, 0:D], MH[:, p, :].bitcast(F32), ALU.subtract))

        def fold_g(p):
            wo, wv, wq, G, wc, wr, U = bufs[p % nbuf]
            bank = upper_bank()
            pe.wait(t_U[p], t_a[p])
            for odd in range(2):
                t = product(psum[:, bank, odd * DC:(odd + 1) * DC],
                            [(wc[:, odd, c, :], U[:, odd, c, :]) for c in range(2)])
            act.wait(t, used_a.get(p - nbuf))
            bank_free[bank] = t_G[p] = act.do(lambda e: e.activation(
                G[:, :, :].rearrange("p h d -> p (h d)"), psum[:, bank, 0:2 * DC], ACT.Copy))

        def fold_a(p):
            wq, G = bufs[p % nbuf][2:4]
            bank = upper_bank()
            pe.wait(t_a[p], t_G.get(p))
            for kd in range(KD):
                for odd in range(2):
                    n = kd * P + odd * DC
                    t = pe.do(mm(psum[:, bank, n:n + DC], wq[0:KH, odd, kd * P:(kd + 1) * P], G[0:KH, odd, :], True, True))
            used_a[p] = t
            scale = 1.0 / np.sqrt(16.0) if first else 1.0
            src = psum[:, bank, 0:KD * P].rearrange("p (k n) -> p k n", k=KD)
            cols = slice(p * P, (p + 1) * P)
            act.wait(t)
            t = act.do(lambda e: e.activation(AH[:, :, cols], src, ACT.Copy, scale=float(scale)))
            dve.wait(t)
            bank_free[bank] = dve.do(lambda e: e.scalar_tensor_tensor(
                AL[:, :, cols], src, float(scale), AH[:, :, cols].bitcast(F32), ALU.mult, ALU.subtract))

        for p in range(max(nbuf - 1, 1)):
            load(p)
        yield
        for p in range(H // 2):
            if nbuf > 1 and p + nbuf - 1 < H // 2:
                load(p + nbuf - 1)
            if not first:
                fold_u(p)
                yield
            fold_m(p)
            yield
            if layer in (1, 3):
                fold_g(p)
                yield
            if layer != 2:
                fold_a(p)
            if nbuf == 1 and p + 1 < H // 2:
                load(p + 1)
            yield

    w1_at = base + 55 * 1024
    heads_at = w1_at - H // 2 * D * 4 - H * DQ * 4

    def attention(layer):
        mem.at = base
        first = layer == 0
        to_transpose = layer in (0, 2)
        mem.at = base
        QR = mem.take("QR", [P, H // 2, T], F32)
        top = mem.at
        tk = {}
        if not first:
            K1t = [mem.take("K1", [P, L], F32R) for _ in range(3)]

            def load_keys(b):
                sp.wait(tk.get(("scored", b - 3)))
                tk["k1", b] = dma.start(dsem(f"k1{b % 3}"), K1t[b % 3][:, :].bitcast(F32), KT[b])

            load_keys(0)
            if layer != 2:
                load_keys(1)
            after_k1 = mem.at
            mem.at = top
        w = lambda n: io[f"a{layer}_{n}"]
        t_AH, t_AL = act.tick(), dve.tick()
        if layer == 2:
            Wq, Wc, t_heads = heads2["Wq"], heads2["Wc"], heads2["ticks"]
            assert mem.at + L * 4 <= heads_at
            mem.at = w1_at
            rope = mem.take("rope_q", [DQH, 4, S], F32)
            t_rope = dma.start(dsem("rope_q"), rope[:, :, :], io["rope_q"])
        t_yh, t_yl = norm["yh"], norm["yl"]

        if layer != 2:
            pe.wait(t_yh, t_yl, t_AH, t_AL)
            for mt in range(H // 2):
                for c in range(2):
                    bank = (mt * 2 + c) % 8
                    pe.wait(bank_free[bank])
                    pairs = []
                    for kd in range(KD):
                        m, n = slice(mt * P, (mt + 1) * P), slice(c * HT, (c + 1) * HT)
                        pairs += split_pairs(AH[:, kd, m], AL[:, kd, m], YH[:, kd, n], YL[:, kd, n])
                    t = product(psum[:, bank, 0:HT], pairs)
                    act.wait(t)
                    bank_free[bank] = act.do(lambda e, mt=mt, c=c, bank=bank: e.activation(
                        QR[:, mt, c * HT:(c + 1) * HT], psum[:, bank, 0:HT], ACT.Copy))
        else:
            NB, NR = 4, 4
            BH = [mem.take("BH", [P, KD, DQ], F32R) for _ in range(NB)]
            BL = [mem.take("BL", [P, KD, DQ], F32R) for _ in range(NB)]
            terms = [mem.take("rope_term", [DQH, 4, HT], F32) for _ in range(2)]
            turned = [mem.take("turned", [DQH, 2, HT], F32) for _ in range(NR)]
            t_turn_free, t_term_free, t_B, t_B_free = [None] * NR, [None] * 2, {}, [None] * NB
            t_turned = {}

            def head_weights(h):
                pe.wait(t_heads[h // 4], bank_free[0])
                for kd in range(KD):
                    t = pe.do(mm(psum[:, 0, kd * DQ:(kd + 1) * DQ], Wq[h // 8][:, h % 8, kd * P:(kd + 1) * P],
                                 Wc[:, h, :], True, True))
                bh, bl = BH[h % NB], BL[h % NB]
                act.wait(t, t_B_free[h % NB])
                t_bh = act.do(lambda e: e.activation(
                    bh[:, :, :].rearrange("p k q -> p (k q)"), psum[:, 0, 0:KD * DQ], ACT.Copy))
                dve.wait(t_bh)
                t_bl = dve.do(lambda e: e.tensor_tensor(
                    bl[:, :, :].rearrange("p k q -> p (k q)"), psum[:, 0, 0:KD * DQ],
                    bh[:, :, :].rearrange("p k q -> p (k q)").bitcast(F32), ALU.subtract))
                bank_free[0] = t_bl
                t_B[h] = (t_bh, t_bl)

            def turn(unit):
                h, c = unit // 4 * 2 + unit % 2, unit % 4 // 2
                bh, bl = BH[h % NB], BL[h % NB]
                n = slice(c * HT, (c + 1) * HT)
                banks = (1 + 2 * (unit % 2), 2 + 2 * (unit % 2))
                pe.wait(*t_B[h], t_yh, t_yl)
                for half, bank in enumerate(banks):
                    pe.wait(bank_free[bank])
                    m = slice(half * DQH, (half + 1) * DQH)
                    pairs = []
                    for kd in range(KD):
                        pairs += split_pairs(bh[:, kd, m], bl[:, kd, m], YH[:, kd, n], YL[:, kd, n])
                    t = product(psum[0:DQH, bank, 0:HT], pairs)
                if c == 1:
                    t_B_free[h % NB] = t
                tm, tu = terms[unit % 2], turned[unit % NR]
                dve.wait(t, t_rope, t_term_free[unit % 2])
                for k, (half, tab) in enumerate(((0, 0), (1, 1), (1, 2), (0, 3))):
                    t_m = dve.do(lambda e, k=k, half=half, tab=tab: e.tensor_tensor(
                        tm[:, k, :].rearrange("p (b s) -> p b s", s=S),
                        psum[0:DQH, banks[half], 0:HT].rearrange("p (b s) -> p b s", s=S),
                        rope[:, tab:tab + 1, :].broadcast_to([DQH, HT // S, S]), ALU.mult))
                for bank in banks:
                    bank_free[bank] = t_m
                pool.wait(t_m, t_turn_free[unit % NR])
                pool.do(lambda e: e.tensor_tensor(tu[:, 0, :], tm[:, 0, :], tm[:, 1, :], ALU.subtract))
                t_t = pool.do(lambda e: e.tensor_tensor(tu[:, 1, :], tm[:, 2, :], tm[:, 3, :], ALU.add))
                t_term_free[unit % 2] = t_turned[unit] = t_t

            def to_keys(unit):
                pair, c, bank = unit // 4, unit % 4 // 2, 5 + unit // 2 % 3
                pe.wait(t_turned[unit - 1], t_turned[unit], bank_free[bank])
                for half in range(2):
                    for odd in range(2):
                        tu = turned[(unit - 1 + odd) % NR]
                        t = pe.do(mm(psum[odd * DC:(odd + 1) * DC, bank, 0:HT], U2[:, 2 * pair + odd, half, :],
                                     tu[:, half, :], half == 0, half == 1))
                t_turn_free[(unit - 1) % NR] = t_turn_free[unit % NR] = t
                act.wait(t)
                bank_free[bank] = act.do(lambda e: e.activation(
                    QR[:, pair, c * HT:(c + 1) * HT], psum[:, bank, 0:HT], ACT.Copy))

            head_weights(0)
            head_weights(1)
            for unit in range(2 * H + 2):
                if unit < 2 * H:
                    turn(unit)
                if unit % 4 < 2 and unit // 4 * 2 + 2 + unit % 4 < H:
                    head_weights(unit // 4 * 2 + 2 + unit % 4)
                if unit >= 2 and unit % 2 == 1:
                    to_keys(unit - 2)
        t_qr_done = act.tick()
        phase_barrier()

        o_rows = 32 + NT
        mem.at = folded_at
        Q1 = [mem.take("Q1", [P, T], F32R) for _ in range(2)]
        Q2 = [mem.take("Q2", [P, T], F32R) for _ in range(2)]
        assert mem.at <= base
        mem.at = top if first else after_k1
        Q1.append(mem.take("Q1", [P, T], F32R))
        if first:
            Q1 += [mem.take("Q1", [P, T], F32R) for _ in range(3)]
            Q2 += [mem.take("Q2", [P, T], F32R) for _ in range(4)]
        bd = mem.take("bd", [64, T], F32)
        RT = mem.take("RT", [64, P], F32R)
        RD = mem.take("RD", [64, T], F32R)
        rden = mem.take("rden", [P, NT], F32)
        ones_r = mem.take("ones_r", [64, P], F32R)
        t_bd = dma.start(dsem("bd"), bd[:, :], io["blockdiag"])
        t_zero = dve.do(lambda e: e.memset(RT[:, :].bitcast(F32), 0.0))
        t_one_r = dve.do(lambda e: e.tensor_copy(ones_r[:, :], ones[0:64, :]))

        def make_queries(b, q1, q2, t_free):
            tok = slice(b * S, (b + 1) * S)

            def copy_hi(odd, copy):
                raw = QR[odd * DC:(odd + 1) * DC, :, tok]
                act.wait(t_qr_done, t_free)
                return act.do(lambda e: e.activation(
                    q1[copy * DC:(copy + 1) * DC, odd * HT:(odd + 1) * HT].rearrange("p (m s) -> p m s", s=S),
                    raw, ACT.Copy))

            def lo(odd, t1):
                eng = pool if first else dve
                raw = QR[odd * DC:(odd + 1) * DC, :, tok]
                part = slice(odd * DC, (odd + 1) * DC)
                eng.wait(t1, t_free)
                return eng.do(lambda e: e.tensor_tensor(
                    q2[0:DC, odd * HT:(odd + 1) * HT].rearrange("p (m s) -> p m s", s=S), raw,
                    q1[part, odd * HT:(odd + 1) * HT].bitcast(F32).rearrange("p (m s) -> p m s", s=S), ALU.subtract))

            return copy_hi, lo

        def spread_max(q2, neg_max, t_max, bank, t_free):
            pe.wait(t_max, t_ident)
            t = pe.do(lambda e: e.transpose(psum[0:NT, bank, 0:P], neg_max, ident[:, :]))
            dve.wait(t, t_bd, t_free)
            t = dve.do(lambda e: e.tensor_tensor(
                q2[DC:DC + NT, :].rearrange("p (j q) -> p j q", q=P),
                psum[0:NT, bank, 0:P].unsqueeze(1).broadcast_to([NT, NT, P]),
                bd[0:NT, :].rearrange("p (j q) -> p j q", q=P), ALU.mult))
            bank_free[bank] = t
            return t

        def sum_keys(tile, rows, t_sums, bank):
            pe.wait(t_sums, t_ones)
            for j in range(NT):
                t = pe.do(mm(psum[:, bank, j:j + P], tile[0:rows, j * P:(j + 1) * P], ones[0:rows, :], True, True))
            dve.wait(t)
            t_r = dve.do(lambda e: e.reciprocal(rden[:, :], psum[:, bank, 0:NT]))
            bank_free[bank] = t_r
            return t, t_r

        state = {"rd_free": None}

        def spread_reciprocals(t_r, bank):
            pe.wait(t_r)
            t = pe.do(lambda e: e.transpose(psum[0:NT, bank, 0:P], rden[:, :], ident[:, :]))
            dve.wait(t, t_zero)
            t = dve.do(lambda e: e.tensor_copy(RT[0:NT, :], psum[0:NT, bank, 0:P]))
            dve.wait(t)
            t = dve.do(lambda e: e.tensor_tensor(RT[32:o_rows, :], psum[0:NT, bank, 0:P],
                                                 RT[0:NT, :].bitcast(F32), ALU.subtract))
            bank_free[bank] = t
            dve.wait(t, t_bd, state["rd_free"])
            return dve.do(lambda e: e.tensor_tensor(
                RD[0:o_rows, :].rearrange("p (j q) -> p j q", q=P),
                RT[0:o_rows, :].bitcast(F32).unsqueeze(1).broadcast_to([o_rows, NT, P]),
                bd[0:o_rows, :].rearrange("p (j q) -> p j q", q=P), ALU.mult))

        def divide(b, odd, o1, t_o1, t_rd, bank):
            pe.wait(t_rd, t_one_r)
            cols = slice(odd * HT, (odd + 1) * HT)
            t = pe.do(mm(psum[:, bank, 0:HT], ones_r[0:o_rows, :], RD[0:o_rows, cols], True, True))
            state["rd_free"] = t
            dve.wait(t, t_o1)
            t = dve.do(lambda e: e.tensor_tensor(
                QR[odd * DC:(odd + 1) * DC, :, b * S:(b + 1) * S],
                o1[:, cols].rearrange("p (m s) -> p m s", s=S),
                psum[0:DC, bank, 0:HT].rearrange("p (m s) -> p m s", s=S), ALU.mult))
            bank_free[bank] = t
            return t

        if first:
            K1t = mem.take("K1", [P, B // 2, 3, DC], F32R)
            K2t = mem.take("K2", [P, B // 2, 3, DC], F32R)

            def keys_of(K, rows, b):
                return K[0:rows, b // 2, b % 2:b % 2 + 2, :].rearrange("p a n -> p (a n)")

            mkf = mem.take("mask_k", [S, HT], F32)
            mq = mem.take("mask_q_bf", [P, NT * S], BF16)
            mk = mem.take("mask_k_bf", [S, HT], BF16)
            ident_b = mem.take("ident_bf", [P, P], BF16)
            ident2 = mem.take("ident2_bf", [S, P], BF16)
            O1 = [mem.take("O1", [P, T], F32) for _ in range(2)]
            nm = [mem.take("nm", [P, NT], F32) for _ in range(4)]
            V2 = mem.take("V2", [P, B // 2, P], F32)
            ones2 = mem.take("ones2", [P, P], F32)
            bd2 = mem.take("bd2", [64, T], F32)
            pick = mem.take("pick", [64, P], F32)
            pick_r = mem.take("pick_r", [64, P], F32R)
            rden2 = mem.take("rden2", [P, 2 * NT], F32)
            here, mem.at = mem.at, norm_at
            E = [mem.take("E", [P, T], F32) for _ in range(2)]
            assert mem.at <= norm_end
            mem.at = norm_at
            V0 = mem.take("V0", [S, B, DC], F32)
            mqf = mem.take("mask_q", [P, NT * S], F32)
            mem.at = here
            t_v0 = dma.start(dsem("v0"), V0[:, :, :], io["ctx"][:, 0:S, :].rearrange("b l d -> l b d"))
            dma.start(dsem("masks"), mqf[:, :], io["mask_q"])
            dma.start(dsem("masks"), ones2[:, :], io["ones2"])
            dma.start(dsem("masks"), bd2[:, :], io["blockdiag2"])
            dma.start(dsem("masks"), pick[:, :], io["pick2"])
            t_masks = dma.start(dsem("masks"), mkf[:, :], io["mask_k"])
            t = dve.do(lambda e: e.memset(V2[:, :, :], 0.0))
            dve.wait(t, t_v0)
            for r in range(2):
                t_v2 = dve.do(lambda e, r=r: e.tensor_copy(V2[r * DC:r * DC + S, :, r * DC:(r + 1) * DC],
                                                           V0[:, r:B:2, :]))
            t = dve.do(lambda e: e.memset(ident2[:, :], 0.0))
            dve.wait(t, t_ident, t_masks)
            for r in range(2):
                dve.do(lambda e, r=r: e.tensor_copy(ident2[:, r * DC:r * DC + S], ident[0:S, 0:S]))
            dve.do(lambda e: e.tensor_copy(pick_r[:, :], pick[:, :]))
            dve.do(lambda e: e.memset(K1t[:, :, :, :].bitcast(F32), 0.0))
            t = dve.do(lambda e: e.memset(K2t[:, :, :, :].bitcast(F32), 0.0))
            act.wait(t)
            dve.wait(t)
            t_k2 = dve.do(lambda e: e.memset(K2t[DC:DC + NT, :, 0:3:2, 0:S].bitcast(F32), 1.0))
            dve.wait(t_masks, t_ident)
            dve.do(lambda e: e.tensor_copy(mq[:, :], mqf[:, :]))
            dve.do(lambda e: e.tensor_copy(mk[:, :], mkf[:, :]))
            t_masks = dve.do(lambda e: e.tensor_copy(ident_b[:, :], ident[:, :]))
            for c in range(2):
                pe.wait(t_v0, bank_free[c])
                for b in range(8 * c, 8 * c + 8):
                    t = pe.do(lambda e, b=b, c=c: e.transpose(psum[0:DC, c, (b % 8) * S:(b % 8 + 1) * S], V0[:, b, :],
                                                              ident[0:S, 0:S]))
                n = slice(4 * c, 4 * c + 4)
                src = psum[0:DC, c, 0:HT].rearrange("p (a r s) -> p a r s", r=2, s=S)
                act.wait(t)
                act.do(lambda e, n=n, src=src: e.activation(K1t[0:DC, n, 0:3:2, 0:S], src, ACT.Copy))
                t_h = act.do(lambda e, n=n, src=src: e.activation(K2t[0:DC, n, 0:3:2, 0:S], src, ACT.Copy))
                dve.wait(t_h)
                t_keys = dve.do(lambda e, n=n, src=src: e.tensor_tensor(
                    K1t[DC:P, n, 0:3:2, 0:S], src, K1t[0:DC, n, 0:3:2, 0:S].bitcast(F32), ALU.subtract))
                bank_free[c] = t_keys
            at = [2]

            def next_bank():
                at[0] += 1
                bank = at[0] % 8
                pe.wait(bank_free[bank])
                return bank

            ROWS = 2 * NT

            def queries0(p):
                for b in (2 * p, 2 * p + 1):
                    copy_hi, lo = make_queries(b, Q1[b % 6], Q2[b % 6], tk.get(("scored", p - 3)))
                    for odd in range(2):
                        for copy in range(2):
                            tk["q1", b] = copy_hi(odd, copy)
                        tk["q2", b] = lo(odd, tk["q1", b])

            def maxima0(p):
                for b in (2 * p, 2 * p + 1):
                    bank = next_bank()
                    pe.wait(tk["q1", b], t_keys, t_masks)
                    pe.run(mm(psum[:, bank, 0:NT * S], ident_b[:, :], mq[:, :], True, False, skip_group_check=True))
                    for j in range(NT):
                        t = pe.do(mm(psum[:, bank, j * S:(j + 1) * S], Q1[b % 6][:, j * P:(j + 1) * P],
                                     K1t[:, b // 2, b % 2 * 2, 0:S], False, j == NT - 1, skip_group_check=True))
                    dve.wait(t, tk.get(("spread", b - 4)))
                    tk["max", b] = t = dve.do(lambda e, b=b, bank=bank: e.tensor_reduce(
                        nm[b % 4][:, :], psum[:, bank, 0:NT * S].rearrange("p (j l) -> p j l", l=S),
                        AX.X, ALU.max, negate=True))
                    bank_free[bank] = t

            def spread0(p):
                for b in (2 * p, 2 * p + 1):
                    tk["spread", b] = spread_max(Q2[b % 6], nm[b % 4][:, :], tk["max", b], next_bank(),
                                                 tk.get(("scored", p - 3)))

            def scores0(p):
                pe.wait(t_k2, *(tk[name, b] for name in ("q1", "q2", "spread") for b in (2 * p, 2 * p + 1)))
                for c in range(2):
                    bank = next_bank()
                    n = slice(c * HT, (c + 1) * HT)
                    pe.run(mm(psum[0:P, bank, 0:HT], ident2[:, 0:P], mk[:, :], True, False, skip_group_check=True))
                    for r in range(2):
                        b = 2 * p + r
                        pe.run(mm(psum[:, bank, 0:HT], keys_of(K1t, P, b),
                                  Q1[b % 6][:, n], False, False, skip_group_check=True))
                    for r in range(2):
                        b = 2 * p + r
                        t = pe.do(mm(psum[:, bank, 0:HT], keys_of(K2t, DC + NT, b),
                                     Q2[b % 6][0:DC + NT, n], False, r == 1, skip_group_check=True))
                    act.wait(t, tk.get(("summed", p - 2)), tk.get(("valued", p - 2)))
                    t_e = act.do(lambda e, bank=bank, n=n: e.activation(E[p % 2][0:P, n], psum[0:P, bank, 0:HT], ACT.Exp))
                    bank_free[bank] = t_e
                tk["scored", p], tk["exp", p] = t, t_e

            def values0(p):
                for c in range(2):
                    bank = next_bank()
                    pe.wait(tk["exp", p], t_v2)
                    n = slice(c * HT, (c + 1) * HT)
                    t = pe.do(mm(psum[:, bank, 0:HT], V2[0:P, p, :], E[p % 2][0:P, n], True, True))
                    act.wait(t, tk.get(("divided", p - 2)))
                    t_o = act.do(lambda e, bank=bank, n=n: e.activation(O1[p % 2][:, n], psum[:, bank, 0:HT], ACT.Copy))
                    bank_free[bank] = t_o
                tk["valued", p], tk["o1", p] = t, t_o
                bank = next_bank()
                for j in range(NT):
                    t = pe.do(mm(psum[:, bank, 2 * j:2 * j + P], E[p % 2][0:P, j * P:(j + 1) * P],
                                 ones2[0:P, :], True, True))
                dve.wait(t, tk.get(("rt", p - 1)))
                tk["summed", p] = t
                bank_free[bank] = tk["recip", p] = dve.do(lambda e: e.reciprocal(rden2[:, :], psum[:, bank, 0:ROWS]))

            def reciprocals0(p):
                bank = next_bank()
                rows = 32 + ROWS
                pe.wait(tk["recip", p])
                t = pe.do(lambda e: e.transpose(psum[0:ROWS, bank, 0:P], rden2[:, :], ident[:, :]))
                dve.wait(t, t_zero)
                t = dve.do(lambda e: e.tensor_copy(RT[0:ROWS, :], psum[0:ROWS, bank, 0:P]))
                dve.wait(t)
                t = dve.do(lambda e: e.tensor_tensor(RT[32:rows, :], psum[0:ROWS, bank, 0:P],
                                                     RT[0:ROWS, :].bitcast(F32), ALU.subtract))
                bank_free[bank] = t
                dve.wait(t, tk.get(("divided", p - 1)), state["rd_free"])
                tk["rd", p] = tk["rt", p] = dve.do(lambda e: e.tensor_tensor(
                    RD[0:rows, :].rearrange("p (j q) -> p j q", q=P),
                    RT[0:rows, :].bitcast(F32).unsqueeze(1).broadcast_to([rows, NT, P]),
                    bd2[0:rows, :].rearrange("p (j q) -> p j q", q=P), ALU.mult))

            def divide0(p):
                for odd in range(2):
                    bank = next_bank()
                    cols = slice(odd * HT, (odd + 1) * HT)
                    pe.wait(tk["rd", p])
                    t = pe.do(mm(psum[:, bank, 0:HT], pick_r[0:32 + ROWS, :], RD[0:32 + ROWS, cols], True, True))
                    state["rd_free"] = t
                    dve.wait(t, tk["o1", p])
                    for r in range(2):
                        b, part = 2 * p + r, slice(r * DC, (r + 1) * DC)
                        t = dve.do(lambda e, b=b, part=part, odd=odd, cols=cols, bank=bank: e.tensor_tensor(
                            QR[odd * DC:(odd + 1) * DC, :, b * S:(b + 1) * S],
                            O1[p % 2][part, cols].rearrange("p (m s) -> p m s", s=S),
                            psum[part, bank, 0:HT].rearrange("p (m s) -> p m s", s=S), ALU.mult))
                    bank_free[bank] = t
                tk["divided", p] = t

            stages = [queries0, maxima0, spread0, scores0, values0, reciprocals0, divide0]
            for step in range(B // 2 + len(stages) - 1):
                for n in reversed(range(len(stages))):
                    if 0 <= step - n < B // 2:
                        stages[n](step - n)
            t_out_last = tk["divided", B // 2 - 1]
        else:
            NE = 6
            CW = L // 3
            K2t = [mem.take("K2", [P, L], F32R) for _ in range(2)]
            E = [mem.take("E", [P, T], F32) for _ in range(NE)]
            here, mem.at = mem.at, norm_at
            SA = [mem.take("SA", [P, T], F32) for _ in range(2)]
            assert mem.at <= norm_end
            mem.at = here
            O1 = mem.take("O1", [DC, T], F32)
            mx = mem.take("mx", [P, 2, NT * 3], F32)
            nm = mem.take("nm", [P, 2, NT], F32)
            for k in K2t:
                t_k2 = dve.do(lambda e, k=k: e.memset(k[DC:DC + NT, :].bitcast(F32), 1.0))
            at = [0]

            def small_bank():
                at[0] += 1
                bank = 6 + at[0] % 2
                pe.wait(bank_free[bank])
                return bank

            def copy_keys(b, n):
                act.wait(tk["k1", b], tk.get(("scored", b - 2)))
                cols = slice(n * CW, (n + 1) * CW)
                tk["k2", b] = act.do(lambda e: e.activation(
                    K2t[b % 2][0:DC, cols], K1t[b % 3][0:DC, cols].bitcast(F32), ACT.Copy))

            def queries(b, n):
                copy_hi, lo = make_queries(b, Q1[b % 3], Q2[b % 2], None)
                if n < 4:
                    act.wait(tk.get(("scored", b - 3)))
                    tk["q1", b] = copy_hi(n // 2, n % 2)
                else:
                    dve.wait(tk.get(("scored", b - 2)))
                    tk["q2", b] = lo(n - 4, tk["q1", b])

            def max_unit(b, j, c):
                bank = small_bank()
                pe.wait(tk["q1", b], tk["k1", b])
                t = pe.do(mm(psum[:, bank, 0:CW], Q1[b % 3][:, j * P:(j + 1) * P], K1t[b % 3][:, c * CW:(c + 1) * CW],
                             True, True))
                dve.wait(t)
                bank_free[bank] = tk["mx", b] = dve.do(lambda e: e.tensor_reduce(
                    mx[:, b % 2, j * 3 + c:j * 3 + c + 1], psum[:, bank, 0:CW], AX.X, ALU.max))

            def max_total(b):
                dve.wait(tk["mx", b])
                tk["max", b] = dve.do(lambda e: e.tensor_reduce(
                    nm[:, b % 2, :], mx[:, b % 2, :].rearrange("p (j c) -> p j c", c=3), AX.X, ALU.max, negate=True))

            def max_spread(b):
                tk["spread", b] = spread_max(Q2[b % 2], nm[:, b % 2, :], tk["max", b], small_bank(),
                                             tk.get(("scored", b - 2)))

            def ring(b, k):
                return (b * NL + k) % NE

            readers = {}

            def scores(b, k):
                pair = (0, 1) if k % 2 == 0 else (2, 3)
                cols = slice(k * LP, (k + 1) * LP)
                pe.wait(tk["k1", b], tk["k2", b], tk["q1", b], tk["q2", b], tk["spread", b], t_k2, bank_free[pair[0]])
                for c in range(2):
                    pe.run(mm(psum[0:LP, pair[c], 0:HT], K1t[b % 3][:, cols], Q1[b % 3][:, c * HT:(c + 1) * HT], True, False))
                for c in range(2):
                    t = pe.do(mm(psum[0:LP, pair[c], 0:HT], K2t[b % 2][0:DC + NT, cols],
                                 Q2[b % 2][0:DC + NT, c * HT:(c + 1) * HT], False, True))
                if k == NL - 1:
                    tk["scored", b] = t
                n = ring(b, k)
                act.wait(t, *readers.get(n, ()))
                t = act.do(lambda e: e.activation(E[n][0:LP, :].rearrange("p (c q) -> p c q", c=2),
                                                  psum[0:LP, pair[0]:pair[0] + 2, 0:HT], ACT.Exp))
                bank_free[pair[0]] = bank_free[pair[1]] = t
                tk["exp", b, k] = t
                readers[n] = []
                if k == 0:
                    return
                eng = dve if k == 1 else pool
                a = SA[b % 2][0:LP, :]
                prev = E[ring(b, 0)][0:LP, :] if k == 1 else a
                eng.wait(t, tk.get(("summed", b - 2)) if k == 1 else tk["sum", b])
                t = eng.do(lambda e: e.tensor_tensor(a, prev, E[n][0:LP, :], ALU.add))
                tk["sum", b] = t
                readers[n].append(t)
                if k == 1:
                    readers[ring(b, 0)].append(t)

            def values(b, pair, c):
                ks = (2 * pair, 2 * pair + 1)
                pe.wait(tk["exp", b, ks[1]], bank_free[4 + c])
                for k in ks:
                    t = pe.do(mm(psum[(k % 2) * DC:(k % 2 + 1) * DC, 4 + c, 0:HT], V[0:LP, b, k * DC:(k + 1) * DC],
                                 E[ring(b, k)][0:LP, c * HT:(c + 1) * HT], pair == 0, pair == NL // 2 - 1))
                for k in ks:
                    readers[ring(b, k)].append(t)
                if pair == NL // 2 - 1:
                    cols = slice(c * HT, (c + 1) * HT)
                    act.wait(t, tk.get(("divided", b - 1)))
                    t = act.do(lambda e: e.activation(O1[:, cols], psum[DC:P, 4 + c, 0:HT], ACT.Copy))
                    dve.wait(t)
                    t = dve.do(lambda e: e.tensor_tensor(O1[:, cols], psum[0:DC, 4 + c, 0:HT], O1[:, cols], ALU.add))
                    bank_free[4 + c] = tk["o1", b] = t

            def total(b):
                dve.wait(tk.get(("rt", b - 1)))
                tk["summed", b], tk["recip", b] = sum_keys(SA[b % 2], LP, tk["sum", b], small_bank())

            def reciprocals(b):
                tk["rd", b] = tk["rt", b] = spread_reciprocals(tk["recip", b], small_bank())

            def division(b, odd):
                tk["divided", b] = divide(b, odd, O1, tk["o1", b], tk["rd", b], small_bank())

            units = [(j, c) for j in range(NT) for c in range(3)]
            if layer == 2:
                load_keys(1)
            for n in range(4):
                queries(0, n)
            for n, (j, c) in enumerate(units):
                max_unit(0, j, c)
                if n < 3:
                    copy_keys(0, n)
                if n in (4, 5):
                    queries(0, n)
                if 6 <= n < 10:
                    queries(1, n - 6)
            max_total(0)
            max_spread(0)
            for b in range(B):
                todo = list(units) if b + 1 < B else []
                if b + 2 < B:
                    load_keys(b + 2)
                for slot in range(2 * NL):
                    if slot % 2 == 0:
                        scores(b, slot // 2)
                    elif slot >= 4:
                        values(b, slot // 4 - 1, (slot % 4) // 2)
                    elif b > 0:
                        values(b - 1, NL // 2 - 1, (slot % 4) // 2)
                    if b + 2 < B and slot in (5, 9, 13, 17):
                        queries(b + 2, (5, 9, 13, 17).index(slot))
                    if b + 1 < B:
                        if slot in (7, 11, 15):
                            copy_keys(b + 1, (7, 11, 15).index(slot))
                        if slot in (4, 6):
                            queries(b + 1, 4 + (slot - 4) // 2)
                        for _ in range(0 if slot == 3 else 2 if slot == 19 else 1):
                            if todo:
                                max_unit(b + 1, *todo.pop(0))
                                if not todo:
                                    max_total(b + 1)
                        if slot == 21:
                            max_spread(b + 1)
                    if b > 0:
                        if slot == 8:
                            total(b - 1)
                        if slot == 12:
                            reciprocals(b - 1)
                        if slot == 16:
                            division(b - 1, 0)
                        if slot == 18:
                            division(b - 1, 1)
            for c in range(2):
                values(B - 1, NL // 2 - 1, c)
            total(B - 1)
            reciprocals(B - 1)
            for odd in range(2):
                division(B - 1, odd)
            t_out_last = tk["divided", B - 1]
        phase_barrier()

        mem.at = top
        NC = 3
        CH = [mem.take("CH", [P, H // 2, P], F32R) for _ in range(NC)]
        CL = [mem.take("CL", [P, H // 2, P], F32R) for _ in range(NC)]
        t_c, c_free = {}, {}
        assert mem.at <= w1_at
        side = ternary_weights() if layer == 1 else iter(())
        next(side, None)

        def parts(i):
            ch, cl, tok = CH[i % NC], CL[i % NC], slice(i * P, (i + 1) * P)
            act.wait(t_out_last, c_free.get(i - NC))
            t = act.do(lambda e: e.activation(ch[:, :, :], QR[:, :, tok], ACT.Copy))
            pool.wait(t)
            t_c[i] = pool.do(lambda e: e.tensor_tensor(cl[:, :, :], QR[:, :, tok], ch[:, :, :].bitcast(F32), ALU.subtract))

        parts(0)
        parts(1)
        for i in range(NT):
            if i + 2 < NT:
                parts(i + 2)
            pe.wait(bank_free[i % 4], t_c[i])
            pairs = []
            for m in range(H // 2):
                pairs += split_pairs(CH[i % NC][:, m, :], CL[i % NC][:, m, :], MH[:, m, :], ML[:, m, :])
            t = c_free[i] = product(psum[:, i % 4, 0:D], pairs)
            if to_transpose and i >= 2:
                norm_transpose(i - 2)
            dve.wait(t, t_tanh)
            t_x = dve.do(lambda e, i=i: e.scalar_tensor_tensor(
                X[:, i, :], psum[:, i % 4, 0:D], tanh_g[:, layer:layer + 1], X[:, i, :], ALU.mult, ALU.add))
            bank_free[i % 4] = t_x
            norm_stats(i, t_x)
            if i >= 1:
                norm_apply(i - 1)
            next(side, None)
        for _ in side:
            pass
        norm_apply(NT - 1)
        if to_transpose:
            norm_transpose(NT - 2)
            norm_transpose(NT - 1)
        phase_barrier()
        return t_x

    def logits(gate, n_exp, t_yh, t_yl):
        GW = mem.take("gate_w", [P, KD, n_exp], F32)
        GH = mem.take("gate_hi", [P, KD, n_exp], F32R)
        GL = mem.take("gate_lo", [P, KD, n_exp], F32R)
        t = dma.start(dsem("gate_w"), GW[:, :, :], gate)
        dve.wait(t)
        t = dve.do(lambda e: e.tensor_copy(GH[:, :, :], GW[:, :, :]))
        dve.wait(t)
        t = dve.do(lambda e: e.tensor_tensor(GL[:, :, :], GW[:, :, :], GH[:, :, :].bitcast(F32), ALU.subtract))
        pe.wait(t, t_yh, t_yl, bank_free[3])
        for i in range(NT):
            tok = slice(i * P, (i + 1) * P)
            pairs = []
            for kd in range(KD):
                pairs += split_pairs(YH[:, kd, tok], YL[:, kd, tok], GH[:, kd, :], GL[:, kd, :])
            t = product(psum[:, 3, i * n_exp:(i + 1) * n_exp], pairs)
        return t, psum[:, 3, 0:NT * n_exp].rearrange("p (i n) -> p i n", n=n_exp)

    def choose(values, t_in, n, top, name):
        wide = n + 8 - top
        v8 = mem.take(name + "_top8", [P, NT, 8], F32)
        left = mem.take(name + "_left", [P, NT, wide], F32)
        mask = mem.take(name + "_mask", [P, NT, n], F32)
        dve.wait(t_in)
        for i in range(NT):
            t = dve.do(lambda e, i=i: e.max(v8[:, i, :], values[:, i, :]))
        dve.wait(t)
        for i in range(NT):
            t = dve.do(lambda e, i=i: e.match_replace(left[:, i, :], v8[:, i, :], values[:, i, :], -BIG))
        dve.wait(t)
        t = dve.do(lambda e: e.tensor_tensor(mask[:, :, :], values[:, :, 0:n], left[:, :, 0:n], ALU.not_equal))
        return mask, t

    def softmax_rows(src, n, t_in, wide):
        m = mem.take("lmax", [P, NT], F32)
        ex = mem.take("lexp", [P, NT, n], F32)
        sm = mem.take("lsum", [P, NT], F32)
        pr = mem.take("probs", [P, NT, wide], F32)
        t0 = dve.do(lambda e: e.memset(pr[:, :, :], BIG))
        dve.wait(t_in)
        t = dve.do(lambda e: e.tensor_reduce(m[:, :], src, AX.X, ALU.max))
        dve.wait(t)
        t = dve.do(lambda e: e.tensor_tensor(ex[:, :, :], src, m[:, :].unsqueeze(2).broadcast_to([P, NT, n]), ALU.subtract))
        bank_free[3] = t
        act.wait(t)
        t = act.do(lambda e: e.activation(ex[:, :, :], ex[:, :, :], ACT.Exp))
        dve.wait(t)
        t = dve.do(lambda e: e.tensor_reduce(sm[:, :], ex[:, :, :], AX.X, ALU.add))
        dve.wait(t)
        t = dve.do(lambda e: e.reciprocal(sm[:, :], sm[:, :]))
        dve.wait(t, t0)
        t = dve.do(lambda e: e.tensor_tensor(pr[:, :, 0:n], ex[:, :, :], sm[:, :].unsqueeze(2).broadcast_to([P, NT, n]), ALU.mult))
        return pr, t

    def gates_transposed(Gt, n, lo_row, t_in):
        GT = mem.take("GT", [P, T], F32R)
        t0 = None
        if lo_row != n:
            t0 = dve.do(lambda e: e.memset(GT[:, :].bitcast(F32), 0.0))
        pe.wait(t_in)
        for a, tiles in enumerate((range(0, 4), range(4, NT))):
            bank = upper_bank()
            for i in tiles:
                t = pe.do(lambda e, i=i, a=a, bank=bank: e.transpose(
                    psum[0:n, bank, (i - 4 * a) * P:(i - 4 * a + 1) * P], Gt[:, i, :], ident[:, :]))
            w = len(tiles) * P
            cols = slice(a * 512, a * 512 + w)
            dve.wait(t, t0)
            t = dve.do(lambda e, cols=cols, bank=bank, w=w: e.tensor_copy(GT[0:n, cols], psum[0:n, bank, 0:w]))
            dve.wait(t)
            t = dve.do(lambda e, cols=cols, bank=bank, w=w: e.tensor_tensor(
                GT[lo_row:lo_row + n, cols], psum[0:n, bank, 0:w], GT[0:n, cols].bitcast(F32), ALU.subtract))
            bank_free[bank] = t
        return GT, t

    def expert_blocks(weights, gate_col, nblk, swiglu, selector, sel_rows, n_free, GT, t_yh, t_yl, routing=(), side=(), last=False):
        routing, side = iter(routing), iter(side)
        WID = 768 if swiglu else 512
        NW = 4
        w_at = mem.at
        WS = [mem.take("WS", [P, WID], F32) for _ in range(NW)]
        WH = [mem.take("WH", [P, WID], F32R) for _ in range(NW)]
        WL = [mem.take("WL", [P, WID], F32R) for _ in range(NW)]
        NH = 4
        here, mem.at = mem.at, norm_at
        R = [mem.take("R", [P, HT], F32) for _ in range(NH)]
        assert mem.at <= norm_end
        mem.at = here
        HF = [mem.take("HF", [P, HT], F32) for _ in range(NH)]
        HH = [mem.take("HH", [P, HT], F32R) for _ in range(NH)]
        HL = [mem.take("HL", [P, HT], F32R) for _ in range(NH)]
        ws_free, w_free = [None] * NW, [None] * NW
        r_free, h_free, hf_free = [None] * NH, [None] * NH, [None] * NH
        t_w = {}

        t_load, t_up = {}, {}

        def fetch(n):
            k = n % NW
            sp.wait(*(ws_free[k] or ()))
            t_load[n] = dma.start(dsem(f"ws{k}"), WS[k][:, :], weights[n])

        def split(n):
            k = n % NW
            act.wait(t_load[n], w_free[k])
            t_h = act.do(lambda e: e.activation(WH[k][:, :], WS[k][:, :], ACT.Copy))
            pool.wait(t_h, w_free[k])
            t_l = pool.do(lambda e: e.tensor_tensor(WL[k][:, :], WS[k][:, :], WH[k][:, :].bitcast(F32), ALU.subtract))
            ws_free[k] = (t_h, t_l)
            t_w[n] = (t_h, t_l)

        def up(n, c):
            k, u = n % NW, (2 * n + c) % NH
            cols = slice(c * HT, (c + 1) * HT)
            pe.wait(*t_w[n], t_yh, t_yl)
            outs = []
            for part in range(2 if swiglu else 1):
                bank = upper_bank()
                pairs = []
                for kd in range(KD):
                    m = slice(part * D + kd * P, part * D + (kd + 1) * P)
                    pairs += split_pairs(WH[k][:, m], WL[k][:, m], YH[:, kd, cols], YL[:, kd, cols])
                t = product(psum[:, bank, 0:HT], pairs)
                outs.append((bank, t))
            r, hf = R[u], HF[u]
            bank, t = outs[0]
            act.wait(t, r_free[u])
            t_r = act.do(lambda e: e.activation(r[:, :], psum[:, bank, 0:HT], ACT.Silu if swiglu else ACT.Relu))
            bank_free[bank] = t_r
            if swiglu:
                b2, t2 = outs[1]
                dve.wait(t_r, t2, hf_free[u])
                t_r = dve.do(lambda e: e.tensor_tensor(hf[:, :], r[:, :], psum[:, b2, 0:HT], ALU.mult))
                bank_free[b2] = r_free[u] = t_r
            t_up[n, c] = t_r

        def gate(n, c):
            u = (2 * n + c) % NH
            cols = slice(c * HT, (c + 1) * HT)
            r, hf, hh, hl = R[u], HF[u], HH[u], HL[u]
            t = t_up[n, c]
            src = hf if swiglu else r
            if n >= n_free:
                gb = upper_bank()
                pe.wait(GT["tick"])
                t_g = pe.do(mm(psum[:, gb, 0:HT], selector(n - n_free), GT["tile"][0:sel_rows, cols], True, True))
                dve.wait(t, t_g, hf_free[u])
                t = dve.do(lambda e: e.tensor_tensor(hf[:, :], src[:, :], psum[:, gb, 0:HT], ALU.mult))
                bank_free[gb] = t
            if not swiglu:
                once = hf if n >= n_free else r
                dve.wait(t, hf_free[u])
                t = dve.do(lambda e: e.tensor_tensor(hf[:, :], once[:, :], r[:, :], ALU.mult))
                r_free[u] = t
            act.wait(t, h_free[u])
            t_hh = act.do(lambda e: e.activation(hh[:, :], hf[:, :], ACT.Copy))
            pool.wait(t_hh, h_free[u])
            t_hl = pool.do(lambda e: e.tensor_tensor(hl[:, :], hf[:, :], hh[:, :].bitcast(F32), ALU.subtract))
            hf_free[u] = t_hl
            return t_hh, t_hl

        def down(n, c, ticks):
            k, u = n % NW, (2 * n + c) % NH
            off = WID - D
            pe.wait(*ticks)
            for m in range(KD):
                mcol = slice(off + m * P, off + (m + 1) * P)
                if n == 0:
                    pe.wait(bank_free[m * 2 + c])
                prs = split_pairs(WH[k][:, mcol], WL[k][:, mcol], HH[u][:, :], HL[u][:, :])
                for q, (a, bb) in enumerate(prs):
                    f = mm(psum[:, m * 2 + c, 0:HT], a, bb, n == 0 and q == 0, n == nblk - 1 and q == 2)
                    if q == 2:
                        t = pe.do(f)
                    else:
                        pe.run(f)
            h_free[u] = t
            if c == 1:
                w_free[k] = t
            return t

        for n in range(3):
            fetch(n)
        split(0)
        split(1)
        slots = [(n, c) for n in range(nblk) for c in range(2)]
        ready = {}
        for k in range(len(slots) + 3):
            if k < len(slots):
                n, c = slots[k]
                if c == 0 and n + 3 < nblk:
                    fetch(n + 3)
                up(n, c)
            if 0 <= k - 1 < len(slots):
                if slots[k - 1] == (n_free, 0):
                    for _ in routing:
                        pass
                ready[k - 1] = gate(*slots[k - 1])
            if k >= 3:
                t = down(*slots[k - 3], ready[k - 3])
                if slots[k - 3] == (nblk - 1, 0):
                    here, mem.at = mem.at, w_at
                    OT = mem.take("OT", [P, KD, T], F32)
                    mem.at = here
                    for _ in side:
                        pass
                    back_to_tokens(0, t, gate_col, OT, last)
            if k < len(slots):
                next(routing if k < 2 * n_free else side, None)
                if c == 1 and n + 2 < nblk:
                    split(n + 2)
        return back_to_tokens(1, t, gate_col, OT, last)

    def ffn0():
        mem.at = base
        t_yh, t_yl = norm["yh"], norm["yl"]
        t_lg, lg = logits(io["f0_gate"], E0, t_yh, t_yl)
        sel = mem.take("sel", [P, E0], F32)
        selr = mem.take("selr", [P, E0], F32R)
        t = dma.start(dsem("sel"), sel[:, :], io["sel0"])
        dve.wait(t)
        t_sel = dve.do(lambda e: e.tensor_copy(selr[:, :], sel[:, :]))
        GT = {}

        def routing():
            sc = mem.take("scores", [P, NT, E0], F32)
            sb = mem.take("biased", [P, NT, E0], F32)
            eb = mem.take("e_bias", [P, E0], F32)
            t_eb = dma.start(dsem("eb"), eb[:, :], io["f0_bias"].rearrange("(a n) -> a n", a=1).broadcast_to([P, E0]))
            act.wait(t_lg)
            t_sc = act.do(lambda e: e.activation(sc[:, :, :], lg, ACT.Sigmoid))
            bank_free[3] = t_sc
            dve.wait(t_sc, t_eb)
            t = dve.do(lambda e: e.tensor_tensor(sb[:, :, :], sc[:, :, :], eb[:, :].unsqueeze(1).broadcast_to([P, NT, E0]), ALU.add))
            yield
            g8 = mem.take("group_top8", [P, NT, NG0, 8], F32)
            gs = mem.take("group_score", [P, NT, NG0 + 8 - TOPG0], F32)
            t0 = dve.do(lambda e: e.memset(gs[:, :, :], BIG))
            dve.wait(t, t0)
            for i in range(NT):
                for g in range(NG0):
                    t = dve.do(lambda e, i=i, g=g: e.max(g8[:, i, g, :], sb[:, i, g * 8:(g + 1) * 8]))
            dve.wait(t)
            t = dve.do(lambda e: e.tensor_tensor(gs[:, :, 0:NG0], g8[:, :, :, 0], g8[:, :, :, 1], ALU.add))
            yield
            gm, t = choose(gs, t, NG0, TOPG0, "group")
            yield
            low = mem.take("low", [P, NT, NG0], F32)
            ms = mem.take("masked", [P, NT, E0 + 8 - TOP0], F32)
            dve.wait(t)
            t0 = dve.do(lambda e: e.memset(ms[:, :, :], BIG))
            t = dve.do(lambda e: e.tensor_scalar(low[:, :, :], gm[:, :, :], 1.0, 1e30, ALU.subtract, ALU.mult))
            dve.wait(t0, t)
            for i in range(NT):
                out3 = ms[:, i, 0:E0].rearrange("p (g k) -> p g k", k=8)
                t = dve.do(lambda e, i=i, out3=out3: e.tensor_tensor(
                    out3, sb[:, i, :].rearrange("p (g k) -> p g k", k=8),
                    gm[:, i, :].unsqueeze(2).broadcast_to([P, NG0, 8]), ALU.mult))
            dve.wait(t)
            for i in range(NT):
                out3 = ms[:, i, 0:E0].rearrange("p (g k) -> p g k", k=8)
                t = dve.do(lambda e, i=i, out3=out3: e.tensor_tensor(
                    out3, out3, low[:, i, :].unsqueeze(2).broadcast_to([P, NG0, 8]), ALU.add))
            yield
            mask, t = choose(ms, t, E0, TOP0, "expert")
            yield
            mb = mem.take("mask_bf", [P, NT, E0], BF16)
            tri = mem.take("before", [P, P], F32)
            trib = mem.take("before_bf", [P, P], BF16)
            onesb = mem.take("ones_bf", [P, P], BF16)
            t_tri = dma.start(dsem("tri"), tri[:, :], io["before"])
            dve.wait(t_tri, t)
            dve.do(lambda e: e.memset(onesb[:, :], 1.0))
            dve.do(lambda e: e.tensor_copy(trib[:, :], tri[:, :]))
            t_mb = dve.do(lambda e: e.tensor_copy(mb[:, :, :], mask[:, :, :]))
            pos_bank = upper_bank()
            pe.wait(t_mb)
            for i in range(NT):
                t_pos = product(psum[:, pos_bank, i * E0:(i + 1) * E0],
                                [(trib[:, :], mb[:, i, :])] + [(onesb[:, :], mb[:, j, :]) for j in range(i)])
            yield
            w = mem.take("w", [P, NT, E0], F32)
            keep = mem.take("keep", [P, NT, E0], F32)
            ws = mem.take("wsum", [P, NT], F32)
            t = dve.do(lambda e: e.tensor_tensor(w[:, :, :], sc[:, :, :], mask[:, :, :], ALU.mult))
            dve.wait(t)
            t = dve.do(lambda e: e.tensor_reduce(ws[:, :], w[:, :, :], AX.X, ALU.add))
            dve.wait(t)
            t = dve.do(lambda e: e.tensor_scalar(ws[:, :], ws[:, :], 1e-20, None, ALU.add))
            dve.wait(t)
            t = dve.do(lambda e: e.reciprocal(ws[:, :], ws[:, :]))
            dve.wait(t)
            t = dve.do(lambda e: e.tensor_tensor(w[:, :, :], w[:, :, :], ws[:, :].unsqueeze(2).broadcast_to([P, NT, E0]), ALU.mult))
            dve.wait(t, t_pos)
            pos = psum[:, pos_bank, 0:NT * E0].rearrange("p (i n) -> p i n", n=E0)
            t = dve.do(lambda e: e.tensor_scalar(keep[:, :, :], pos, float(CAP0), 2.5, ALU.is_lt, ALU.mult))
            bank_free[pos_bank] = t
            dve.wait(t)
            t = dve.do(lambda e: e.tensor_tensor(w[:, :, :], w[:, :, :], keep[:, :, :], ALU.mult))
            yield
            GT["tile"], GT["tick"] = gates_transposed(w, E0, E0, t)

        def side():
            at = mem.at
            yield from prepare_context()
            mem.at = at
            yield from fold_weights(1, 2, after_context)

        pe.wait(t_sel)
        t = expert_blocks(io["f0_w"], 4, NB0, False, lambda n: selr[:, n:n + 1].broadcast_to([P, P]), P, NB0 - E0,
                              GT, t_yh, t_yl, routing(), side())
        phase_barrier()
        return t

    def ffn2():
        mem.at = base
        t_yh, t_yl = norm["yh"], norm["yl"]
        t_lg, lg = logits(io["f2_gate"], E2, t_yh, t_yl)
        GT = {}

        def routing():
            pr, t = softmax_rows(lg, E2, t_lg, E2 + 8 - TOP2)
            yield
            mask, t = choose(pr, t, E2, TOP2, "expert")
            w = mem.take("w", [P, NT, E2], F32)
            dve.wait(t)
            t = dve.do(lambda e: e.tensor_tensor(w[:, :, :], pr[:, :, 0:E2], mask[:, :, :], ALU.mult))
            GT["tile"], GT["tick"] = gates_transposed(w, E2, 32, t)

        sel = mem.take("sel", [64, E2 * I2], F32)
        selr = mem.take("selr", [64, E2 * I2], F32R)
        t = dma.start(dsem("sel"), sel[:, :], io["sel2"])
        dve.wait(t)
        t_sel = dve.do(lambda e: e.tensor_copy(selr[:, :], sel[:, :]))
        pe.wait(t_sel)
        rows = 32 + E2
        t = expert_blocks(io["f2_w"], 6, NB2, True, lambda n: selr[0:rows, n * P:(n + 1) * P], rows, 0,
                              GT, t_yh, t_yl, routing(), fold_weights(3, 1))
        phase_barrier()
        return t

    def ffn3():
        mem.at = base
        t_y = [norm["y", i] for i in range(NT)]
        rw = mem.take("rms_w", [P, D], F32)
        t_rw = dma.start(dsem("rms_w"), rw[:, :], io["f3_rms"].rearrange("(a n) -> a n", a=1).broadcast_to([P, D]))
        sq = mem.take("sq", [P, D], F32)
        ss = mem.take("ss", [P, NT], F32)
        act.wait(*t_y)
        for i in range(NT):
            t = act.do(lambda e, i=i: e.activation(sq[:, :], Y[:, i, :], ACT.Square, accum_out=ss[:, i:i + 1]))
            act.wait(t)
        rr = mem.take("rr", [P, NT], F32)
        dve.wait(t)
        t = dve.do(lambda e: e.tensor_scalar(rr[:, :], ss[:, :], 1.0 / D, 1e-6, ALU.mult, ALU.add))
        dve.wait(t)
        pool.wait(t)
        t = pool.do(lambda e: e.tensor_tensor(rr[:, :], rr[:, :], exponent[:, :], ALU.pow))
        dve.wait(t, t_rw)
        t_y = [dve.do(lambda e, i=i: e.scalar_tensor_tensor(
            Y[:, i, :], Y[:, i, :], rr[:, i:i + 1], rw[:, :], ALU.mult, ALU.mult)) for i in range(NT)]
        for i in range(NT):
            norm["y", i] = t_y[i]
            norm_transpose(i)
        t_yh, t_yl = norm["yh"], norm["yl"]
        t_lg, lg = logits(io["f3_gate"], E3, t_yh, t_yl)
        GT = {}

        def routing():
            pr, t = softmax_rows(lg, E3, t_lg, E3 + 8 - TOP3)
            yield
            mask, t = choose(pr, t, E3, TOP3, "expert")
            w = mem.take("w", [P, NT, E3], F32)
            ws = mem.take("wsum", [P, NT], F32)
            dve.wait(t)
            t = dve.do(lambda e: e.tensor_tensor(w[:, :, :], pr[:, :, 0:E3], mask[:, :, :], ALU.mult))
            dve.wait(t)
            t = dve.do(lambda e: e.tensor_reduce(ws[:, :], w[:, :, :], AX.X, ALU.add))
            dve.wait(t)
            t = dve.do(lambda e: e.reciprocal(ws[:, :], ws[:, :]))
            dve.wait(t)
            t = dve.do(lambda e: e.tensor_tensor(w[:, :, :], w[:, :, :], ws[:, :].unsqueeze(2).broadcast_to([P, NT, E3]), ALU.mult))
            GT["tile"], GT["tick"] = gates_transposed(w, E3, 32, t)

        sel = mem.take("sel", [64, E3], F32)
        selr = mem.take("selr", [64, E3], F32R)
        t = dma.start(dsem("sel"), sel[:, :], io["sel3"])
        dve.wait(t)
        t_sel = dve.do(lambda e: e.tensor_copy(selr[:, :], sel[:, :]))
        pe.wait(t_sel)
        rows = 32 + E3
        t = expert_blocks(io["f3_w"], 7, NB3, True, lambda n: selr[0:rows, n:n + 1].broadcast_to([rows, P]), rows, NB3 - E3,
                              GT, t_yh, t_yl, routing(), last=True)
        phase_barrier()
        return t

    def quantise(raw, scale, low, high, last_out):
        t = dve.do(lambda e: e.tensor_scalar(raw, raw, scale, ROUND, ALU.mult, ALU.add))
        dve.wait(t)
        t = dve.do(lambda e: e.tensor_scalar(raw, raw, ROUND, high, ALU.subtract, ALU.min))
        dve.wait(t)
        return dve.do(lambda e: e.tensor_scalar(last_out, raw, low, None, ALU.max))

    def ternary_weights():
        mem.at = w1_at
        widths = [I1 * KD, I1 * KD, D * I1 // P]
        raws = [mem.take("wraw", [P, n], F32) for n in widths]
        mem.at = w1_at + NT * I1 * 4
        qs = [mem.take("wq", [P, n], BF16) for n in widths]
        part = mem.take("wpart", [P, 3], F32)
        inv = mem.take("w_unit", [P, 3], F32)
        sw = mem.take("w_scale", [P, 3], F32)
        t_raw = [dma.start(dsem(f"w1_{k}"), raws[k][:, :], io[name])
                 for k, name in enumerate(("f1_gate", "f1_up", "f1_down"))]
        ternary.update(qs=qs, inv=inv)
        yield
        for k in range(3):
            dve.wait(t_raw[k])
            t = dve.do(lambda e, k=k: e.tensor_reduce(part[:, k:k + 1], raws[k][:, :], AX.X, ALU.add,
                                                      apply_absolute_value=True))
            yield
        bank = upper_bank()
        pe.wait(t, t_ones)
        t = pe.do(mm(psum[:, bank, 0:3], ones[:, :], part[:, :], True, True))
        dve.wait(t)
        t = dve.do(lambda e: e.tensor_scalar(inv[:, :], psum[:, bank, 0:3], 1.0 / (I1 * D), 1e-5, ALU.mult, ALU.max))
        bank_free[bank] = t
        dve.wait(t)
        t = dve.do(lambda e: e.reciprocal(sw[:, :], inv[:, :]))
        dve.wait(t)
        for k in range(3):
            ternary["tick"] = quantise(raws[k][:, :], sw[:, k:k + 1], -1.0, 1.0, qs[k][:, :])
            yield

    ternary, heads2 = {}, {}

    def ffn1():
        mem.at = w1_at
        Hb = mem.take("h", [P, NT, I1], F32)
        mem.at = base
        t_y = [norm["y", i] for i in range(NT)]
        Wg, Wu = (q[:, :].rearrange("p (k n) -> p k n", k=KD) for q in ternary["qs"][0:2])
        Wd = ternary["qs"][2][:, :].rearrange("p (k n) -> p k n", k=I1 // P)
        inv = ternary["inv"]
        lw = mem.take("ln_w", [P, I1], F32)
        t_lw = dma.start(dsem("ln_w"), lw[:, :], io["f1_ln"].rearrange("(a n) -> a n", a=1).broadcast_to([P, I1]))
        fold = fold_weights(2, 1)
        next(fold)
        here, mem.at = mem.at, folded_at + H * 2 * DC * 4
        Wq = [mem.take("Wq", [P, H // 2, D], F32)]
        assert mem.at <= base
        mem.at = heads_at
        Wq.append(mem.take("Wq", [P, H // 2, D], F32))
        Wc = mem.take("Wc", [P, H, DQ], F32)
        assert mem.at <= w1_at
        mem.at = here
        t_heads = []
        for g in range(4):
            hs = slice(4 * g, 4 * g + 4)
            dma.start(dsem(f"heads{g}"), Wq[g // 2][:, 4 * (g % 2):4 * (g % 2) + 4, :], io["a2_Wq"][:, hs, :])
            t_heads.append(dma.start(dsem(f"heads{g}"), Wc[:, hs, :], io["a2_Wc"][:, hs, :]))
        heads2.update(Wq=Wq, Wc=Wc, ticks=t_heads)
        am = mem.take("amax", [P, NT], F32)
        sx = mem.take("x_scale", [P, NT], F32)
        ux = mem.take("x_unit", [P, NT], F32)
        cg = mem.take("c_gate", [P, NT], F32)
        cu = mem.take("c_up", [P, NT], F32)
        dve.wait(*t_y)
        t = dve.do(lambda e: e.tensor_reduce(am[:, :], Y[:, :, :], AX.X, ALU.max, apply_absolute_value=True))
        dve.wait(t)
        t = dve.do(lambda e: e.tensor_scalar(am[:, :], am[:, :], 1e-5, None, ALU.max))
        dve.wait(t)
        t = dve.do(lambda e: e.reciprocal(sx[:, :], am[:, :]))
        dve.wait(t)
        t = dve.do(lambda e: e.tensor_scalar(sx[:, :], sx[:, :], 127.0, None, ALU.mult))
        t_q = [dve.do(lambda e: e.tensor_scalar(ux[:, :], am[:, :], 1.0 / 127.0, None, ALU.mult))]
        dve.wait(t, *t_q)
        dve.do(lambda e: e.tensor_scalar(cg[:, :], ux[:, :], inv[:, 0:1], None, ALU.mult))
        t_cu = dve.do(lambda e: e.tensor_scalar(cu[:, :], ux[:, :], inv[:, 1:2], None, ALU.mult))
        XT = mem.take("xqT", [P, KD, T], BF16)
        HQ = mem.take("hqT", [P, I1 // P, T], BF16)
        SG = [mem.take("sg", [P, I1], F32) for _ in range(2)]
        small = lambda name: mem.take(name, [P, NT], F32)
        ss, rr, hm, sh, cd = small("ss"), small("rr"), small("hmax"), small("h_scale"), small("c_down")
        t_xt, t_h, t_ss, t_hw, t_hq, t_turn, sg_free = {}, {}, {}, {}, {}, {}, [None] * 2

        def inputs(i):
            t = quantise(Y[:, i, :], sx[:, i:i + 1], -128.0, 127.0, Y[:, i, :])
            bank = upper_bank()
            pe.wait(t)
            for kd in range(KD):
                t = pe.do(lambda e, kd=kd: e.transpose(psum[:, bank, kd * P:(kd + 1) * P],
                                                       Y[:, i, kd * P:(kd + 1) * P], ident[:, :]))
            act.wait(t)
            bank_free[bank] = t_xt[i] = act.do(lambda e: e.activation(
                XT[:, :, i * P:(i + 1) * P], psum[:, bank, 0:KD * P].rearrange("p (k n) -> p k n", k=KD), ACT.Copy))

        def hidden(i):
            pe.wait(t_xt[i], ternary["tick"])
            for which, W in ((0, Wg), (1, Wu)):
                for n in range(2):
                    bank = 2 * which + n
                    pe.wait(bank_free[bank])
                    t = product(psum[:, bank, :], [(XT[:, kd, i * P:(i + 1) * P], W[:, kd, n * 512:(n + 1) * 512])
                                                   for kd in range(KD)])
                if which == 0:
                    t_gate = t
            sg = SG[i % 2]
            act.wait(t_gate, t_cu, sg_free[i % 2])
            t_s = act.do(lambda e: e.activation(
                sg[:, :].rearrange("p (a n) -> p a n", a=2), psum[:, 0:2, :], ACT.Silu, scale=cg[:, i:i + 1]))
            bank_free[0] = bank_free[1] = t_s
            dve.wait(t_s, t)
            t_h[i] = dve.do(lambda e: e.scalar_tensor_tensor(
                Hb[:, i, :].rearrange("p (a n) -> p a n", a=2), psum[:, 2:4, :], cu[:, i:i + 1],
                sg[:, :].rearrange("p (a n) -> p a n", a=2), ALU.mult, ALU.mult))
            bank_free[2] = bank_free[3] = t_h[i]
            act.wait(t_h[i])
            t_ss[i] = sg_free[i % 2] = act.do(lambda e: e.activation(
                sg[:, :], Hb[:, i, :], ACT.Square, accum_out=ss[:, i:i + 1]))

        def rms(i):
            dve.wait(t_ss[i])
            t = dve.do(lambda e: e.tensor_scalar(rr[:, i:i + 1], ss[:, i:i + 1], 1.0 / I1, 1e-6, ALU.mult, ALU.add))
            pool.wait(t)
            t = pool.do(lambda e: e.tensor_tensor(rr[:, i:i + 1], rr[:, i:i + 1], exponent[:, 0:1], ALU.pow))
            act.wait(t)
            t = act.do(lambda e: e.activation(Hb[:, i, :], Hb[:, i, :], ACT.Copy, scale=rr[:, i:i + 1]))
            pool.wait(t, t_lw)
            t_hw[i] = pool.do(lambda e: e.tensor_tensor(Hb[:, i, :], Hb[:, i, :], lw[:, :], ALU.mult))

        def quantised(i):
            one = slice(i, i + 1)
            dve.wait(t_hw[i])
            t = dve.do(lambda e: e.tensor_reduce(hm[:, one], Hb[:, i, :], AX.X, ALU.max, apply_absolute_value=True))
            dve.wait(t)
            t = dve.do(lambda e: e.tensor_scalar(hm[:, one], hm[:, one], 1e-5, None, ALU.max))
            dve.wait(t)
            t = dve.do(lambda e: e.reciprocal(sh[:, one], hm[:, one]))
            dve.wait(t)
            t = dve.do(lambda e: e.tensor_scalar(sh[:, one], sh[:, one], 127.0, None, ALU.mult))
            t2 = dve.do(lambda e: e.tensor_scalar(cd[:, one], hm[:, one], 1.0 / 127.0, inv[:, 2:3], ALU.mult, ALU.mult))
            dve.wait(t, t2, t_tanh)
            dve.do(lambda e: e.tensor_scalar(cd[:, one], cd[:, one], tanh_g[:, 5:6], None, ALU.mult))
            t_hq[i] = quantise(Hb[:, i, :], sh[:, one], -128.0, 127.0, Hb[:, i, :])

        def turn_hidden(i):
            for a in range(2):
                bank = upper_bank()
                pe.wait(t_hq[i])
                for k in range(4):
                    t = pe.do(lambda e, a=a, k=k, bank=bank: e.transpose(
                        psum[:, bank, k * P:(k + 1) * P], Hb[:, i, (4 * a + k) * P:(4 * a + k + 1) * P], ident[:, :]))
                act.wait(t)
                bank_free[bank] = t = act.do(lambda e, a=a, bank=bank: e.activation(
                    HQ[:, 4 * a:4 * a + 4, i * P:(i + 1) * P],
                    psum[:, bank, :].rearrange("p (k n) -> p k n", k=4), ACT.Copy))
            t_turn[i] = t

        def down(i):
            bank = upper_bank()
            pe.wait(t_turn[i])
            t = product(psum[:, bank, 0:D], [(HQ[:, k, i * P:(i + 1) * P], Wd[:, k, :]) for k in range(I1 // P)])
            dve.wait(t, t_hq[i])
            t = dve.do(lambda e: e.scalar_tensor_tensor(
                X[:, i, :], psum[:, bank, 0:D], cd[:, i:i + 1], X[:, i, :], ALU.mult, ALU.add))
            bank_free[bank] = t
            norm_stats(i, t)
            return t

        inputs(0)
        inputs(1)
        for k in range(NT + 6):
            if k < NT:
                hidden(k)
            if 0 <= k - 4 < NT:
                t = down(k - 4)
            if 0 <= k - 3 < NT:
                turn_hidden(k - 3)
            if k + 2 < NT:
                inputs(k + 2)
            if 0 <= k - 5 < NT:
                norm_apply(k - 5)
            if 0 <= k - 6 < NT:
                norm_transpose(k - 6)
            if 0 <= k - 1 < NT:
                rms(k - 1)
            if 0 <= k - 2 < NT:
                quantised(k - 2)
            next(fold, None)
            next(fold, None)
        for _ in fold:
            pass
        assert mem.at <= heads_at
        phase_barrier()
        return t

    for i in range(NT):
        norm_stats(i, t_x)
    for i in range(NT):
        norm_apply(i)
        norm_transpose(i)
    for _ in fold_weights(0, 6):
        pass
    phase_barrier()
    t_now = t_x
    ffns = [ffn0, ffn1, ffn2, ffn3]
    for n in range(4):
        if steps > 2 * n:
            t_now = attention(n)
        if steps > 2 * n + 1:
            t_now = ffns[n]()
    sp.wait(t_now)
    t_out = dma.start(dsem("out"), out.rearrange("b s d -> (b s) d").rearrange("(i p) d -> p i d", p=P), X[:, :, :])
    sp.wait(t_out)

    with nc.Block() as block:
        for queue, stream in ((block.sync, sp), (block.tensor, pe), (block.scalar, act), (block.vector, dve),
                              (block.gpsimd, pool)):
            queue(stream.emit)


def layouts(i):
    c = np.ascontiguousarray
    a = {"x": c(i["x"]), "ctx": c(i["ctx_512"]), "g_xattn": c(i["g_xattn"]), "g_ffn": c(i["g_ffn"])}
    heads = lambda w, k, n: c(w.reshape(H, k, n).transpose(1, 0, 2))
    kv = i["L0_xattn_Wkv_expand"]
    a["a0_Wq"] = heads(i["L0_xattn_Wq"], 16, D)
    a["a0_Wk"] = heads(kv[:D], 16, DC)
    a["a0_Wv"] = heads(kv[D:], 16, DC)
    a["a0_WoT"] = heads(c(i["L0_xattn_Wout"].T), 16, D)
    for n in (1, 2, 3):
        w = lambda s: i[f"L{n}_xattn_{s}"]
        a[f"a{n}_Wq"] = heads(w("Wq"), K1, D)
        a[f"a{n}_WoT"] = heads(c(w("Wo").T), K1, D)
        a[f"a{n}_Wv"] = c(w("w_kc_kv").transpose(1, 0, 2))
        a[f"a{n}_WrT"] = c(np.concatenate([w("W_qr"), w("W_kr")], 1).transpose(2, 0, 1))
        if n == 2:
            a["a2_Wc"] = c(w("w_kc_q").transpose(1, 0, 2))
        else:
            a[f"a{n}_WcT"] = c(w("w_kc_q").transpose(0, 2, 1).reshape(H, 2, DQH, K1).transpose(2, 0, 1, 3))

    def chunks(w):
        n = w.shape[0] // P
        return w.reshape(n, P, KD, P).transpose(0, 3, 2, 1).reshape(n, P, KD * P)

    up = np.concatenate([chunks(i["L0_ffn_shared_up_w"]), chunks(i["L0_ffn_w1"].reshape(-1, D))])
    dn = np.concatenate([i["L0_ffn_shared_down_w"].T, i["L0_ffn_w2"].transpose(0, 2, 1).reshape(-1, D)]).reshape(-1, P, D)
    a["f0_w"] = c(np.concatenate([up, dn], -1))
    flat = lambda w: w.reshape(-1, D)
    dn = flat(i["L2_ffn_w_down"].transpose(0, 2, 1)).reshape(-1, P, D)
    a["f2_w"] = c(np.concatenate([chunks(flat(i["L2_ffn_w_gate"])), chunks(flat(i["L2_ffn_w_up"])), dn], -1))
    hid = lambda e, s: np.concatenate([i["L3_ffn_" + s].T, flat(i["L3_ffn_" + e].transpose(0, 2, 1))])
    dn = np.concatenate([i["L3_ffn_sw_down"], flat(i["L3_ffn_w_down"])]).reshape(-1, P, D)
    a["f3_w"] = c(np.concatenate([chunks(hid("w_gate", "sw_gate")), chunks(hid("w_up", "sw_up")), dn], -1))
    rows = lambda w: c(w.reshape(-1, P, w.shape[-1]).transpose(1, 0, 2))
    a["f0_gate"] = rows(i["L0_ffn_gate_w"].T)
    a["f2_gate"] = rows(i["L2_ffn_gate_w"].T)
    a["f3_gate"] = rows(i["L3_ffn_router_w"])
    a["f0_bias"] = c(i["L0_ffn_e_bias"])
    a["f3_rms"] = c(i["L3_ffn_rms_weight"])
    a["f1_ln"] = c(i["L1_ffn_ln_weight"])
    for k in ("gate", "up", "down"):
        w = rows(i[f"L1_ffn_w_{k}"].T)
        a[f"f1_{k}"] = c(w.reshape(P, -1))
    a.update(constants())
    a["blockdiag"] = a["blockdiag"].reshape(64, T)
    a["blockdiag2"] = a["blockdiag2"].reshape(64, T)
    return a


def program(nc, arrays, steps=8):
    io = {k: nc.dram_tensor("in_" + k, v.shape, F32, kind="ExternalInput").ap() for k, v in arrays.items()}
    out = nc.dram_tensor("out", (B, S, D), F32, kind="ExternalOutput").ap()
    build(nc, io, out, steps)


def kernel(**inputs):
    import concourse.bacc as bacc
    from concourse.bass_utils import run_bass_kernel_spmd

    arrays = layouts({k: np.asarray(v) for k, v in inputs.items()})
    nc = bacc.Bacc("TRN2", target_bir_lowering=False, num_devices=1)
    program(nc, arrays)
    r = run_bass_kernel_spmd(nc, [{"in_" + k: v for k, v in arrays.items()}], core_ids=[0])
    return r.results[0]["out"]
```
